# Optimizing a Trainium2 kernel written in Bass

```python
import numpy as np
import jax
import jax.numpy as jnp

def _softmax(x, axis=-1):
    return jax.nn.softmax(x, axis=axis)

def _gelu(x):
    return jax.nn.gelu(x, approximate=True)

def _silu(x):
    return jax.nn.silu(x)

def _sigmoid(x):
    return jax.nn.sigmoid(x)

def _layernorm(x, axis=-1, eps=1e-05):
    m = jnp.mean(x, axis=axis, keepdims=True)
    v = jnp.var(x, axis=axis, keepdims=True)
    return (x - m) / jnp.sqrt(v + eps)

def _scatter_add(tgt, idx, src, axis=0):
    return tgt.at[idx].add(src)

def _segment_sum(src, seg, n):
    return jax.ops.segment_sum(src, seg, n)
kernel_name = 'mk_gnn_preln_d2_gnn_r32_a006a5'

def setup_inputs(seed: int=0):
    np.random.seed(seed)
    _w = jnp.asarray

    def _rec_inputs():
        import jax
        import jax.numpy as jnp
        _gk = jax.random.key(seed)
        x = -0.000202 + 1 * jax.random.normal(jax.random.fold_in(_gk, 1), (3125, 64), jnp.float32)
        _s = jax.random.randint(jax.random.fold_in(_gk, 2), (50000,), 0, 3125, jnp.int32)
        _d = jax.random.randint(jax.random.fold_in(_gk, 3), (50000,), 0, 3125, jnp.int32)
        _loop = jnp.arange(3125, dtype=jnp.int32)
        src = jnp.concatenate([_s, _d, _loop])
        dst = jnp.concatenate([_d, _s, _loop])
        _o = jnp.argsort(dst, stable=True)
        src = src[_o]
        dst = dst[_o]
        edge_attr_32 = 0.000196303 + 1.00016 * jax.random.normal(jax.random.fold_in(_gk, 11), (103125, 32), jnp.float32)
        return (x, src, dst, edge_attr_32)
    x, src, dst, edge_attr_32 = _rec_inputs()

    def _L0_gnn_setup():
        import jax, jax.numpy as jnp
        import numpy as np
        N = 3125
        E = 25000
        F_IN = 64
        F_OUT = 64
        H = 4
        HOPS = 2
        NEG_SLOPE = 0.2

        def _segment_softmax(scores, dst, num_segments):
            m = jax.ops.segment_max(scores, dst, num_segments=num_segments)
            m = jnp.where(jnp.isneginf(m), 0.0, m)
            ex = jnp.exp(scores - m[dst])
            den = jax.ops.segment_sum(ex, dst, num_segments=num_segments)
            return ex / jnp.maximum(den[dst], 1e-16)

        def _multi_head_attention(x, src, dst, W_att, a_src, a_dst):
            h = jnp.einsum('ni,hio->nho', x, W_att)
            e = jnp.einsum('eho,ho->eh', h[src], a_src) + jnp.einsum('eho,ho->eh', h[dst], a_dst)
            e = jax.nn.leaky_relu(e, NEG_SLOPE)
            alpha = _segment_softmax(e, dst, N)
            msg = alpha[:, :, None] * h[src]
            out = jax.ops.segment_sum(msg, dst, num_segments=N)
            return out.mean(axis=1)

        def _gf(x, src, dst, num_hops):
            ones = jnp.ones((src.shape[0],), x.dtype)
            deg = jax.ops.segment_sum(ones, dst, num_segments=N)
            deg = jnp.maximum(deg, 1.0)[:, None]
            h = x
            for _ in range(num_hops):
                h = jax.ops.segment_sum(h[src], dst, num_segments=N) / deg
            return h
        key = jax.random.key(seed)
        ks = jax.random.split(key, 9)
        node_features = jax.random.normal(ks[0], (N, F_IN), jnp.float32)
        edge_index = jax.random.randint(ks[1], (2, E), 0, N, dtype=jnp.int64)
        s_in = 1.0 / np.sqrt(F_IN)
        s_out = 1.0 / np.sqrt(F_OUT)
        W_att = jax.random.normal(ks[2], (H, F_IN, F_OUT), jnp.float32) * s_in
        a_src = jax.random.normal(ks[3], (H, F_OUT), jnp.float32) * s_out
        a_dst = jax.random.normal(ks[4], (H, F_OUT), jnp.float32) * s_out
        W_g = jax.random.normal(ks[5], (F_IN, F_OUT), jnp.float32) * s_in
        b_g = jnp.zeros((F_OUT,), jnp.float32)
        W_w = jax.random.normal(ks[6], (2 * F_OUT, F_OUT), jnp.float32) * (1.0 / np.sqrt(2 * F_OUT))
        b_w = jnp.zeros((F_OUT,), jnp.float32)
        return {'node_features': node_features, 'edge_index': edge_index, 'W_att': W_att, 'a_src': a_src, 'a_dst': a_dst, 'W_g': W_g, 'b_g': b_g, 'W_w': W_w, 'b_w': b_w}
    _L0_gnn_all = _L0_gnn_setup()
    _L0_gnn_in = {k: v for k, v in _L0_gnn_all.items() if k in ('W_att', 'a_src', 'a_dst', 'W_g', 'b_g', 'W_w', 'b_w')}
    del _L0_gnn_all

    def _L1_gnn_setup():
        import jax, jax.numpy as jnp
        import numpy as np
        N, D, E, ED, L = (3125, 64, 25000, 32, 5)
        LN_EPS = 1e-05

        def _leaky(x):
            return jax.nn.leaky_relu(x, negative_slope=0.1)
        key = jax.random.key(seed)
        ks = jax.random.split(key, 16)
        s = 0.05
        return {'x': jax.random.normal(ks[0], (N, D), dtype=jnp.float32), 'edge_index': jax.random.randint(ks[1], (2, E), 0, N, dtype=jnp.int64), 'edge_attr': jax.random.normal(ks[2], (E, ED), dtype=jnp.float32), 'W1': jax.random.normal(ks[3], (L, D, 2 * D), dtype=jnp.float32) * s, 'b1': jnp.zeros((L, 2 * D), dtype=jnp.float32), 'W2': jax.random.normal(ks[4], (L, 2 * D, D), dtype=jnp.float32) * s, 'b2': jnp.zeros((L, D), dtype=jnp.float32), 'We1': jax.random.normal(ks[5], (L, ED, D), dtype=jnp.float32) * s, 'be1': jnp.zeros((L, D), dtype=jnp.float32), 'We2': jax.random.normal(ks[6], (L, D, D), dtype=jnp.float32) * s, 'be2': jnp.zeros((L, D), dtype=jnp.float32), 'res_w': jnp.ones((L,), dtype=jnp.float32), 'dot_scale': jnp.ones((L,), dtype=jnp.float32), 'ln_g': jnp.ones((L, D), dtype=jnp.float32), 'ln_b': jnp.zeros((L, D), dtype=jnp.float32)}
    _L1_gnn_all = _L1_gnn_setup()
    _L1_gnn_in = {k: v for k, v in _L1_gnn_all.items() if k in ('W1', 'b1', 'W2', 'b2', 'We1', 'be1', 'We2', 'be2', 'res_w', 'dot_scale', 'ln_g', 'ln_b')}
    del _L1_gnn_all
    return {'x': x, 'src': src, 'dst': dst, 'edge_attr_32': edge_attr_32, 'L0_gnn_W_att': _L0_gnn_in['W_att'], 'L0_gnn_a_src': _L0_gnn_in['a_src'], 'L0_gnn_a_dst': _L0_gnn_in['a_dst'], 'L0_gnn_W_g': _L0_gnn_in['W_g'], 'L0_gnn_b_g': _L0_gnn_in['b_g'], 'L0_gnn_W_w': _L0_gnn_in['W_w'], 'L0_gnn_b_w': _L0_gnn_in['b_w'], 'L1_gnn_W1': _L1_gnn_in['W1'], 'L1_gnn_b1': _L1_gnn_in['b1'], 'L1_gnn_W2': _L1_gnn_in['W2'], 'L1_gnn_b2': _L1_gnn_in['b2'], 'L1_gnn_We1': _L1_gnn_in['We1'], 'L1_gnn_be1': _L1_gnn_in['be1'], 'L1_gnn_We2': _L1_gnn_in['We2'], 'L1_gnn_be2': _L1_gnn_in['be2'], 'L1_gnn_res_w': _L1_gnn_in['res_w'], 'L1_gnn_dot_scale': _L1_gnn_in['dot_scale'], 'L1_gnn_ln_g': _L1_gnn_in['ln_g'], 'L1_gnn_ln_b': _L1_gnn_in['ln_b']}

def reference(x, src, dst, edge_attr_32, L0_gnn_W_att, L0_gnn_a_src, L0_gnn_a_dst, L0_gnn_W_g, L0_gnn_b_g, L0_gnn_W_w, L0_gnn_b_w, L1_gnn_W1, L1_gnn_b1, L1_gnn_W2, L1_gnn_b2, L1_gnn_We1, L1_gnn_be1, L1_gnn_We2, L1_gnn_be2, L1_gnn_res_w, L1_gnn_dot_scale, L1_gnn_ln_g, L1_gnn_ln_b):
    import jax
    import jax.numpy as jnp

    def _L0_gnn_ref(node_features, edge_index, W_att, a_src, a_dst, W_g, b_g, W_w, b_w):
        import jax, jax.numpy as jnp
        import numpy as np
        N = 3125
        E = 25000
        F_IN = 64
        F_OUT = 64
        H = 4
        HOPS = 2
        NEG_SLOPE = 0.2

        def _segment_softmax(scores, dst, num_segments):
            m = jax.ops.segment_max(scores, dst, num_segments=num_segments)
            m = jnp.where(jnp.isneginf(m), 0.0, m)
            ex = jnp.exp(scores - m[dst])
            den = jax.ops.segment_sum(ex, dst, num_segments=num_segments)
            return ex / jnp.maximum(den[dst], 1e-16)

        def _multi_head_attention(x, src, dst, W_att, a_src, a_dst):
            h = jnp.einsum('ni,hio->nho', x, W_att)
            e = jnp.einsum('eho,ho->eh', h[src], a_src) + jnp.einsum('eho,ho->eh', h[dst], a_dst)
            e = jax.nn.leaky_relu(e, NEG_SLOPE)
            alpha = _segment_softmax(e, dst, N)
            msg = alpha[:, :, None] * h[src]
            out = jax.ops.segment_sum(msg, dst, num_segments=N)
            return out.mean(axis=1)

        def _gf(x, src, dst, num_hops):
            ones = jnp.ones((src.shape[0],), x.dtype)
            deg = jax.ops.segment_sum(ones, dst, num_segments=N)
            deg = jnp.maximum(deg, 1.0)[:, None]
            h = x
            for _ in range(num_hops):
                h = jax.ops.segment_sum(h[src], dst, num_segments=N) / deg
            return h
        src, dst = (edge_index[0], edge_index[1])
        local = _multi_head_attention(node_features, src, dst, W_att, a_src, a_dst)
        glob = _gf(node_features, src, dst, HOPS)
        glob = glob @ W_g + b_g
        cat = jnp.concatenate([local, glob], axis=-1)
        return cat @ W_w + b_w

    def _L1_gnn_ref(x, edge_index, edge_attr, W1, b1, W2, b2, We1, be1, We2, be2, res_w, dot_scale, ln_g, ln_b):
        import jax, jax.numpy as jnp
        import numpy as np
        N, D, E, ED, L = (3125, 64, 25000, 32, 5)
        LN_EPS = 1e-05

        def _leaky(x):
            return jax.nn.leaky_relu(x, negative_slope=0.1)
        src, dst = (edge_index[0], edge_index[1])
        n = x.shape[0]
        for l in range(W1.shape[0]):
            h = _leaky(x @ W1[l] + b1[l]) @ W2[l] + b2[l]
            e = _leaky(edge_attr @ We1[l] + be1[l]) @ We2[l] + be2[l]
            msg = h[src] * e * dot_scale[l]
            agg = jax.ops.segment_sum(msg, dst, num_segments=n)
            out = x + agg * res_w[l]
            mu = jnp.mean(out, axis=-1, keepdims=True)
            var = jnp.mean(jnp.square(out - mu), axis=-1, keepdims=True)
            x = (out - mu) * jax.lax.rsqrt(var + LN_EPS) * ln_g[l] + ln_b[l]
        return x
    edge_index = jnp.stack([src, dst])
    h = jnp.maximum(_layernorm(x, axis=-1), 0.0)
    x = x + _L0_gnn_ref(h, edge_index, L0_gnn_W_att, L0_gnn_a_src, L0_gnn_a_dst, L0_gnn_W_g, L0_gnn_b_g, L0_gnn_W_w, L0_gnn_b_w)
    h = jnp.maximum(_layernorm(x, axis=-1), 0.0)
    x = x + _L1_gnn_ref(h, edge_index, edge_attr_32, L1_gnn_W1, L1_gnn_b1, L1_gnn_W2, L1_gnn_b2, L1_gnn_We1, L1_gnn_be1, L1_gnn_We2, L1_gnn_be2, L1_gnn_res_w, L1_gnn_dot_scale, L1_gnn_ln_g, L1_gnn_ln_b)
    return x

_drawn_inputs = setup_inputs


def setup_inputs(seed=0):
    import zlib

    import numpy as np

    out = dict(_drawn_inputs(seed))
    spreads = {'L0_gnn_b_g': (0.0, 0.1),
     'L0_gnn_b_w': (0.0, 0.1),
     'L1_gnn_b1': (0.0, 0.1),
     'L1_gnn_b2': (0.0, 0.1),
     'L1_gnn_be1': (0.0, 0.1),
     'L1_gnn_be2': (0.0, 0.1),
     'L1_gnn_res_w': (1.0, 0.2),
     'L1_gnn_dot_scale': (1.0, 0.2),
     'L1_gnn_ln_g': (1.0, 0.2),
     'L1_gnn_ln_b': (0.0, 0.1)}
    factors = {'L0_gnn_a_src': 2.911, 'L0_gnn_a_dst': 8.0}
    for name, (base, spread) in spreads.items():
        noise = np.random.default_rng([zlib.crc32(name.encode()), seed]).standard_normal(out[name].shape)
        drawn = base * np.exp(spread * noise) if base else spread * noise
        out[name] = jnp.asarray(drawn.astype(out[name].dtype))
    for name, factor in factors.items():
        out[name] = (out[name] * factor).astype(out[name].dtype)
    return out
```

```python
from contextlib import ExitStack

import numpy as np
import concourse.bass as bass
from concourse import mybir
from concourse.alu_op_type import AluOpType as ALU

ACT = mybir.ActivationFunctionType
AX = mybir.AxisListType
F32 = mybir.dt.float32
BF16 = mybir.dt.bfloat16
I32 = mybir.dt.int32

P = 128
N, F, E, ED = 3125, 64, 103125, 32
H, L = 4, 5
F2 = 2 * F
K = 8
SL = 4
T = -(-E // (P * K)) * K
EP = P * T
CH = T // K
LOOPS = CH // SL - 1
FULL = LOOPS * SL
LAST = E - (P - 1) * T
NJ = 25
NQ = N // NJ
GJ = 5
NG = NJ // GJ
W1R = F + H
W2R = 2 * F + 1
WH = F + 1
WG = F + H * WH
BIG = 1.0e38
ROUND = 12582912.0
NEG = 0.2
LEAK = 0.1
EPS = 1e-5

C_W1 = 0
C_W2 = C_W1 + F2
C_E1 = C_W2 + F
C_E2 = C_E1 + 2 * P
C_B1 = C_E2 + P
C_BE1 = C_B1 + 1
CW = C_BE1 + 1
C_W2N = CW
C_E2N = C_W2N + F
C_B1N = C_E2N + P
C_BE1N = C_B1N + 1
CP = C_BE1N + 1


class Steps:

    def __init__(self, eng, sem, base=0):
        self.eng, self.sem, self.base, self.n = eng, sem, base, 0

    def done(self, ins):
        self.n += 1
        ins.then_inc(self.sem, 1)

    def then(self, ins):
        self.done(ins)
        self.eng.wait_ge(self.sem, self.base + self.n)


def build(nc, x, src, dst, attr, W_att, a_src, a_dst, W_g, b_g, W_w, b_w, W1, b1, W2, b2, We1, be1, We2, be2,
          res_w, dot_scale, ln_g, ln_b, out):
    ctx = ExitStack()
    with ctx:
        def sb(name, shape, dt=F32):
            return ctx.enter_context(nc.sbuf_tensor(name, shape, dt))

        def sem(name):
            return ctx.enter_context(nc.semaphore(name))

        def dram(name, shape):
            return nc.dram_tensor(name, shape, F32, kind="Internal").ap()

        attr_pad = dram("attr_pad", (EP, ED))
        table1 = dram("table1", (N, W1R))
        table2 = dram("table2", (N, W2R))
        tableh = dram("tableh", (N, F))
        rows1 = dram("rows1", (EP, F))
        rows2 = dram("rows2", (EP, WG))
        rowsg = dram("rowsg", (EP, F))
        ed_nodes = dram("ed_nodes", (N, H))
        ed_edges = dram("ed_edges", (EP + N, H))

        src_i = sb("src_i", [P, T], I32)
        dst_i = sb("dst_i", [P, T], I32)
        dst_f = sb("dst_f", [P, T])
        mask = sb("mask", [P, T])
        pen = sb("pen", [P, T + 1])
        pen_first = sb("pen_first", [P, T])
        pen_last = sb("pen_last", [P, T])
        es_w = sb("es_w", [P, T, H])
        union = sb("union", [P, NJ * WG])
        agg2 = union[0:NQ, :].rearrange("q (j w) -> q j w", w=WG)
        crossq = union[0:NQ, 0:NJ * P].rearrange("q (j p) -> q j p", p=P)
        crossq2 = union[0:NQ, NJ * P:2 * NJ * P].rearrange("q (j p) -> q j p", p=P)
        sm_a = union[:, 0:T * H].rearrange("p (t h) -> p t h", h=H)
        sm_b = union[:, T * H:2 * T * H].rearrange("p (t h) -> p t h", h=H)
        d25 = union[:, 2 * T * H:2 * T * H + T]
        drem = union[:, 2 * T * H + T:2 * T * H + 2 * T]
        reached = union[:, 2 * T * H:2 * T * H + H * P].rearrange("p (h n) -> p h n", h=H)
        zeros = union[:, 0:T * H // 2]
        cross = sb("cross", [P, NJ, NQ])
        idx = sb("idx", [P, SL, K], I32)
        gring = sb("gring", [P, SL * K * W2R])
        pack = es_w[:, :, :].rearrange("p t h -> p (t h)")[:, 0:L * CW].rearrange("p (l c) -> p l c", l=L)
        gather1 = gring[:, 0:SL * K * W1R].rearrange("p (s k w) -> p s k w", s=SL, k=K)
        gather2 = gring[:, :].rearrange("p (s k w) -> p s k w", s=SL, k=K)
        gatherg = gring[:, 0:SL * K * F].rearrange("p (s k w) -> p s k w", s=SL, k=K)
        stage = sb("stage", [P, 4 * K * WG])
        msg2 = stage[:, 0:2 * K * WG].rearrange("p (b k w) -> p b k w", b=2, k=K)
        run2 = stage[:, 2 * K * WG:].rearrange("p (b k w) -> p b k w", b=2, k=K)
        t1 = stage[0:NQ, 0:NJ * W1R].rearrange("q (j w) -> q j w", w=W1R)
        t2 = stage[0:NQ, NJ * W1R:NJ * (W1R + W2R)].rearrange("q (j w) -> q j w", w=W2R)
        used = [0]

        def part(width):
            used[0] += width
            return stage[:, used[0] - width:used[0]]

        attr_nat = part(SL * K * ED).rearrange("p (s d) -> p s d", s=SL)
        attr_T = part(2 * K * ED).rearrange("p (b d) -> p b d", b=2)
        act_p = part(8 * P).rearrange("p (b n) -> p b n", b=2)
        act_n = part(8 * P).rearrange("p (b n) -> p b n", b=2)
        cat2 = gring[0:NQ, 0:GJ * (H * F + F)].rearrange("q (k w) -> q k w", k=GJ)
        msgg = part(K * F).rearrange("p (k f) -> p k f", k=K)
        yp = part(GJ * NQ).rearrange("p (k n) -> p k n", k=GJ)
        yn = part(GJ * NQ).rearrange("p (k n) -> p k n", k=GJ)
        hsb = part(NJ * F)[0:NQ, :].rearrange("q (j f) -> q j f", j=NJ)
        run1 = sb("run1", [P, SL, K, F])
        hot_q = sb("hot_q", [P, 2, K, NQ], BF16)
        hot_j = sb("hot_j", [P, 2, K, NJ], BF16)
        q25 = sb("q25", [P, NQ])
        jcol = sb("jcol", [P, NJ])
        bound = sb("bound", [P, P])
        spare = sb("spare", [P, NJ])
        ident = sb("ident", [P, P])
        below = sb("below", [P, P])
        above = sb("above", [P, P])
        zero16 = sb("zero16", [P, NQ], BF16)
        ones = sb("ones", [P, P])
        xin = sb("xin", [NQ, NJ, F])
        x1 = sb("x1", [NQ, NJ, F])
        xg = sb("xg", [NQ, NJ, F])
        agg = sb("agg", [NQ, NJ, F])
        ed_sb = sb("ed_sb", [NQ, NJ, H])
        ed0 = sb("ed0", [P, H])
        cen = sb("cen", [NQ, 2, GJ, F])
        sq = sb("sq", [NQ, GJ, F])
        st_sum = sb("st_sum", [NQ, 2, GJ])
        st_var = sb("st_var", [NQ, 2, GJ])
        st_std = sb("st_std", [NQ, 2, GJ])
        node = sb("node", [NQ, 12, NJ])
        deg, incl, last, first = (node[:, i, :] for i in range(4))
        nonempty, cmean, tmpn, lastc, msl = (node[:, i, :] for i in range(4, 9))
        rowoff = sb("rowoff", [NQ, 1])
        last_i = sb("last_i", [NQ, NJ], I32)
        slot_i = sb("slot_i", [NQ, NJ], I32)
        edge1 = sb("edge1", [P, 2, H])
        diag = sb("diag", [P, 2, P])
        pen_m = sb("pen_m", [P, 2, P])
        diag4 = sb("diag4", [P, H, P])
        carry = sb("carry", [P, 2, H])
        watt = sb("watt", [F, H, F])
        wattT = sb("wattT", [F, H, F])
        wstack = sb("wstack", [P, 2, F])
        avec = sb("avec", [F, 2, H])
        vvec = sb("vvec", [F, 2 * H])
        wg_sb = sb("wg_sb", [F, F])
        ww_sb = sb("ww_sb", [P, F])
        cat_s = sb("cat_s", [P, 2])
        bw_row = sb("bw_row", [1, F])
        hT = sb("hT", [F, GJ, NQ])
        aT = sb("aT", [P, 3, NQ])
        catT = sb("catT", [P, NQ])
        recd = sb("recd", [NQ, GJ, H])
        cur = sb("cur", [P, CP])
        rows_b = sb("rows_b", [1, L, 2 * F])
        cur_b = sb("cur_b", [1, 2 * F])
        lnp = sb("lnp", [NQ, L, 2 * F + 2])
        cur_ln = sb("cur_ln", [NQ, 2 * F + 2])

        psum = ctx.enter_context(nc.psum_tensor("psum", [P, 8, 512], F32))

        passed = [sem(f"passed_{e}") for e in ("pool", "pe", "act", "dve")]
        pads_set, consts_set, pack_zero = sem("pads_set"), sem("consts_set"), sem("pack_zero")
        x_in, edges_in, att_in, weights_in = sem("x_in"), sem("edges_in"), sem("att_in"), sem("weights_in")
        attr_padded, ed_zeroed = sem("attr_padded"), sem("ed_zeroed")
        ln_var, ln_std = sem("ln_var"), sem("ln_std")
        dve_steps, prep_steps, act_steps = sem("dve_steps"), sem("prep_steps"), sem("act_steps")
        v_T, v_Tsb, v_ps, v_sb = sem("v_T"), sem("v_Tsb"), sem("v_ps"), sem("v_sb")
        h0_ready, h0_T, h0_Tsb, es_ps, es_sb, t1_out = (sem(n) for n in (
            "h0_ready", "h0_T", "h0_Tsb", "es_ps", "es_sb", "t1_out"))
        ed_out = sem("ed_out")
        idx1, g1_ready = sem("idx1"), [sem(f"g1_ready{s}") for s in range(SL)]
        hop_steps, hot_ready, hot_used, es_done = sem("hop_steps"), sem("hot_ready"), sem("hot_used"), sem("es_done")
        run1_free, rows1_out, rows1_all = sem("run1_free"), sem("rows1_out"), sem("rows1_all")
        deg_ready, rowtot, rowoff_ps, last_ready = sem("deg_ready"), sem("rowtot"), sem("rowoff_ps"), sem("last_ready")
        crossq_ready, cross_T, cross_sb = sem("crossq_ready"), sem("cross_T"), sem("cross_sb")
        slots_ready, ed_scattered, ed0_in, edx_in = sem("slots_ready"), sem("ed_scattered"), sem("ed0_in"), sem("edx_in")
        agg1_in = [sem(f"agg1_in{g}") for g in range(NG)]
        c1_ready, c1_used, t2_ready, t2h_ready, t2_out = (sem(n) for n in (
            "c1_ready", "c1_used", "t2_ready", "t2h_ready", "t2_out"))
        diag_ready, bc_ready, diag4_ready, bc4_ready = sem("diag_ready"), sem("bc_ready"), sem("diag4_ready"), sem("bc4_ready")
        w_arg, w_ready = sem("w_arg"), sem("w_ready")
        idx2, g2_ready = sem("idx2"), [sem(f"g2_ready{s}") for s in range(SL)]
        hopcopy, msg_steps, gat_steps = sem("hopcopy"), sem("msg_steps"), sem("gat_steps")
        run2_free, rows2_out, rows2_all = sem("run2_free"), sem("rows2_out"), sem("rows2_all")
        agg2_in = [sem(f"agg2_in{g}") for g in range(NG)]
        c2_ready, c2_used, cat2_ready, aT_ps, aT_sb = (sem(n) for n in (
            "c2_ready", "c2_used", "cat2_ready", "aT_ps", "aT_sb"))
        catT_ps, catT_sb, x1_ps, x1_used = sem("catT_ps"), sem("catT_sb"), sem("x1_ps"), sem("x1_used")
        x_ready, packed, pack_in, cur_ready = sem("x_ready"), sem("packed"), sem("pack_in"), sem("cur_ready")
        xT_ps, xT_sb, y_ps, y_sb, h_ps, h_sb, table_out = (sem(n) for n in (
            "xT_ps", "xT_sb", "y_ps", "y_sb", "h_ps", "h_sb", "table_out"))
        idxg, gg_ready = sem("idxg"), [sem(f"gg_ready{s}") for s in range(SL)]
        attr_in = [sem(f"attr_in{s}") for s in range(SL)]
        at_ps, at_sb, ye_ps, ye_sb, e_ready, edge_steps = (sem(n) for n in (
            "at_ps", "at_sb", "ye_ps", "ye_sb", "e_ready", "edge_steps"))
        rung_free, rowsg_out, rowsg_all = sem("rung_free"), sem("rowsg_out"), sem("rowsg_all")
        aggg_in = [sem(f"aggg_in{g}") for g in range(NG)]
        cg_ready, cg_used = sem("cg_ready"), sem("cg_used")
        out_ready, out_done = sem("out_ready"), sem("out_done")

        def chunk_rows(rows, c, width):
            return rows.rearrange("(p t) w -> p t w", p=P)[:, bass.ds(c * K, K), 0:width]

        def node_rows(table):
            return table.rearrange("(q j) w -> q j w", j=NJ)

        def grp(g):
            return slice(g * GJ, (g + 1) * GJ)

        block = ctx.enter_context(nc.Block())

        @block.sync
        def _(sp):
            sp.dma_start(xin[:, :, :], x.rearrange("(q j) f -> q j f", j=NJ)).then_inc(x_in, 16)
            sp.dma_start(watt[:, :, :], W_att.rearrange("h i o -> i h o")).then_inc(att_in, 16)
            with nc.allow_non_contiguous_dma(reason="two vectors of 256 elements"):
                sp.dma_start(avec[:, 0, :], a_src.rearrange("h o -> o h")).then_inc(att_in, 16)
                sp.dma_start(avec[:, 1, :], a_dst.rearrange("h o -> o h")).then_inc(att_in, 16)
            sp.wait_ge(pads_set, 2)
            for to, of in ((src_i, src), (dst_i, dst)):
                sp.dma_start(to[0:P - 1, :], of[0:(P - 1) * T].rearrange("(p t) -> p t", p=P - 1))\
                    .then_inc(edges_in, 16)
                sp.dma_start(to[P - 1:P, 0:LAST], of[(P - 1) * T:E].rearrange("(p t) -> p t", p=1))\
                    .then_inc(edges_in, 16)
            for g in range(NG):
                sp.wait_ge(es_sb, 2 * g + 2)
                sp.dma_start(node_rows(table1)[:, grp(g), :], t1[:, grp(g), :]).then_inc(t1_out, 16)
            sp.dma_start(node_rows(ed_nodes), ed_sb[:, :, :]).then_inc(ed_out, 16)
            sp.wait_ge(consts_set, 2)
            half = ed_edges[0:EP, :].rearrange("(p a t) h -> p a (t h)", p=P, a=2)
            for a in range(2):
                sp.dma_start(half[:, a, :], zeros[:, :]).then_inc(ed_zeroed, 16)
            sp.dma_start(attr_pad[0:E, :].rearrange("(a b) d -> a (b d)", b=E // 375),
                         attr.rearrange("(a b) d -> a (b d)", b=E // 375)).then_inc(attr_padded, 16)
            tail = EP - E
            sp.dma_start(attr_pad[E:EP, :].rearrange("(a b) d -> a (b d)", b=tail // 23),
                         zeros[0:23, 0:tail // 23 * ED]).then_inc(attr_padded, 16)
            sp.dma_start(wstack[:, :, :], W_att.rearrange("(c b) i o -> (b i) c o", b=2)).then_inc(weights_in, 16)
            sp.dma_start(wg_sb[:, :], W_g).then_inc(weights_in, 16)
            sp.dma_start(ww_sb[:, :], W_w).then_inc(weights_in, 16)
            sp.dma_start(bw_row[:, :], b_w.rearrange("(a f) -> a f", a=1)).then_inc(weights_in, 16)
            sp.wait_ge(consts_set, N_CONSTS)
            with nc.allow_non_contiguous_dma(reason="bias vector"):
                sp.dma_start(cat_s[F:P, 1:2], b_g.rearrange("(f a) -> f a", a=1)).then_inc(weights_in, 16)
            sp.dma_start(rows_b[:, :, 0:F], be2.rearrange("(a l) f -> a l f", a=1)).then_inc(weights_in, 16)
            sp.dma_start(rows_b[:, :, F:2 * F], b2.rearrange("(a l) f -> a l f", a=1)).then_inc(weights_in, 16)
            sp.dma_start(lnp[:, :, 0:F], ln_g.partition_broadcast(NQ)).then_inc(weights_in, 16)
            sp.dma_start(lnp[:, :, F:2 * F], ln_b.partition_broadcast(NQ)).then_inc(weights_in, 16)
            with nc.allow_non_contiguous_dma(reason="one number per layer"):
                sp.dma_start(lnp[:, :, 2 * F], dot_scale.partition_broadcast(NQ)).then_inc(weights_in, 16)
                sp.dma_start(lnp[:, :, 2 * F + 1], res_w.partition_broadcast(NQ)).then_inc(weights_in, 16)

            def store1(c, s):
                sp.wait_ge(hop_steps, (c + 1) * K)
                sp.dma_start(chunk_rows(rows1, c, F), run1[:, s, :, :]).then_inc(rows1_out, 16)
                sp.wait_ge(rows1_out, (c + 1) * 16)
                sp.sem_inc(run1_free, 1)

            sp.sem_inc(run1_free, SL)
            with sp.Fori(0, LOOPS) as i:
                for s in range(SL):
                    store1(i * SL + s, s)
            for c in range(FULL, CH):
                store1(c, c % SL)
            sp.sem_inc(rows1_all, 1)

            for g in range(NG):
                sp.wait_ge(t2_ready, g + 1)
                if g == 0:
                    sp.wait_ge(t2h_ready, 1)
                sp.dma_start(node_rows(table2)[:, grp(g), :], t2[:, grp(g), :]).then_inc(t2_out, 16)
            sp.wait_ge(ed_scattered, NJ * 16)
            sp.wait_ge(cross_sb, NJ)
            sp.dma_start(sm_a, ed_edges[0:EP, :].rearrange("(p t) h -> p t h", p=P)).then_inc(edx_in, 16)

            def store2(c, s):
                sp.wait_ge(gat_steps, (c + 3) * K)
                sp.dma_start(chunk_rows(rows2, c, WG), run2[:, s % 2, :, :]).then_inc(rows2_out, 16)
                sp.wait_ge(rows2_out, (c + 1) * 16)
                sp.sem_inc(run2_free, 1)

            sp.sem_inc(run2_free, 2)
            with sp.Fori(0, LOOPS) as i:
                for s in range(SL):
                    store2(i * SL + s, s)
            for c in range(FULL, CH):
                store2(c, c % SL)
            sp.sem_inc(rows2_all, 1)

            sp.wait_ge(pack_zero, 1)
            loads = [(pack[0:F, :, C_W1:C_W1 + F2], W1.rearrange("l d m -> d l m")),
                     (pack[:, :, C_W2:C_W2 + F], W2.rearrange("l m d -> m l d")),
                     (pack[:, :, C_B1], b1.rearrange("l m -> m l"))]
            for q in range(4):
                col = C_E1 + (q // 2) * P + (q % 2) * F
                loads.append((pack[q * ED:(q + 1) * ED, :, col:col + F], We1.rearrange("l a d -> a l d")))
            for q in range(2):
                col = C_E2 + q * F
                loads.append((pack[q * F:(q + 1) * F, :, col:col + F], We2.rearrange("l d e -> d l e")))
                loads.append((pack[q * F:(q + 1) * F, :, C_BE1], be1.rearrange("l d -> d l")))
            assert len(loads) == N_PACK
            with nc.allow_non_contiguous_dma(reason="bias vectors"):
                for to, of in loads:
                    sp.dma_start(to, of).then_inc(pack_in, 16)

            def load_attr(c, s):
                return sp.dma_start(attr_nat[:, s, :].rearrange("p (k d) -> p k d", d=ED),
                                    chunk_rows(attr_pad, c, ED)).then_inc(attr_in[s], 16)

            def store_g(l, c, s):
                sp.wait_ge(edge_steps, 2 * (K + 1) + (l * CH + c + 1) * (K + 1))
                sp.dma_start(chunk_rows(rowsg, c, F), run1[:, s, :, :]).then_inc(rowsg_out, 16)
                sp.wait_ge(rowsg_out, (l * CH + c + 1) * 16)
                sp.sem_inc(rung_free, 1)

            sp.sem_inc(rung_free, SL)
            sp.wait_ge(attr_padded, 32)
            sp.wait_ge(x_ready, NG)
            with sp.Fori(0, L) as l:
                for c in range(SL):
                    load_attr(c, c)
                for g in range(NG):
                    sp.wait_ge(h_sb, l * NG + g + 1)
                    sp.dma_start(node_rows(tableh)[:, grp(g), :], hsb[:, grp(g), :]).then_inc(table_out, 16)
                with sp.Fori(0, LOOPS) as i:
                    for s in range(SL):
                        c = i * SL + s
                        sp.wait_ge(at_ps, l * CH + c + 1)
                        load_attr(c + SL, s)
                        store_g(l, c, s)
                for c in range(FULL, CH):
                    if c + SL < CH:
                        sp.wait_ge(at_ps, l * CH + (c + 1))
                        load_attr(c + SL, c % SL)
                    store_g(l, c, c % SL)
                sp.sem_inc(rowsg_all, 1)

            sp.wait_ge(out_ready, 1)
            sp.dma_start(out.rearrange("(q j) f -> q j f", j=NJ), xin[:, :, :]).then_inc(out_done, 16)
            sp.wait_ge(out_done, 16)

        @block.gpsimd
        def _(pool):
            def settle():
                pool.sem_inc(passed[0], 1)

            pool.memset(src_i[:, :], 0).then_inc(pads_set, 1)
            pool.memset(dst_i[:, :], 4095).then_inc(pads_set, 1)
            pool.memset(ident[:, :], 0.0).then_inc(consts_set, 1)
            pool.memset(zeros[:, :], 0.0).then_inc(consts_set, 1)
            pool.memset(below[:, :], 1.0).then_inc(consts_set, 1)
            pool.memset(above[:, :], 1.0).then_inc(consts_set, 1)
            pool.wait_ge(consts_set, 4)
            pool.affine_select(out=ident[:, :], in_=ident[:, :], compare_op=ALU.not_equal, fill=1.0, base=0,
                               pattern=[[-1, P]], channel_multiplier=1).then_inc(consts_set, 1)
            pool.affine_select(out=below[:, :], in_=below[:, :], compare_op=ALU.is_gt, fill=0.0, base=0,
                               pattern=[[-1, P]], channel_multiplier=1).then_inc(consts_set, 1)
            pool.affine_select(out=above[:, :], in_=above[:, :], compare_op=ALU.is_gt, fill=0.0, base=0,
                               pattern=[[1, P]], channel_multiplier=-1).then_inc(consts_set, 1)
            pool.iota(q25[:, :], [[NJ, NQ]], base=0, channel_multiplier=0,
                      allow_small_or_imprecise_dtypes=True).then_inc(consts_set, 1)
            pool.iota(jcol[:, :], [[1, NJ]], base=0, channel_multiplier=0,
                      allow_small_or_imprecise_dtypes=True).then_inc(consts_set, 1)
            pool.iota(bound[:, :], [[T, P]], base=T, channel_multiplier=0,
                      allow_small_or_imprecise_dtypes=True).then_inc(consts_set, 1)
            pool.iota(spare[:, :], [[1, NJ]], base=EP, channel_multiplier=NJ,
                      allow_small_or_imprecise_dtypes=True).then_inc(consts_set, 1)
            pool.memset(zero16[:, :], 0.0).then_inc(consts_set, 1)
            pool.memset(ones[:, :], 1.0).then_inc(consts_set, 1)
            pool.memset(t2[:, :, 2 * F:], 1.0).then_inc(consts_set, 1)
            pool.memset(run1[:, SL - 1, K - 1, :], 0.0).then_inc(consts_set, 1)
            pool.memset(run2[:, 1, K - 1, :], 0.0).then_inc(consts_set, 1)
            pool.memset(cat_s[:, :], 0.0).then_inc(consts_set, 1)

            def gather_chunk(idx_ready, n, table, ring, ready, s):
                pool.wait_ge(idx_ready, n)
                settle()
                for k in range(K):
                    pool.indirect_dma_start(ring[:, s, k, :], None, table,
                                            bass.IndirectOffsetOnAxis(ap=idx[:, s, k:k + 1], axis=0))\
                        .then_inc(ready[s], 16)

            def gather_pass(idx_ready, base, table, ring, ready):
                with pool.Fori(0, LOOPS) as i:
                    for s in range(SL):
                        gather_chunk(idx_ready, base + i * SL + (s + 1), table, ring, ready, s)
                for c in range(FULL, CH):
                    gather_chunk(idx_ready, base + (c + 1), table, ring, ready, c % SL)

            def gather_nodes(rows, to, arrived):
                for j in range(NJ):
                    pool.indirect_dma_start(to[:, j, :], None, rows,
                                            bass.IndirectOffsetOnAxis(ap=last_i[:, j:j + 1], axis=0))\
                        .then_inc(arrived[j // GJ], 16)

            pool.wait_ge(t1_out, NG * 16)
            gather_pass(idx1, 0, table1, gather1, g1_ready)
            pool.wait_ge(rows1_all, 1)
            pool.wait_ge(last_ready, 1)
            settle()
            gather_nodes(rows1, agg, agg1_in)
            pool.wait_ge(slots_ready, 1)
            pool.wait_ge(ed_zeroed, 32)
            pool.wait_ge(ed_out, 16)
            settle()
            for j in range(NJ):
                pool.indirect_dma_start(ed_edges, bass.IndirectOffsetOnAxis(ap=slot_i[:, j:j + 1], axis=0),
                                        ed_sb[:, j, :], None).then_inc(ed_scattered, 16)
            pool.indirect_dma_start(ed0[:, :], None, ed_nodes,
                                    bass.IndirectOffsetOnAxis(ap=dst_i[:, 0:1], axis=0)).then_inc(ed0_in, 16)
            pool.wait_ge(t2_out, NG * 16)
            settle()
            gather_pass(idx2, 0, table2, gather2, g2_ready)
            pool.wait_ge(rows2_all, 1)
            settle()
            gather_nodes(rows2, agg2, agg2_in)
            pool.memset(pack, 0.0).then_inc(pack_zero, 1)
            with pool.Fori(0, L) as l:
                pool.wait_ge(table_out, (l + 1) * (NG * 16))
                settle()
                gather_pass(idxg, l * CH, tableh, gatherg, gg_ready)
                pool.wait_ge(rowsg_all, l + 1)
                settle()
                gather_nodes(rowsg, agg, aggg_in)

        def es_group(act, copy, g):
            act.wait_ge(h0_T, g + 1)
            copy(hT[:, :, :], psum[0:F, 2:4, :].rearrange("p b n -> p (b n)")[:, 0:GJ * P]
                 .rearrange("p (k n) -> p k n", n=P)[:, :, 0:NQ]).then_inc(h0_Tsb, 1)
            act.wait_ge(es_ps, g + 1)
            scores = psum[0:NQ, 1, 64:64 + GJ * 2 * H].rearrange("q (k h) -> q k h", k=GJ)
            copy(t1[:, grp(g), F:F + H], scores[:, :, 0:H]).then_inc(es_sb, 1)
            copy(ed_sb[:, grp(g), :], scores[:, :, H:2 * H]).then_inc(es_sb, 1)

        @block.scalar
        def _(act):
            copy = nc.scalar.copy

            def settle():
                act.sem_inc(passed[2], 1)

            def ln_sqrt(g):
                return nc.scalar.activation(st_std[:, g % 2, :], st_var[:, g % 2, :], ACT.Sqrt)

            act.wait_ge(v_T, 1)
            copy(wattT[:, :, :], psum[0:F, 0, 0:H * F].rearrange("p (h i) -> p h i", h=H)).then_inc(v_Tsb, 1)
            act.wait_ge(v_ps, 1)
            copy(vvec[:, :], psum[0:F, 1, 0:2 * H]).then_inc(v_sb, 1)
            for g in range(NG):
                act.wait_ge(ln_var, g + 1)
                ln_sqrt(g).then_inc(ln_std, 1)
                if g:
                    es_group(act, copy, g - 1)
            es_group(act, copy, NG - 1)
            copy(t2[:, :, F:2 * F], t1[:, :, 0:F]).then_inc(t2h_ready, 1)

            act.wait_ge(weights_in, N_WEIGHTS * 16)
            act.wait_ge(consts_set, N_CONSTS)
            nc.scalar.activation(cat_s[0:F, 0:1], ident[0:F, 0:1], ACT.Copy, scale=0.0, bias=1.0 / H).then_inc(packed, 1)
            nc.scalar.activation(cat_s[F:P, 0:1], ident[F:P, 0:1], ACT.Copy, scale=0.0, bias=1.0).then_inc(packed, 1)

            for j in range(NJ):
                act.wait_ge(cross_T, j + 1)
                copy(cross[:, j, :], psum[:, 2 + j % 2, 0:NQ]).then_inc(cross_sb, 1)

            act.wait_ge(w_arg, 1)
            nc.scalar.activation(es_w[:, :, :], es_w[:, :, :], ACT.Exp).then_inc(w_ready, 1)

            def hop_part(c, s, n):
                act.wait_ge(g2_ready[s], n * (16 * K))
                act.wait_ge(gat_steps, (c + 1) * K)
                settle()
                copy(msg2[:, s % 2, :, 0:F], gather2[:, s, :, 0:F]).then_inc(hopcopy, 1)

            with act.Fori(0, LOOPS) as i:
                for s in range(SL):
                    hop_part(i * SL + s, s, i + 1)
            for c in range(FULL, CH):
                hop_part(c, c % SL, c // SL + 1)

            for j in range(NJ):
                act.wait_ge(aT_ps, j + 1)
                copy(aT[:, 0:2, :], psum[:, 5, 0:2 * P].rearrange("p (c q) -> p c q", c=2)[:, :, 0:NQ])
                copy(aT[0:F, 2, :], psum[0:F, 5, 2 * P:2 * P + NQ]).then_inc(aT_sb, 1)
                act.wait_ge(catT_ps, j + 1)
                nc.scalar.activation(catT[:, :], psum[:, 6, 0:NQ], ACT.Identity, scale=cat_s[:, 0:1],
                                     bias=cat_s[:, 1:2]).then_inc(catT_sb, 1)
            for g in range(NG):
                act.wait_ge(ln_var, NG + g + 1)
                ln_sqrt(g).then_inc(ln_std, 1)

            act.wait_ge(packed, 2)
            act.wait_ge(pack_in, N_PACK * 16)
            with act.Fori(0, L) as l:
                copy(cur[:, 0:CW], pack[:, bass.ds(l, 1), :].rearrange("p a c -> p (a c)")).then_inc(cur_ready, 1)
                copy(cur_b[:, :], rows_b[:, bass.ds(l, 1), :].rearrange("p a c -> p (a c)")).then_inc(cur_ready, 1)
                act.wait_ge(cur_ready, l * 5 + 2)
                nc.scalar.mul(cur[:, C_W2N:C_W2N + F], cur[:, C_W2:C_W2 + F], -LEAK).then_inc(cur_ready, 1)
                nc.scalar.mul(cur[:, C_E2N:C_E2N + P], cur[:, C_E2:C_E2 + P], -LEAK).then_inc(cur_ready, 1)
                nc.scalar.mul(cur[:, C_B1N:C_B1N + 2], cur[:, C_B1:C_B1 + 2], -1.0).then_inc(cur_ready, 1)
                act.wait_ge(cur_ready, l * 5 + 5)
                settle()
                for g in range(NG):
                    act.wait_ge(xT_ps, l * NG + (g + 1))
                    copy(hT[:, :, :], psum[0:F, 0:2, :].rearrange("p b n -> p (b n)")[:, 0:GJ * P]
                         .rearrange("p (k n) -> p k n", n=P)[:, :, 0:NQ]).then_inc(xT_sb, 1)
                    act.wait_ge(y_ps, l * NG + (g + 1))
                    y = psum[:, 2:4, :].rearrange("p b n -> p (b n)")[:, 0:GJ * P]\
                        .rearrange("p (k n) -> p k n", n=P)[:, :, 0:NQ]
                    nc.scalar.activation(yp[:, :, :], y, ACT.Relu, bias=cur[:, C_B1:C_B1 + 1]).then_inc(y_sb, 1)
                    nc.scalar.activation(yn[:, :, :], y, ACT.Relu, bias=cur[:, C_B1N:C_B1N + 1], scale=-1.0)\
                        .then_inc(y_sb, 1)
                    act.wait_ge(h_ps, l * NG + (g + 1))
                    copy(hsb[:, grp(g), :], psum[0:NQ, 7, 0:GJ * F].rearrange("q (k f) -> q k f", f=F)).then_inc(h_sb, 1)

                def attr_copy(c, b):
                    act.wait_ge(at_ps, l * CH + c + 1)
                    copy(attr_T[:, b, :], psum[:, 5 + b, 0:256]).then_inc(at_sb, 1)

                def relu_edges(c, b):
                    act.wait_ge(ye_ps, l * CH + c + 1)
                    nc.scalar.activation(act_p[:, b, :], psum[:, b, :], ACT.Relu, bias=cur[:, C_BE1:C_BE1 + 1])\
                        .then_inc(ye_sb, 1)
                    nc.scalar.activation(act_n[:, b, :], psum[:, b, :], ACT.Relu, bias=cur[:, C_BE1N:C_BE1N + 1],
                                         scale=-1.0).then_inc(ye_sb, 1)

                attr_copy(0, 0)
                attr_copy(1, 1)
                relu_edges(0, 0)
                with act.Fori(0, LOOPS) as i:
                    for s in range(SL):
                        attr_copy(i * SL + (s + 2), s % 2)
                        relu_edges(i * SL + (s + 1), (s + 1) % 2)
                for c in range(FULL, CH):
                    if c + 2 < CH:
                        attr_copy(c + 2, c % 2)
                    if c + 1 < CH:
                        relu_edges(c + 1, (c + 1) % 2)

                for g in range(NG):
                    act.wait_ge(ln_var, l * NG + (2 * NG + g + 1))
                    ln_sqrt(g).then_inc(ln_std, 1)

        @block.tensor
        def _(pe):
            mm = nc.tensor.matmul

            def settle():
                pe.sem_inc(passed[1], 1)

            pe.wait_ge(consts_set, N_CONSTS)
            pe.wait_ge(att_in, 48)
            for h in range(H):
                ins = nc.tensor.transpose(psum[0:F, 0, h * F:(h + 1) * F], watt[:, h, :], ident[0:F, 0:F])
            ins.then_inc(v_T, 1)
            pe.wait_ge(v_Tsb, 1)
            for a in range(2):
                for h in range(H):
                    ins = mm(psum[0:F, 1, a * H + h:a * H + h + 1], wattT[:, h, :], avec[:, a, h:h + 1],
                             start=True, stop=True)
            ins.then_inc(v_ps, 1)

            def transpose_group(x_tile, bank, signal):
                for k in range(GJ):
                    ins = nc.tensor.transpose(psum[0:F, bank + k // 4, (k % 4) * P:(k % 4) * P + NQ],
                                              x_tile[:, k, :], ident[0:NQ, 0:NQ])
                ins.then_inc(signal, 1)

            for g in range(NG):
                pe.wait_ge(h0_ready, g + 1)
                if g:
                    pe.wait_ge(es_sb, 2 * g)
                transpose_group(t1[:, grp(g), 0:F], 2, h0_T)
                pe.wait_ge(h0_Tsb, g + 1)
                if g == 0:
                    pe.wait_ge(v_sb, 1)
                for k in range(GJ):
                    ins = mm(psum[0:NQ, 1, 64 + k * 2 * H:64 + (k + 1) * 2 * H], hT[:, k, :], vvec[:, :],
                             start=True, stop=True)
                ins.then_inc(es_ps, 1)

            pe.wait_ge(diag_ready, 1)
            for a in range(2):
                ins = mm(psum[:, 0, a * P:(a + 1) * P], ones[:, :], diag[:, a, :], start=True, stop=True)
            ins.then_inc(bc_ready, 1)

            degree = psum[0:NQ, 7, 0:NJ]
            mm(degree, zero16[:, :], zero16[:, 0:NJ], start=True, stop=False)

            def degrees(c, s):
                pe.wait_ge(hot_ready, c + 1)
                settle()
                for k in range(K):
                    ins = mm(degree, hot_q[:, s % 2, k, :], hot_j[:, s % 2, k, :], start=False, stop=False)
                ins.then_inc(hot_used, 1)

            pe.sem_inc(hot_used, 2)
            with pe.Fori(0, LOOPS) as i:
                for s in range(SL):
                    degrees(i * SL + s, s)
            for c in range(FULL, CH):
                degrees(c, c % SL)
            mm(degree, zero16[:, :], zero16[:, 0:NJ], start=False, stop=True).then_inc(deg_ready, 1)
            pe.wait_ge(rowtot, 1)
            mm(psum[0:NQ, 4, 0:1], above[0:NQ, 0:NQ], incl[:, NJ - 1:NJ], start=True, stop=True).then_inc(rowoff_ps, 1)
            pe.wait_ge(crossq_ready, 1)
            for j in range(NJ):
                if j >= 2:
                    pe.wait_ge(cross_sb, j - 1)
                nc.tensor.transpose(psum[:, 2 + j % 2, 0:NQ], crossq[:, j, :], ident[0:NQ, 0:NQ]).then_inc(cross_T, 1)

            def tails(tail, ready, used, base):
                for g in range(NG):
                    if g >= 2:
                        pe.wait_ge(used, base + (g - 1))
                        settle()
                    for k in range(GJ):
                        ins = mm(psum[0:NQ, 4 + g % 2, k * F:(k + 1) * F], cross[:, g * GJ + k, :], tail,
                                 start=True, stop=True)
                    ins.then_inc(ready, 1)

            pe.wait_ge(cross_sb, NJ)
            pe.wait_ge(hop_steps, CH * K)
            settle()
            tails(run1[:, (CH - 1) % SL, K - 1, :], c1_ready, c1_used, 0)

            for a in range(2):
                pe.wait_ge(diag4_ready, a + 1)
                mm(psum[:, a, :], ones[:, :], diag4[:, :, :].rearrange("p h n -> p (h n)"),
                   start=True, stop=True).then_inc(bc4_ready, 1)

            pe.wait_ge(gat_steps, (CH + 2) * K)
            settle()
            pe.wait_ge(weights_in, N_WEIGHTS * 16)
            tail2 = run2[:, (CH - 1) % 2, K - 1, :]
            for g in range(NG + 1):
                if g < NG:
                    for k in range(GJ):
                        j = g * GJ + k
                        if j >= 5:
                            pe.wait_ge(c2_used, j - 4)
                        mm(psum[0:NQ, j % 5, 0:WG], cross[:, j, :], tail2, start=True, stop=True).then_inc(c2_ready, 1)
                if g:
                    pe.wait_ge(cat2_ready, g)
                    for k in range(GJ):
                        j = (g - 1) * GJ + k
                        for c in range(3):
                            w = P if c < 2 else F
                            ins = nc.tensor.transpose(psum[0:w, 5, c * P:c * P + NQ], cat2[:, k, c * P:c * P + w],
                                                      ident[0:NQ, 0:NQ])
                        ins.then_inc(aT_ps, 1)
                        pe.wait_ge(aT_sb, j + 1)
                        mm(psum[0:F, 6, 0:NQ], wstack[:, 0, :], aT[:, 0, :], start=True, stop=False)
                        mm(psum[0:F, 6, 0:NQ], wstack[:, 1, :], aT[:, 1, :], start=False, stop=True)
                        mm(psum[F:P, 6, 0:NQ], wg_sb[:, :], aT[0:F, 2, :], start=True, stop=True).then_inc(catT_ps, 1)
                        pe.wait_ge(catT_sb, j + 1)
                        if k == 0 and g > 1:
                            pe.wait_ge(x1_used, g - 1)
                        o = psum[0:NQ, 7, k * F:(k + 1) * F]
                        mm(o, ones[0:1, 0:NQ], bw_row[0:1, :], start=True, stop=False)
                        ins = mm(o, catT[:, :], ww_sb[:, :], start=False, stop=True)
                        if k == GJ - 1:
                            ins.then_inc(x1_ps, 1)

            with pe.Fori(0, L) as l:
                w1 = cur[0:F, C_W1:C_W1 + F2]
                pe.wait_ge(cur_ready, l * 5 + 5)
                for g in range(NG):
                    pe.wait_ge(x_ready, l * NG + (g + 1))
                    settle()
                    transpose_group(xg[:, grp(g), :], 0, xT_ps)
                    pe.wait_ge(xT_sb, l * NG + (g + 1))
                    settle()
                    for k in range(GJ):
                        ins = mm(psum[:, 2 + k // 4, (k % 4) * P:(k % 4) * P + NQ], w1, hT[:, k, :], start=True, stop=True)
                    ins.then_inc(y_ps, 1)
                    pe.wait_ge(y_sb, l * (2 * NG) + 2 * (g + 1))
                    settle()
                    mm(psum[0:NQ, 7, 0:GJ * F], ones[0:1, 0:NQ],
                       cur_b[0:1, F:2 * F].unsqueeze(1).to_broadcast([1, GJ, F]), start=True, stop=False, skip_group_check=True)
                    for k in range(GJ):
                        o = psum[0:NQ, 7, k * F:(k + 1) * F]
                        mm(o, yp[:, k, :], cur[:, C_W2:C_W2 + F], start=False, stop=False, skip_group_check=True)
                        ins = mm(o, yn[:, k, :], cur[:, C_W2N:C_W2N + F], start=False, stop=(k == GJ - 1), skip_group_check=True)
                    ins.then_inc(h_ps, 1)
                    if g < NG - 1:
                        pe.wait_ge(h_sb, l * NG + (g + 1))
                        settle()

                def transpose_attr(c, s, n):
                    pe.wait_ge(attr_in[s], n * 16)
                    settle()
                    for u in range(2):
                        ins = nc.tensor.transpose(psum[:, 5 + s % 2, u * P:(u + 1) * P],
                                                  attr_nat[:, s, u * P:(u + 1) * P], ident[:, :])
                    ins.then_inc(at_ps, 1)

                def first_half(c, b):
                    pe.wait_ge(at_sb, l * CH + c + 1)
                    settle()
                    for u in range(4):
                        ins = mm(psum[:, b, u * P:(u + 1) * P], cur[:, C_E1 + (u % 2) * P:C_E1 + (u % 2 + 1) * P],
                                 attr_T[:, b, (u // 2) * P:(u // 2 + 1) * P], start=True, stop=True)
                    ins.then_inc(ye_ps, 1)

                def second_half(c, b):
                    pe.wait_ge(ye_sb, (l * CH + c + 1) * 2)
                    pe.wait_ge(edge_steps, (l * CH + c) * (K + 1) + 1)
                    settle()
                    mm(psum[:, 2 + b, :], ones[0:1, :], cur_b[0:1, 0:F].unsqueeze(1).to_broadcast([1, K, F]),
                       start=True, stop=False, skip_group_check=True)
                    for u in range(4):
                        o = psum[:, 2 + b, u * P:(u + 1) * P]
                        mm(o, act_p[:, b, u * P:(u + 1) * P], cur[:, C_E2:C_E2 + P], start=False, stop=False, skip_group_check=True)
                        ins = mm(o, act_n[:, b, u * P:(u + 1) * P], cur[:, C_E2N:C_E2N + P], start=False,
                                 stop=(u == 3), skip_group_check=True)
                    ins.then_inc(e_ready, 1)

                def arrivals(s):
                    return len(range(s, CH, SL))

                transpose_attr(0, 0, l * arrivals(0) + 1)
                transpose_attr(1, 1, l * arrivals(1) + 1)
                first_half(0, 0)
                with pe.Fori(0, LOOPS) as i:
                    for s in range(SL):
                        c = i * SL + s
                        s2 = (s + 2) % SL
                        transpose_attr(c + 2, s2, l * arrivals(s2) + i + (1 + (s + 2) // SL))
                        first_half(c + 1, (s + 1) % 2)
                        second_half(c, s % 2)
                for c in range(FULL, CH):
                    if c + 2 < CH:
                        s2 = (c + 2) % SL
                        transpose_attr(c + 2, s2, l * arrivals(s2) + ((c + 2) // SL + 1))
                    if c + 1 < CH:
                        first_half(c + 1, (c + 1) % 2)
                    second_half(c, c % 2)

                pe.wait_ge(edge_steps, 2 * (K + 1) + (l + 1) * (CH * (K + 1)))
                settle()
                tails(run1[:, (CH - 1) % SL, K - 1, :], cg_ready, cg_used, l * NG)

        @block.vector
        def _(dve):
            tt = nc.vector.tensor_tensor
            ts = nc.vector.tensor_scalar
            stt = nc.vector.scalar_tensor_tensor
            st = Steps(dve, dve_steps)

            def per_node(v, g, width=F):
                return v[:, grp(g)].unsqueeze(2).to_broadcast([NQ, GJ, width])

            def ln_stats(st, xs, g):
                b = g % 2
                st.then(nc.vector.tensor_reduce(st_sum[:, b, :], xs, AX.X, ALU.add))
                st.then(ts(st_sum[:, b, :], st_sum[:, b, :], 1.0 / F, None, ALU.mult))
                st.then(tt(cen[:, b, :, :], xs, st_sum[:, b, :].unsqueeze(2).to_broadcast([NQ, GJ, F]), ALU.subtract))
                st.then(tt(sq[:, :, :], cen[:, b, :, :], cen[:, b, :, :], ALU.mult))
                st.then(nc.vector.tensor_reduce(st_sum[:, b, :], sq[:, :, :], AX.X, ALU.add))
                ts(st_var[:, b, :], st_sum[:, b, :], 1.0 / F, EPS, ALU.mult, ALU.add).then_inc(ln_var, 1)

            def ln_scaled(st, g, n):
                b = g % 2
                dve.wait_ge(ln_std, n)
                st.then(nc.vector.reciprocal(st_std[:, b, :], st_std[:, b, :]))
                st.then(tt(cen[:, b, :, :], cen[:, b, :, :], st_std[:, b, :].unsqueeze(2).to_broadcast([NQ, GJ, F]), ALU.mult))

            def ln_relu(st, to, g, n, signal):
                ln_scaled(st, g, n)
                ts(to, cen[:, g % 2, :, :], 0.0, None, ALU.max).then_inc(signal, 1)

            dve.wait_ge(x_in, 16)
            for g in range(NG):
                ln_stats(st, xin[:, grp(g), :], g)
                if g:
                    ln_relu(st, t1[:, grp(g - 1), 0:F], g - 1, g, h0_ready)
            ln_relu(st, t1[:, grp(NG - 1), 0:F], NG - 1, NG, h0_ready)

            dve.wait_ge(edges_in, 64)
            for s in range(SL):
                nc.vector.tensor_copy(idx[:, s, :], src_i[:, s * K:(s + 1) * K]).then_inc(idx1, 1)
            st.then(nc.vector.tensor_copy(dst_f[:, :], dst_i[:, :]))
            st.done(nc.vector.memset(mask[:, 0:1], 0.0))
            st.done(nc.vector.memset(pen[:, T:T + 1], -BIG))
            st.then(tt(mask[:, 1:T], dst_f[:, 1:T], dst_f[:, 0:T - 1], ALU.is_equal))
            st.done(ts(pen[:, 0:T], mask[:, :], 1.0, BIG, ALU.subtract, ALU.mult))
            st.done(ts(pen_first[:, :], dst_f[:, :], dst_f[:, 0:1], 1.0, ALU.is_equal, ALU.subtract))
            st.then(ts(pen_last[:, :], dst_f[:, :], dst_f[:, T - 1:T], 1.0, ALU.is_equal, ALU.subtract))
            st.done(ts(pen_first[:, :], pen_first[:, :], BIG, None, ALU.mult))
            st.done(ts(pen_last[:, :], pen_last[:, :], BIG, None, ALU.mult))
            st.then(ts(d25[:, :], dst_f[:, :], 1.0 / NJ, 0.48, ALU.mult, ALU.subtract))
            st.then(ts(d25[:, :], d25[:, :], ROUND, ROUND, ALU.add, ALU.subtract))
            st.then(ts(d25[:, :], d25[:, :], float(NJ), None, ALU.mult))
            st.then(tt(drem[:, :], dst_f[:, :], d25[:, :], ALU.subtract))
            dve.wait_ge(consts_set, N_CONSTS)
            ts(diag[:, 0, :], ident[:, :], dst_f[:, T - 1:T], None, ALU.mult)
            ts(diag[:, 1, :], ident[:, :], dst_f[:, 0:1], None, ALU.mult).then_inc(diag_ready, 1)
            dve.wait_ge(bc_ready, 1)
            st.done(ts(pen_m[:, 0, :], psum[:, 0, 0:P], dst_f[:, 0:1], None, ALU.is_equal))
            st.then(ts(pen_m[:, 1, :], psum[:, 0, P:2 * P], dst_f[:, T - 1:T], None, ALU.is_equal))
            st.done(tt(pen_m[:, 0, :], pen_m[:, 0, :], below[:, :], ALU.mult))
            st.then(tt(pen_m[:, 1, :], pen_m[:, 1, :], above[:, :], ALU.mult))
            st.then(ts(pen_m[:, :, :], pen_m[:, :, :], 1.0, BIG, ALU.subtract, ALU.mult))

            def hop_chunk(c, s, n, more):
                prev = run1[:, (s - 1) % SL, K - 1, :]
                dve.wait_ge(g1_ready[s], n * (16 * K))
                dve.wait_ge(run1_free, c + 1)
                for k in range(K):
                    stt(run1[:, s, k, :], prev, mask[:, bass.ds(c * K + k, 1)], gather1[:, s, k, 0:F],
                        ALU.mult, ALU.add).then_inc(hop_steps, 1)
                    prev = run1[:, s, k, :]
                    if k == 0:
                        dve.wait_ge(hot_used, c + 1)
                        tt(hot_q[:, s % 2, :, :], d25[:, bass.ds(c * K, K)].unsqueeze(2).to_broadcast([P, K, NQ]),
                           q25[:, :].unsqueeze(1).to_broadcast([P, K, NQ]), ALU.is_equal)
                    if k == 1:
                        tt(hot_j[:, s % 2, :, :], drem[:, bass.ds(c * K, K)].unsqueeze(2).to_broadcast([P, K, NJ]),
                           jcol[:, :].unsqueeze(1).to_broadcast([P, K, NJ]), ALU.is_equal).then_inc(hot_ready, 1)
                    if k == 2:
                        nc.vector.tensor_copy(es_w[:, bass.ds(c * K, K), :], gather1[:, s, :, F:F + H]).then_inc(es_done, 1)
                    if k < K - 1:
                        dve.wait_ge(hop_steps, c * K + (k + 1))
                if more:
                    nc.vector.tensor_copy(idx[:, s, :], src_i[:, bass.ds((c + SL) * K, K)]).then_inc(idx1, 1)
                dve.wait_ge(hop_steps, c * K + K)

            with dve.Fori(0, LOOPS) as i:
                for s in range(SL):
                    hop_chunk(i * SL + s, s, i + 1, True)
            for c in range(FULL, CH):
                hop_chunk(c, c % SL, c // SL + 1, c + SL < CH)

            dve.wait_ge(deg_ready, 1)
            st.then(nc.vector.tensor_copy(deg, psum[0:NQ, 7, 0:NJ]))
            nc.vector.tensor_tensor_scan(incl, zeros[0:NQ, 0:NJ], deg, 0.0, ALU.add, ALU.add).then_inc(rowtot, 1)
            dve.wait_ge(rowoff_ps, 1)
            st.then(nc.vector.tensor_copy(rowoff[:, :], psum[0:NQ, 4, 0:1]))
            st.then(ts(last, incl, rowoff[:, 0:1], 1.0, ALU.add, ALU.subtract))
            st.then(ts(lastc, last, 0.0, None, ALU.max))
            nc.vector.tensor_copy(last_i[:, :], lastc).then_inc(last_ready, 1)
            st.then(tt(first, last, deg, ALU.subtract))
            st.done(ts(first, first, 1.0, None, ALU.add))
            st.done(ts(nonempty, deg, 0.5, None, ALU.is_gt))
            st.then(ts(cmean, deg, 1.0, None, ALU.max))
            st.then(nc.vector.reciprocal(cmean, cmean))
            st.done(tt(cmean, cmean, nonempty, ALU.mult))
            st.then(tt(tmpn, first, spare[0:NQ, :], ALU.subtract))
            st.then(tt(tmpn, tmpn, nonempty, ALU.mult))
            st.then(tt(tmpn, tmpn, spare[0:NQ, :], ALU.add))
            nc.vector.tensor_copy(slot_i[:, :], tmpn).then_inc(slots_ready, 1)
            dve.wait_ge(ed_zeroed, 32)
            dve.wait_ge(attr_padded, 32)
            bounds = bound[0:NQ, :].unsqueeze(1).to_broadcast([NQ, NJ, P])
            st.done(tt(crossq, bounds, first.unsqueeze(2).to_broadcast([NQ, NJ, P]), ALU.is_gt))
            st.then(tt(crossq2, bounds, last.unsqueeze(2).to_broadcast([NQ, NJ, P]), ALU.is_le))
            tt(crossq, crossq, crossq2, ALU.mult).then_inc(crossq_ready, 1)

            for g in range(NG):
                dve.wait_ge(agg1_in[g], GJ * 16)
                dve.wait_ge(c1_ready, g + 1)
                tt(agg[:, grp(g), :], agg[:, grp(g), :], psum[0:NQ, 4 + g % 2, 0:GJ * F].rearrange("q (k f) -> q k f", f=F),
                   ALU.add).then_inc(c1_used, 1)
                dve.wait_ge(c1_used, g + 1)
                tt(t2[:, grp(g), 0:F], agg[:, grp(g), :], per_node(cmean, g), ALU.mult).then_inc(t2_ready, 1)
            for s in range(SL):
                nc.vector.tensor_copy(idx[:, s, :], src_i[:, s * K:(s + 1) * K]).then_inc(idx2, 1)

            dve.wait_ge(edx_in, 16)
            dve.wait_ge(ed0_in, 16)
            dve.wait_ge(es_done, CH)
            st.then(nc.vector.tensor_copy(sm_a[:, 0, :], ed0[:, :]))
            for h in range(H):
                st.done(nc.vector.tensor_tensor_scan(sm_b[:, :, h], mask[:, :], sm_a[:, :, h], 0.0, ALU.mult, ALU.add))
            dve.wait_ge(dve_steps, st.n)
            st.then(tt(es_w[:, :, :], es_w[:, :, :], sm_b, ALU.add))
            st.then(stt(es_w[:, :, :].rearrange("p t h -> p (t h)"), es_w[:, :, :].rearrange("p t h -> p (t h)"), NEG,
                        es_w[:, :, :].rearrange("p t h -> p (t h)"), ALU.mult, ALU.max))
            for h in range(H):
                st.done(nc.vector.tensor_tensor_scan(sm_a[:, :, h], pen[:, 0:T], es_w[:, :, h], 0.0, ALU.add, ALU.max))
                st.done(nc.vector.tensor_tensor_scan(sm_b[:, ::-1, h], pen[:, T:0:-1], es_w[:, ::-1, h], 0.0,
                                                     ALU.add, ALU.max))
            dve.wait_ge(dve_steps, st.n)
            for a, state in ((0, sm_a[:, T - 1, :]), (1, sm_b[:, 0, :])):
                if a:
                    dve.wait_ge(bc4_ready, a)
                tt(diag4[:, :, :], ident[:, :].unsqueeze(1).to_broadcast([P, H, P]),
                   state.unsqueeze(2).to_broadcast([P, H, P]), ALU.mult).then_inc(diag4_ready, 1)
            st.then(tt(sm_a, sm_a, sm_b, ALU.max))
            for a in range(2):
                dve.wait_ge(bc4_ready, a + 1)
                st.then(tt(reached, psum[:, a, :].rearrange("p (h n) -> p h n", h=H),
                           pen_m[:, a, :].unsqueeze(1).to_broadcast([P, H, P]), ALU.add))
                st.then(nc.vector.tensor_reduce(carry[:, a, :], reached, AX.X, ALU.max))
            for a, reach in ((0, pen_first), (1, pen_last)):
                for h in range(H):
                    st.done(stt(sm_a[:, :, h], reach[:, :], carry[:, a, h:h + 1], sm_a[:, :, h], ALU.add, ALU.max))
                dve.wait_ge(dve_steps, st.n)
            tt(es_w[:, :, :], es_w[:, :, :], sm_a, ALU.subtract).then_inc(w_arg, 1)
            dve.wait_ge(w_ready, 1)

            def weigh(c, s, k):
                return tt(msg2[:, s % 2, k, F:WG].rearrange("p (h w) -> p h w", h=H),
                          gather2[:, s, k, F:W2R].unsqueeze(1).to_broadcast([P, H, WH]),
                          es_w[:, bass.ds(c * K + k, 1), :].rearrange("p a h -> p (a h)").unsqueeze(2)
                          .to_broadcast([P, H, WH]), ALU.mult)

            def gat_chunk(c, s, n2, more, ahead):
                dve.wait_ge(hopcopy, c + 1)
                dve.wait_ge(run2_free, c + 1)
                dve.wait_ge(msg_steps, (c + 1) * K)
                prev = run2[:, (s - 1) % 2, K - 1, :]
                for k in range(K):
                    stt(run2[:, s % 2, k, :], prev, mask[:, bass.ds(c * K + k, 1)], msg2[:, s % 2, k, :],
                        ALU.mult, ALU.add).then_inc(gat_steps, 1)
                    prev = run2[:, s % 2, k, :]
                    if ahead:
                        s1 = (s + 1) % SL
                        if k == 0:
                            dve.wait_ge(g2_ready[s1], n2 * (16 * K))
                        weigh(c + 1, s1, k).then_inc(msg_steps, 1)
                    if more and k == K - 1:
                        nc.vector.tensor_copy(idx[:, s, :], src_i[:, bass.ds((c + SL) * K, K)]).then_inc(idx2, 1)
                    dve.wait_ge(gat_steps, (c + 2) * K + (k + 1))

            dve.sem_inc(gat_steps, 2 * K)
            dve.wait_ge(g2_ready[0], 16 * K)
            for k in range(K):
                weigh(0, 0, k).then_inc(msg_steps, 1)
            with dve.Fori(0, LOOPS) as i:
                for s in range(SL):
                    gat_chunk(i * SL + s, s, i + (1 + (s + 1) // SL), True, True)
            for c in range(FULL, CH):
                gat_chunk(c, c % SL, (c + 1) // SL + 1, c + SL < CH, c + 1 < CH)

            def gat_nodes(g):
                dve.wait_ge(agg2_in[g], GJ * 16)
                for k in range(GJ):
                    j = g * GJ + k
                    dve.wait_ge(c2_ready, j + 1)
                    stt(agg2[:, j, :], agg2[:, j, :], nonempty[:, j:j + 1], psum[0:NQ, j % 5, 0:WG], ALU.mult, ALU.add)\
                        .then_inc(c2_used, 1)
                dve.wait_ge(c2_used, (g + 1) * GJ)
                heads = agg2[:, grp(g), F:WG].rearrange("q j (h w) -> q j h w", h=H)
                st.then(ts(recd[:, :, :], heads[:, :, :, F], 1e-16, None, ALU.max))
                st.then(nc.vector.reciprocal(recd[:, :, :], recd[:, :, :]))
                if g:
                    dve.wait_ge(aT_sb, g * GJ)
                for k in range(GJ):
                    st.done(tt(cat2[:, k, 0:H * F].rearrange("q (h f) -> q h f", h=H), heads[:, k, :, 0:F],
                               recd[:, k, :].unsqueeze(2).to_broadcast([NQ, H, F]), ALU.mult))
                tt(cat2[:, :, H * F:], agg2[:, grp(g), 0:F], per_node(cmean, g), ALU.mult).then_inc(cat2_ready, 1)

            def residual(g):
                dve.wait_ge(x1_ps, g + 1)
                tt(x1[:, grp(g), :], xin[:, grp(g), :], psum[0:NQ, 7, 0:GJ * F].rearrange("q (k f) -> q k f", f=F),
                   ALU.add).then_inc(x1_used, 1)
                dve.wait_ge(x1_used, g + 1)

            for g in range(NG):
                gat_nodes(g)
                if g:
                    residual(g - 1)
            residual(NG - 1)
            for g in range(NG):
                ln_stats(st, x1[:, grp(g), :], g)
                if g:
                    ln_relu(st, xg[:, grp(g - 1), :], g - 1, NG + g, x_ready)
            ln_relu(st, xg[:, grp(NG - 1), :], NG - 1, 2 * NG, x_ready)

            dve.sem_inc(edge_steps, 2 * (K + 1))
            dve.wait_ge(weights_in, N_WEIGHTS * 16)
            with dve.Fori(0, L) as l:
                for s in range(SL):
                    nc.vector.tensor_copy(idx[:, s, :], src_i[:, s * K:(s + 1) * K]).then_inc(idxg, 1)
                gs = Steps(dve, prep_steps, l * N_GINE_STEPS)
                dve.wait_ge(x_ready, l * NG + NG)
                gs.then(nc.vector.tensor_copy(cur_ln[:, :], lnp[:, bass.ds(l, 1), :].rearrange("q a c -> q (a c)")))
                gs.then(tt(cur_ln[:, 2 * F:2 * F + 1], cur_ln[:, 2 * F:2 * F + 1], cur_ln[:, 2 * F + 1:2 * F + 2], ALU.mult))
                gs.then(ts(msl, nonempty, cur_ln[:, 2 * F:2 * F + 1], None, ALU.mult))
                dve.sem_inc(passed[3], 1)

                def edge_chunk(c, s, n, more):
                    done = 2 * (K + 1) + (l * CH + c) * (K + 1)
                    prev = run1[:, (s - 1) % SL, K - 1, :]
                    dve.wait_ge(e_ready, l * CH + c + 1)
                    dve.wait_ge(gg_ready[s], n * (16 * K))
                    tt(msgg[:, :, :], psum[:, 2 + s % 2, :].rearrange("p (k f) -> p k f", f=F), gatherg[:, s, :, :],
                       ALU.mult).then_inc(edge_steps, 1)
                    dve.wait_ge(rung_free, l * CH + c + 1)
                    dve.wait_ge(edge_steps, done + 1)
                    for k in range(K):
                        stt(run1[:, s, k, :], prev, mask[:, bass.ds(c * K + k, 1)], msgg[:, k, :], ALU.mult, ALU.add)\
                            .then_inc(edge_steps, 1)
                        prev = run1[:, s, k, :]
                        if k == 0 and more:
                            nc.vector.tensor_copy(idx[:, s, :], src_i[:, bass.ds((c + SL) * K, K)]).then_inc(idxg, 1)
                        dve.wait_ge(edge_steps, done + (k + 2))

                with dve.Fori(0, LOOPS) as i:
                    for s in range(SL):
                        edge_chunk(i * SL + s, s, l * len(range(s, CH, SL)) + i + 1, True)
                for c in range(FULL, CH):
                    edge_chunk(c, c % SL, l * len(range(c % SL, CH, SL)) + (c // SL + 1), c + SL < CH)

                def affine(g):
                    b = g % 2
                    ln_scaled(gs, g, l * NG + (2 * NG + g + 1))
                    gs.then(tt(cen[:, b, :, :], cen[:, b, :, :], cur_ln[:, 0:F].unsqueeze(1).to_broadcast([NQ, GJ, F]),
                               ALU.mult))
                    tt(xg[:, grp(g), :], cen[:, b, :, :], cur_ln[:, F:2 * F].unsqueeze(1).to_broadcast([NQ, GJ, F]),
                       ALU.add).then_inc(x_ready, 1)

                for g in range(NG):
                    dve.wait_ge(aggg_in[g], l * (GJ * 16) + GJ * 16)
                    dve.wait_ge(cg_ready, l * NG + (g + 1))
                    a = agg[:, grp(g), :]
                    tt(a, a, psum[0:NQ, 4 + g % 2, 0:GJ * F].rearrange("q (k f) -> q k f", f=F), ALU.add).then_inc(cg_used, 1)
                    dve.wait_ge(cg_used, l * NG + (g + 1))
                    gs.then(tt(a, a, per_node(msl, g), ALU.mult))
                    gs.then(tt(a, a, xg[:, grp(g), :], ALU.add))
                    ln_stats(gs, a, g)
                    if g:
                        affine(g - 1)
                affine(NG - 1)
                assert gs.n == N_GINE_STEPS, gs.n

            dve.wait_ge(x_ready, (L + 1) * NG)
            tt(xin[:, :, :], x1[:, :, :], xg[:, :, :], ALU.add).then_inc(out_ready, 1)

    return nc


N_WEIGHTS = 4 + 1 + 2 + 4
N_PACK = 3 + 4 + 4
N_CONSTS = 17
N_GINE_STEPS = 3 + NG * (2 + 5 + 2 + 1)


def kernel(x, src, dst, edge_attr_32, **weights):
    import concourse.bacc as bacc
    from concourse.bass_utils import run_bass_kernel_spmd

    nc = bacc.Bacc("TRN2", target_bir_lowering=False, num_devices=1)
    names = ("W_att", "a_src", "a_dst", "W_g", "b_g", "W_w", "b_w")
    ordered = [x, src, dst, edge_attr_32] + [weights["L0_gnn_" + n] for n in names]
    names = ("W1", "b1", "W2", "b2", "We1", "be1", "We2", "be2", "res_w", "dot_scale", "ln_g", "ln_b")
    ordered += [weights["L1_gnn_" + n] for n in names]
    arrays, args = {}, []
    for i, a in enumerate(ordered):
        a = np.ascontiguousarray(a)
        arrays[f"in_{i}_dram"] = a
        args.append(nc.dram_tensor(f"in_{i}_dram", a.shape, mybir.dt.from_np(a.dtype), kind="ExternalInput").ap())
    out = nc.dram_tensor("out_dram", (N, F), F32, kind="ExternalOutput").ap()
    build(nc, *args, out)
    return run_bass_kernel_spmd(nc, [arrays], core_ids=[0]).results[0]["out_dram"]
```

```python
from contextlib import ExitStack

import numpy as np
import concourse.bass as bass
from concourse import mybir
from concourse.alu_op_type import AluOpType as ALU

ACT = mybir.ActivationFunctionType
AX = mybir.AxisListType
F32 = mybir.dt.float32
BF16 = mybir.dt.bfloat16
F16 = mybir.dt.float16
I32 = mybir.dt.int32

P = 128
N, F, E, ED = 3125, 64, 103125, 32
H, L = 4, 5
F2 = 2 * F
K = 8
SL = 4
T = -(-E // (P * K)) * K
EP = P * T
CH = T // K
LOOPS = CH // SL - 1
FULL = LOOPS * SL
LAST = E - (P - 1) * T
ON_PE = (2, 1)
PAIR = sum(ON_PE)
PE_COLS = (CH // 2) * PAIR + (CH % 2) * ON_PE[0]
NJ = 25
NQ = N // NJ
GJ = 5
NG = NJ // GJ
W1R = F + H
W2R = 2 * F + 1
WH = F + 1
WG = F + H * WH
BIG = 1.0e38
MID = N // 2
ROUND = 12582912.0
NEG = 0.2
LEAK = 0.1
EPS = 1e-5

C_W1 = 0
C_W2 = C_W1 + F2
C_E1 = C_W2 + F
C_E2 = C_E1 + 2 * P
C_B1 = C_E2 + P
C_BE1 = C_B1 + 1
CW = C_BE1 + 1
C_W2N = CW
C_E2N = C_W2N + F
C_B1N = C_E2N + P
C_BE1N = C_B1N + 1
CP = C_BE1N + 1


class Steps:

    def __init__(self, eng, sem, base=0):
        self.eng, self.sem, self.base, self.n = eng, sem, base, 0

    def done(self, ins):
        self.n += 1
        ins.then_inc(self.sem, 1)
        return self.n

    def wait(self, n):
        self.eng.wait_ge(self.sem, self.base + n)

    def then(self, ins):
        self.wait(self.done(ins))


def build(nc, x, src, dst, attr, W_att, a_src, a_dst, W_g, b_g, W_w, b_w, W1, b1, W2, b2, We1, be1, We2, be2,
          res_w, dot_scale, ln_g, ln_b, out):
    ctx = ExitStack()
    with ctx:
        def sb(name, shape, dt=F32):
            return ctx.enter_context(nc.sbuf_tensor(name, shape, dt))

        def sem(name):
            return ctx.enter_context(nc.semaphore(name))

        def dram(name, shape, dt=F32):
            return nc.dram_tensor(name, shape, dt, kind="Internal").ap()

        attr_pad = dram("attr_pad", (EP, ED))
        table1 = dram("table1", (N, W1R))
        table2 = dram("table2", (N, W2R))
        tableh = dram("tableh", (N, F))
        rows1 = dram("rows1", (EP + 1, F))
        rows2 = dram("rows2", (EP + 1, WG))
        rowsg = dram("rowsg", (EP + 1, F))
        ed_nodes = dram("ed_nodes", (N, H))
        ed_edges = dram("ed_edges", (EP + N, H))

        pe_src = dram("pe_src", (PE_COLS, P), F16)

        src_i = sb("src_i", [P, T], I32)
        dst_i = sb("dst_i", [P, T], I32)
        dst_f = sb("dst_f", [P, T])
        mask = sb("mask", [P, T])
        penalty = sb("penalty", [P, 3 * T + 1])
        pen = penalty[:, 0:T + 1]
        pen_first = penalty[:, T + 1:2 * T + 1]
        pen_last = penalty[:, 2 * T + 1:]
        parts = penalty[0:NQ, 0:NJ * 3 * F // 2].bitcast(BF16)\
            .rearrange("q (j a f) -> q j a f", j=NJ, a=3)
        es_w = sb("es_w", [P, T, H])
        union = sb("union", [P, NJ * WG])
        agg2 = union[0:NQ, :].rearrange("q (j w) -> q j w", w=WG)
        crossq = union[0:NQ, 0:NJ * P].rearrange("q (j p) -> q j p", p=P)
        crossq2 = union[0:NQ, NJ * P:2 * NJ * P].rearrange("q (j p) -> q j p", p=P)
        sm_a = union[:, 0:T * H].rearrange("p (t h) -> p t h", h=H)
        sm_b = union[:, T * H:2 * T * H].rearrange("p (t h) -> p t h", h=H)
        d25 = union[:, 2 * T * H:2 * T * H + T]
        drem = union[:, 2 * T * H + T:2 * T * H + 2 * T]
        reached = union[:, 2 * T * H:2 * T * H + H * P].rearrange("p (h n) -> p h n", h=H)
        zeros = union[:, 0:T * H // 2]
        hot = union[:, 0:2 * NJ * max(ON_PE) * P // 2].bitcast(BF16)[0:NQ, :]\
            .rearrange("q (b j m e) -> q b j m e", b=2, j=NJ, e=P)
        node_id = sb("node_id", [NQ, NJ, P], F16)
        src_row = dst_f[0:NQ, 0:SL * max(ON_PE) * P // 2].bitcast(F16)\
            .rearrange("q (s m e) -> q s m e", s=SL, e=P)
        src_cols = sb("src_cols", [P, PE_COLS])
        src_T = sb("src_T", [P, 2, P], F16)
        diag4 = sb("diag4", [P, H, P])
        flat4 = diag4[0:96, :, :].rearrange("p h n -> p (h n)")
        be_rows = flat4[:, 0:L * F].rearrange("p (l f) -> p l f", l=L)
        be_tmp = flat4[:, L * F:L * F + L * F // 2].bitcast(BF16).rearrange("p (l f) -> p l f", l=L)
        be_parts = sb("be_parts", [96, L, F], BF16)
        cur_be = sb("cur_be", [96, F], BF16)
        ones16 = sb("ones16", [96, P], BF16)
        cross = sb("cross", [P, NJ, NQ])
        idx = sb("idx", [P, SL, K], I32)
        gring = sb("gring", [P, SL * K * W2R])
        pack = es_w[:, :, :].rearrange("p t h -> p (t h)")[:, 0:L * CW].rearrange("p (l c) -> p l c", l=L)
        gather1 = gring[:, 0:SL * K * W1R].rearrange("p (s k w) -> p s k w", s=SL, k=K)
        gather2 = gring[:, :].rearrange("p (s k w) -> p s k w", s=SL, k=K)
        gatherg = gring[:, 0:SL * K * F].rearrange("p (s k w) -> p s k w", s=SL, k=K)
        stage = sb("stage", [P, 4 * K * WG])
        msg2 = stage[:, 0:2 * K * WG].rearrange("p (b k w) -> p b k w", b=2, k=K)
        run2 = stage[:, 2 * K * WG:].rearrange("p (b k w) -> p b k w", b=2, k=K)
        t1 = stage[0:NQ, 0:NJ * W1R].rearrange("q (j w) -> q j w", w=W1R)
        t2 = stage[0:NQ, NJ * W1R:NJ * (W1R + W2R)].rearrange("q (j w) -> q j w", w=W2R)
        used = [0]

        def part(width):
            used[0] += width
            return stage[:, used[0] - width:used[0]]

        attr_nat = part(SL * K * ED).rearrange("p (s d) -> p s d", s=SL)
        attr_T = part(2 * K * ED).rearrange("p (b d) -> p b d", b=2)
        act_p = part(8 * P).rearrange("p (b n) -> p b n", b=2)
        act_n = part(8 * P).rearrange("p (b n) -> p b n", b=2)
        cat2 = gring[0:NQ, 0:2 * GJ * (H + 1) * F].rearrange("q (b k w) -> q b k w", b=2, k=GJ)
        aT = gring[:, 2 * GJ * (H + 1) * F:2 * GJ * (H + 1) * F + 6 * NQ].rearrange("p (b c q) -> p b c q", b=2, c=3)
        msgg = part(K * F).rearrange("p (k f) -> p k f", k=K)
        yp = part(GJ * NQ).rearrange("p (k n) -> p k n", k=GJ)
        yn = part(GJ * NQ).rearrange("p (k n) -> p k n", k=GJ)
        cur = part(CP)
        hsb = part(NJ * F)[0:NQ, :].rearrange("q (j f) -> q j f", j=NJ)
        run1 = sb("run1", [P, SL, K, F])
        hot_q = sb("hot_q", [P, 2, K, NQ], BF16)
        hot_j = sb("hot_j", [P, 2, K, NJ], BF16)
        q25 = sb("q25", [P, NQ])
        jcol = sb("jcol", [P, NJ])
        bound = sb("bound", [P, P])
        spare = sb("spare", [P, NJ])
        ident = sb("ident", [P, P])
        below = sb("below", [P, P])
        above = sb("above", [P, P])
        zero16 = sb("zero16", [P, NQ], BF16)
        ones = sb("ones", [P, P])
        xin = sb("xin", [NQ, NJ, F])
        x1 = sb("x1", [NQ, NJ, F])
        xg = sb("xg", [NQ, NJ, F])
        agg = sb("agg", [NQ, NJ, F])
        ed_sb = sb("ed_sb", [NQ, NJ, H])
        ed0 = sb("ed0", [P, H])
        cen = sb("cen", [NQ, 2, GJ, F])
        sq = sb("sq", [NQ, GJ, F])
        st_sum = sb("st_sum", [NQ, 2, GJ])
        st_var = sb("st_var", [NQ, 2, GJ])
        st_std = sb("st_std", [NQ, 2, GJ])
        eps_f = sb("eps_f", [NQ, 1])
        node = sb("node", [NQ, 8, NJ])
        deg, incl, last, first = (node[:, i, :] for i in range(4))
        nonempty, cmean, tmpn, lastc = (node[:, i, :] for i in range(4, 8))
        rowoff = sb("rowoff", [NQ, 1])
        last_i = sb("last_i", [NQ, NJ], I32)
        slot_i = sb("slot_i", [NQ, NJ], I32)
        edge1 = sb("edge1", [P, 2, H])
        diag = sb("diag", [P, 2, P])
        pen_m = sb("pen_m", [P, 2, P])
        carry = sb("carry", [P, 2, H])
        watt = sb("watt", [F, H, F])
        wattT = sb("wattT", [F, H, F])
        wstack = sb("wstack", [P, 2, F])
        avec = sb("avec", [F, 2, H])
        vvec = sb("vvec", [F, 2 * H])
        wg_sb = sb("wg_sb", [F, F])
        ww_sb = sb("ww_sb", [P, F])
        cat_s = sb("cat_s", [P, 2])
        bw_row = sb("bw_row", [1, F])
        hT = sb("hT", [F, GJ, NQ])
        catT = sb("catT", [P, NQ])
        recd = sb("recd", [NQ, GJ, H])
        rows_b = sb("rows_b", [1, L, F])
        cur_b = sb("cur_b", [1, F])
        lnp = sb("lnp", [NQ, L, 2 * F + 2])
        cur_ln = sb("cur_ln", [NQ, 2 * F + 2])

        psum = ctx.enter_context(nc.psum_tensor("psum", [P, 8, 512], F32))

        passed = [sem(f"passed_{e}") for e in ("pool", "pe", "act", "dve")]
        pads_set, consts_set, pack_zero = sem("pads_set"), sem("consts_set"), sem("pack_zero")
        x_in, edges_in, att_in, weights_in = sem("x_in"), sem("edges_in"), sem("att_in"), sem("weights_in")
        attr_padded, ed_zeroed = sem("attr_padded"), sem("ed_zeroed")
        ln_var, ln_std = sem("ln_var"), sem("ln_std")
        dve_steps, prep_steps, act_steps = sem("dve_steps"), sem("prep_steps"), sem("act_steps")
        v_T, v_Tsb, v_ps, v_sb = sem("v_T"), sem("v_Tsb"), sem("v_ps"), sem("v_sb")
        h0_ready, h0_T, h0_Tsb, es_ps, es_sb, t1_out = (sem(n) for n in (
            "h0_ready", "h0_T", "h0_Tsb", "es_ps", "es_sb", "t1_out"))
        ed_out = sem("ed_out")
        idx1, g1_ready = sem("idx1"), [sem(f"g1_ready{s}") for s in range(SL)]
        hop_steps, hot_ready, hot_used, es_done = sem("hop_steps"), sem("hot_ready"), sem("hot_used"), sem("es_done")
        run1_free, rows1_out, rows1_all = sem("run1_free"), sem("rows1_out"), sem("rows1_all")
        deg_ready, rowtot, rowoff_ps, last_ready = sem("deg_ready"), sem("rowtot"), sem("rowoff_ps"), sem("last_ready")
        crossq_ready, cross_T, cross_sb = sem("crossq_ready"), sem("cross_T"), sem("cross_sb")
        slots_ready, ed_scattered, ed0_in, edx_in = sem("slots_ready"), sem("ed_scattered"), sem("ed0_in"), sem("edx_in")
        agg1_in = [sem(f"agg1_in{g}") for g in range(NG)]
        c1_ready, c1_used, t2_ready, t2h_ready, t2_out = (sem(n) for n in (
            "c1_ready", "c1_used", "t2_ready", "t2h_ready", "t2_out"))
        diag_ready, bc_ready, diag4_ready, bc4_ready = sem("diag_ready"), sem("bc_ready"), sem("diag4_ready"), sem("bc4_ready")
        w_arg, w_ready = sem("w_arg"), sem("w_ready")
        idx2, g2_ready = sem("idx2"), [sem(f"g2_ready{s}") for s in range(SL)]
        hopcopy, msg_steps, gat_steps = sem("hopcopy"), sem("msg_steps"), sem("gat_steps")
        run2_free, rows2_out, rows2_all = sem("run2_free"), sem("rows2_out"), sem("rows2_all")
        agg2_in = [sem(f"agg2_in{g}") for g in range(NG)]
        c2_ready, c2_used, cat2_ready, aT_ps, aT_sb = (sem(n) for n in (
            "c2_ready", "c2_used", "cat2_ready", "aT_ps", "aT_sb"))
        catT_ps, catT_sb, x1_ps, x1_used = sem("catT_ps"), sem("catT_sb"), sem("x1_ps"), sem("x1_used")
        x_ready, packed, pack_in, cur_ready = sem("x_ready"), sem("packed"), sem("pack_in"), sem("cur_ready")
        xT_ps, xT_sb, y_ps, y_sb, h_ps, h_sb, table_out = (sem(n) for n in (
            "xT_ps", "xT_sb", "y_ps", "y_sb", "h_ps", "h_sb", "table_out"))
        idxg, gg_ready = sem("idxg"), [sem(f"gg_ready{s}") for s in range(SL)]
        attr_in = [sem(f"attr_in{s}") for s in range(SL)]
        at_ps, at_sb, ye_ps, ye_sb, e_ready, edge_steps = (sem(n) for n in (
            "at_ps", "at_sb", "ye_ps", "ye_sb", "e_ready", "edge_steps"))
        rung_free, rowsg_out, rowsg_all = sem("rung_free"), sem("rowsg_out"), sem("rowsg_all")
        aggg_in = [sem(f"aggg_in{g}") for g in range(NG)]
        cg_ready, cg_used = sem("cg_ready"), sem("cg_used")
        src_cols_set, src_T_ps, src_T_sb, pe_src_out = (sem(n) for n in (
            "src_cols_set", "src_T_ps", "src_T_sb", "pe_src_out"))
        src_in = [sem(f"src_in{s}") for s in range(SL)]
        found_ps, found_sb = sem("found_ps"), sem("found_sb")
        hot_done, parts_ready, be_steps = sem("hot_done"), sem("parts_ready"), sem("be_steps")
        out_ready, out_done = sem("out_ready"), sem("out_done")

        def chunk_rows(rows, c, width):
            return rows[0:EP, :].rearrange("(p t) w -> p t w", p=P)[:, bass.ds(c * K, K), 0:width]

        def node_rows(table):
            return table.rearrange("(q j) w -> q j w", j=NJ)

        def grp(g):
            return slice(g * GJ, (g + 1) * GJ)

        block = ctx.enter_context(nc.Block())

        @block.sync
        def _(sp):
            sp.dma_start(xin[:, :, :], x.rearrange("(q j) f -> q j f", j=NJ)).then_inc(x_in, 16)
            sp.dma_start(watt[:, :, :], W_att.rearrange("h i o -> i h o")).then_inc(att_in, 16)
            with nc.allow_non_contiguous_dma(reason="two vectors of 256 elements"):
                sp.dma_start(avec[:, 0, :], a_src.rearrange("h o -> o h")).then_inc(att_in, 16)
                sp.dma_start(avec[:, 1, :], a_dst.rearrange("h o -> o h")).then_inc(att_in, 16)
            sp.wait_ge(pads_set, 2)
            for to, of in ((src_i, src), (dst_i, dst)):
                sp.dma_start(to[0:P - 1, :], of[0:(P - 1) * T].rearrange("(p t) -> p t", p=P - 1))\
                    .then_inc(edges_in, 16)
                sp.dma_start(to[P - 1:P, 0:LAST], of[(P - 1) * T:E].rearrange("(p t) -> p t", p=1))\
                    .then_inc(edges_in, 16)
            for g in range(NG):
                sp.wait_ge(es_sb, 2 * g + 2)
                sp.dma_start(node_rows(table1)[:, grp(g), :], t1[:, grp(g), :]).then_inc(t1_out, 16)
            sp.dma_start(node_rows(ed_nodes), ed_sb[:, :, :]).then_inc(ed_out, 16)
            sp.wait_ge(consts_set, 2)
            half = ed_edges[0:EP, :].rearrange("(p a t) h -> p a (t h)", p=P, a=2)
            for a in range(2):
                sp.dma_start(half[:, a, :], zeros[:, :]).then_inc(ed_zeroed, 16)
            for rows, width in ((rows1, F), (rows2, WG), (rowsg, F)):
                sp.dma_start(rows[EP:EP + 1, :], zeros[0:1, 0:width]).then_inc(ed_zeroed, 16)
            sp.dma_start(attr_pad[0:E, :].rearrange("(a b) d -> a (b d)", b=E // 375),
                         attr.rearrange("(a b) d -> a (b d)", b=E // 375)).then_inc(attr_padded, 16)
            tail = EP - E
            sp.dma_start(attr_pad[E:EP, :].rearrange("(a b) d -> a (b d)", b=tail // 23),
                         zeros[0:23, 0:tail // 23 * ED]).then_inc(attr_padded, 16)
            sp.dma_start(wstack[:, :, :], W_att.rearrange("(c b) i o -> (b i) c o", b=2)).then_inc(weights_in, 16)
            sp.dma_start(wg_sb[:, :], W_g).then_inc(weights_in, 16)
            sp.dma_start(ww_sb[:, :], W_w).then_inc(weights_in, 16)
            sp.dma_start(bw_row[:, :], b_w.rearrange("(a f) -> a f", a=1)).then_inc(weights_in, 16)
            sp.wait_ge(consts_set, N_CONSTS)
            with nc.allow_non_contiguous_dma(reason="bias vector"):
                sp.dma_start(cat_s[F:P, 1:2], b_g.rearrange("(f a) -> f a", a=1)).then_inc(weights_in, 16)
            for k in range(3):
                sp.dma_start(be_rows[32 * k:32 * k + 1, :, :], be2.rearrange("(a l) f -> a l f", a=1)).then_inc(weights_in, 16)
            sp.dma_start(rows_b[:, :, :], b2.rearrange("(a l) f -> a l f", a=1)).then_inc(weights_in, 16)
            sp.dma_start(lnp[:, :, 0:F], ln_g.partition_broadcast(NQ)).then_inc(weights_in, 16)
            sp.dma_start(lnp[:, :, F:2 * F], ln_b.partition_broadcast(NQ)).then_inc(weights_in, 16)
            with nc.allow_non_contiguous_dma(reason="one number per layer"):
                sp.dma_start(lnp[:, :, 2 * F], dot_scale.partition_broadcast(NQ)).then_inc(weights_in, 16)
                sp.dma_start(lnp[:, :, 2 * F + 1], res_w.partition_broadcast(NQ)).then_inc(weights_in, 16)

            sp.wait_ge(src_T_sb, 1)
            sp.dma_start(pe_src[0:P, :], src_T[:, 0, :]).then_inc(pe_src_out, 16)
            sp.dma_start(pe_src[P:, :], src_T[0:PE_COLS - P, 1, :]).then_inc(pe_src_out, 16)

            def store1(c, s):
                sp.wait_ge(hop_steps, (c + 1) * K)
                sp.dma_start(chunk_rows(rows1, c, F), run1[:, s, :, :]).then_inc(rows1_out, 16)
                sp.wait_ge(rows1_out, (c + 1) * 16)
                sp.sem_inc(run1_free, 1)

            sp.sem_inc(run1_free, SL)
            with sp.Fori(0, LOOPS) as i:
                for s in range(SL):
                    store1(i * SL + s, s)
            for c in range(FULL, CH):
                store1(c, c % SL)
            sp.sem_inc(rows1_all, 1)

            for g in range(NG):
                sp.wait_ge(t2_ready, g + 1)
                if g == 0:
                    sp.wait_ge(t2h_ready, 1)
                sp.dma_start(node_rows(table2)[:, grp(g), :], t2[:, grp(g), :]).then_inc(t2_out, 16)
            sp.wait_ge(ed_scattered, NJ * 16)
            sp.wait_ge(cross_sb, NJ)
            sp.dma_start(sm_a, ed_edges[0:EP, :].rearrange("(p t) h -> p t h", p=P)).then_inc(edx_in, 16)

            def store2(c, s):
                sp.wait_ge(gat_steps, (c + 3) * K)
                sp.dma_start(chunk_rows(rows2, c, WG), run2[:, s % 2, :, :]).then_inc(rows2_out, 16)
                sp.wait_ge(rows2_out, (c + 1) * 16)
                sp.sem_inc(run2_free, 1)

            sp.sem_inc(run2_free, 2)
            with sp.Fori(0, LOOPS) as i:
                for s in range(SL):
                    store2(i * SL + s, s)
            for c in range(FULL, CH):
                store2(c, c % SL)
            sp.sem_inc(rows2_all, 1)

            sp.wait_ge(pack_zero, 1)
            loads = [(pack[0:F, :, C_W1:C_W1 + F2], W1.rearrange("l d m -> d l m")),
                     (pack[:, :, C_W2:C_W2 + F], W2.rearrange("l m d -> m l d")),
                     (pack[:, :, C_B1], b1.rearrange("l m -> m l"))]
            for q in range(4):
                col = C_E1 + (q // 2) * P + (q % 2) * F
                loads.append((pack[q * ED:(q + 1) * ED, :, col:col + F], We1.rearrange("l a d -> a l d")))
            for q in range(2):
                col = C_E2 + q * F
                loads.append((pack[q * F:(q + 1) * F, :, col:col + F], We2.rearrange("l d e -> d l e")))
                loads.append((pack[q * F:(q + 1) * F, :, C_BE1], be1.rearrange("l d -> d l")))
            assert len(loads) == N_PACK
            with nc.allow_non_contiguous_dma(reason="bias vectors"):
                for to, of in loads:
                    sp.dma_start(to, of).then_inc(pack_in, 16)

            def load_attr(c, s):
                return sp.dma_start(attr_nat[:, s, :].rearrange("p (k d) -> p k d", d=ED),
                                    chunk_rows(attr_pad, c, ED)).then_inc(attr_in[s], 16)

            def load_src(pair, s):
                m = ON_PE[s % 2]
                of = pe_src[bass.ds(pair * PAIR + (s % 2) * ON_PE[0], m), :].rearrange("m e -> (m e)")
                sp.dma_start(src_row[:, s, 0:m, :].rearrange("q m e -> q (m e)"), of.partition_broadcast(NQ))\
                    .then_inc(src_in[s], 16)

            def store_g(l, c, s):
                sp.wait_ge(edge_steps, 2 * (K + 1) + (l * CH + c + 1) * (K + 1))
                sp.dma_start(chunk_rows(rowsg, c, F), run1[:, s, :, :]).then_inc(rowsg_out, 16)
                sp.wait_ge(rowsg_out, (l * CH + c + 1) * 16)
                sp.sem_inc(rung_free, 1)

            sp.sem_inc(rung_free, SL)
            sp.wait_ge(attr_padded, 32)
            sp.wait_ge(pe_src_out, 32)
            sp.wait_ge(x_ready, NG)
            with sp.Fori(0, L) as l:
                for c in range(SL):
                    load_src(c // 2, c)
                    load_attr(c, c)
                for g in range(NG):
                    sp.wait_ge(h_sb, l * NG + g + 1)
                    sp.dma_start(node_rows(tableh)[:, grp(g), :], hsb[:, grp(g), :]).then_inc(table_out, 16)
                with sp.Fori(0, LOOPS) as i:
                    for s in range(SL):
                        c = i * SL + s
                        sp.wait_ge(at_ps, l * CH + c + 1)
                        load_attr(c + SL, s)
                        sp.wait_ge(hot_done, l * CH + c + 1)
                        load_src(i * (SL // 2) + (s + SL) // 2, s)
                        store_g(l, c, s)
                for c in range(FULL, CH):
                    if c + SL < CH:
                        sp.wait_ge(at_ps, l * CH + (c + 1))
                        load_attr(c + SL, c % SL)
                        sp.wait_ge(hot_done, l * CH + (c + 1))
                        load_src((c + SL) // 2, c % SL)
                    store_g(l, c, c % SL)
                sp.sem_inc(rowsg_all, 1)

            sp.wait_ge(out_ready, 1)
            sp.dma_start(out.rearrange("(q j) f -> q j f", j=NJ), xin[:, :, :]).then_inc(out_done, 16)
            sp.wait_ge(out_done, 16)

        @block.gpsimd
        def _(pool):
            def settle():
                pool.sem_inc(passed[0], 1)

            pool.memset(src_i[:, :], 0).then_inc(pads_set, 1)
            pool.memset(dst_i[:, :], 4095).then_inc(pads_set, 1)
            pool.memset(ident[:, :], 0.0).then_inc(consts_set, 1)
            pool.memset(zeros[:, :], 0.0).then_inc(consts_set, 1)
            pool.memset(below[:, :], 1.0).then_inc(consts_set, 1)
            pool.memset(above[:, :], 1.0).then_inc(consts_set, 1)
            pool.wait_ge(consts_set, 4)
            pool.affine_select(out=ident[:, :], in_=ident[:, :], compare_op=ALU.not_equal, fill=1.0, base=0,
                               pattern=[[-1, P]], channel_multiplier=1).then_inc(consts_set, 1)
            pool.affine_select(out=below[:, :], in_=below[:, :], compare_op=ALU.is_gt, fill=0.0, base=0,
                               pattern=[[-1, P]], channel_multiplier=1).then_inc(consts_set, 1)
            pool.affine_select(out=above[:, :], in_=above[:, :], compare_op=ALU.is_gt, fill=0.0, base=0,
                               pattern=[[1, P]], channel_multiplier=-1).then_inc(consts_set, 1)
            pool.iota(q25[:, :], [[NJ, NQ]], base=0, channel_multiplier=0,
                      allow_small_or_imprecise_dtypes=True).then_inc(consts_set, 1)
            pool.iota(jcol[:, :], [[1, NJ]], base=0, channel_multiplier=0,
                      allow_small_or_imprecise_dtypes=True).then_inc(consts_set, 1)
            pool.iota(bound[:, :], [[T, P]], base=T, channel_multiplier=0,
                      allow_small_or_imprecise_dtypes=True).then_inc(consts_set, 1)
            pool.iota(spare[:, :], [[1, NJ]], base=EP, channel_multiplier=NJ,
                      allow_small_or_imprecise_dtypes=True).then_inc(consts_set, 1)
            pool.memset(zero16[:, :], 0.0).then_inc(consts_set, 1)
            pool.memset(ones[:, :], 1.0).then_inc(consts_set, 1)
            pool.memset(t2[:, :, 2 * F:], 1.0).then_inc(consts_set, 1)
            pool.memset(run1[:, SL - 1, K - 1, :], 0.0).then_inc(consts_set, 1)
            pool.memset(run2[:, 1, K - 1, :], 0.0).then_inc(consts_set, 1)
            pool.memset(cat_s[:, :], 0.0).then_inc(consts_set, 1)
            pool.memset(eps_f[:, :], F * F * EPS).then_inc(consts_set, 1)
            pool.memset(be_rows[:, :, :], 0.0).then_inc(consts_set, 1)
            pool.memset(ones16[:, :], 1.0).then_inc(consts_set, 1)
            pool.iota(node_id[:, :, :], [[1, NJ], [0, P]], base=-MID, channel_multiplier=NJ,
                      allow_small_or_imprecise_dtypes=True).then_inc(consts_set, 1)

            def gather_chunk(idx_ready, n, table, ring, ready, s, on_pe):
                pool.wait_ge(idx_ready, n)
                settle()
                for k in range(K - on_pe[s % 2]):
                    pool.indirect_dma_start(ring[:, s, k, :], None, table,
                                            bass.IndirectOffsetOnAxis(ap=idx[:, s, k:k + 1], axis=0))\
                        .then_inc(ready[s], 16)

            def gather_pass(idx_ready, base, table, ring, ready, on_pe=(0, 0)):
                with pool.Fori(0, LOOPS) as i:
                    for s in range(SL):
                        gather_chunk(idx_ready, base + i * SL + (s + 1), table, ring, ready, s, on_pe)
                for c in range(FULL, CH):
                    gather_chunk(idx_ready, base + (c + 1), table, ring, ready, c % SL, on_pe)

            def gather_nodes(rows, to, arrived):
                for j in range(NJ):
                    pool.indirect_dma_start(to[:, j, :], None, rows,
                                            bass.IndirectOffsetOnAxis(ap=last_i[:, j:j + 1], axis=0))\
                        .then_inc(arrived[j // GJ], 16)

            pool.wait_ge(t1_out, NG * 16)
            gather_pass(idx1, 0, table1, gather1, g1_ready)
            pool.wait_ge(rows1_all, 1)
            pool.wait_ge(last_ready, 1)
            pool.wait_ge(ed_zeroed, 80)
            settle()
            gather_nodes(rows1, agg, agg1_in)
            pool.wait_ge(slots_ready, 1)
            pool.wait_ge(ed_out, 16)
            settle()
            for j in range(NJ):
                pool.indirect_dma_start(ed_edges, bass.IndirectOffsetOnAxis(ap=slot_i[:, j:j + 1], axis=0),
                                        ed_sb[:, j, :], None).then_inc(ed_scattered, 16)
            pool.indirect_dma_start(ed0[:, :], None, ed_nodes,
                                    bass.IndirectOffsetOnAxis(ap=dst_i[:, 0:1], axis=0)).then_inc(ed0_in, 16)
            pool.wait_ge(t2_out, NG * 16)
            settle()
            gather_pass(idx2, 0, table2, gather2, g2_ready)
            pool.wait_ge(rows2_all, 1)
            settle()
            gather_nodes(rows2, agg2, agg2_in)
            pool.memset(pack, 0.0).then_inc(pack_zero, 1)
            with pool.Fori(0, L) as l:
                pool.wait_ge(table_out, (l + 1) * (NG * 16))
                settle()
                gather_pass(idxg, l * CH, tableh, gatherg, gg_ready, ON_PE)
                pool.wait_ge(rowsg_all, l + 1)
                settle()
                gather_nodes(rowsg, agg, aggg_in)

        def es_group(act, copy, g):
            act.wait_ge(h0_T, g + 1)
            copy(hT[:, :, :], psum[0:F, 2:4, :].rearrange("p b n -> p (b n)")[:, 0:GJ * P]
                 .rearrange("p (k n) -> p k n", n=P)[:, :, 0:NQ]).then_inc(h0_Tsb, 1)
            act.wait_ge(es_ps, g + 1)
            scores = psum[0:NQ, 1, 64:64 + GJ * 2 * H].rearrange("q (k h) -> q k h", k=GJ)
            copy(t1[:, grp(g), F:F + H], scores[:, :, 0:H]).then_inc(es_sb, 1)
            copy(ed_sb[:, grp(g), :], scores[:, :, H:2 * H]).then_inc(es_sb, 1)

        @block.scalar
        def _(act):
            copy = nc.scalar.copy

            def settle():
                act.sem_inc(passed[2], 1)

            def ln_sqrt(g):
                return nc.scalar.activation(st_std[:, g % 2, :], st_var[:, g % 2, :], ACT.Sqrt, scale=1.0 / F, bias=eps_f[:, 0:1])

            act.wait_ge(v_T, 1)
            copy(wattT[:, :, :], psum[0:F, 0, 0:H * F].rearrange("p (h i) -> p h i", h=H)).then_inc(v_Tsb, 1)
            act.wait_ge(v_ps, 1)
            copy(vvec[:, :], psum[0:F, 1, 0:2 * H]).then_inc(v_sb, 1)
            act.wait_ge(consts_set, N_CONSTS)
            for g in range(NG):
                act.wait_ge(ln_var, g + 1)
                ln_sqrt(g).then_inc(ln_std, 1)
                if g:
                    es_group(act, copy, g - 1)
            es_group(act, copy, NG - 1)
            copy(t2[:, :, F:2 * F], t1[:, :, 0:F]).then_inc(t2h_ready, 1)

            act.wait_ge(src_T_ps, 1)
            copy(src_T[:, 0, :], psum[:, 6, 0:P])
            copy(src_T[0:PE_COLS - P, 1, :], psum[0:PE_COLS - P, 6, P:2 * P]).then_inc(src_T_sb, 1)

            act.wait_ge(weights_in, N_WEIGHTS * 16)
            act.wait_ge(consts_set, N_CONSTS)
            nc.scalar.activation(cat_s[0:F, 0:1], ident[0:F, 0:1], ACT.Copy, scale=0.0, bias=1.0 / H).then_inc(packed, 1)
            nc.scalar.activation(cat_s[F:P, 0:1], ident[F:P, 0:1], ACT.Copy, scale=0.0, bias=1.0).then_inc(packed, 1)

            for j in range(NJ):
                act.wait_ge(cross_T, j + 1)
                copy(cross[:, j, :], psum[:, 2 + j % 2, 0:NQ]).then_inc(cross_sb, 1)

            act.wait_ge(w_arg, 1)
            nc.scalar.activation(es_w[:, :, :], es_w[:, :, :], ACT.Exp).then_inc(w_ready, 1)

            def hop_part(c, s, n):
                act.wait_ge(g2_ready[s], n * (16 * K))
                act.wait_ge(gat_steps, (c + 1) * K)
                settle()
                copy(msg2[:, s % 2, :, 0:F], gather2[:, s, :, 0:F]).then_inc(hopcopy, 1)

            with act.Fori(0, LOOPS) as i:
                for s in range(SL):
                    hop_part(i * SL + s, s, i + 1)
            for c in range(FULL, CH):
                hop_part(c, c % SL, c // SL + 1)

            for j in range(NJ + 1):
                if j < NJ:
                    act.wait_ge(aT_ps, j + 1)
                    copy(aT[:, j % 2, 0:2, :], psum[:, 5, 0:2 * P].rearrange("p (c q) -> p c q", c=2)[:, :, 0:NQ])
                    copy(aT[0:F, j % 2, 2, :], psum[0:F, 5, 2 * P:2 * P + NQ]).then_inc(aT_sb, 1)
                if j:
                    act.wait_ge(catT_ps, j)
                    nc.scalar.activation(catT[:, :], psum[:, 6, 0:NQ], ACT.Identity, scale=cat_s[:, 0:1],
                                         bias=cat_s[:, 1:2]).then_inc(catT_sb, 1)
                if j >= GJ and j % GJ == 3:
                    act.wait_ge(ln_var, NG + j // GJ)
                    ln_sqrt(j // GJ - 1).then_inc(ln_std, 1)
            act.wait_ge(ln_var, 2 * NG)
            ln_sqrt(NG - 1).then_inc(ln_std, 1)

            act.wait_ge(packed, 2)
            act.wait_ge(be_steps, N_BE)
            act.wait_ge(pack_in, N_PACK * 16)
            with act.Fori(0, L) as l:
                copy(cur[:, 0:CW], pack[:, bass.ds(l, 1), :].rearrange("p a c -> p (a c)")).then_inc(cur_ready, 1)
                copy(cur_b[:, :], rows_b[:, bass.ds(l, 1), :].rearrange("p a c -> p (a c)")).then_inc(cur_ready, 1)
                copy(cur_be[:, :], be_parts[:, bass.ds(l, 1), :].rearrange("p a f -> p (a f)")).then_inc(cur_ready, 1)
                act.wait_ge(cur_ready, l * 6 + 3)
                nc.scalar.mul(cur[:, C_W2N:C_W2N + F], cur[:, C_W2:C_W2 + F], -LEAK).then_inc(cur_ready, 1)
                nc.scalar.mul(cur[:, C_E2N:C_E2N + P], cur[:, C_E2:C_E2 + P], -LEAK).then_inc(cur_ready, 1)
                nc.scalar.mul(cur[:, C_B1N:C_B1N + 2], cur[:, C_B1:C_B1 + 2], -1.0).then_inc(cur_ready, 1)
                act.wait_ge(cur_ready, l * 6 + 6)
                settle()
                def copy_xT(g):
                    act.wait_ge(xT_ps, l * NG + (g + 1))
                    copy(hT[:, :, :], psum[0:F, 0:2, :].rearrange("p b n -> p (b n)")[:, 0:GJ * P]
                         .rearrange("p (k n) -> p k n", n=P)[:, :, 0:NQ]).then_inc(xT_sb, 1)

                copy_xT(0)
                for g in range(NG):
                    act.wait_ge(y_ps, l * NG + (g + 1))
                    y = psum[:, 2:4, :].rearrange("p b n -> p (b n)")[:, 0:GJ * P]\
                        .rearrange("p (k n) -> p k n", n=P)[:, :, 0:NQ]
                    nc.scalar.activation(yp[:, :, :], y, ACT.Relu, bias=cur[:, C_B1:C_B1 + 1]).then_inc(y_sb, 1)
                    nc.scalar.activation(yn[:, :, :], y, ACT.Relu, bias=cur[:, C_B1N:C_B1N + 1], scale=-1.0)\
                        .then_inc(y_sb, 1)
                    if g + 1 < NG:
                        copy_xT(g + 1)
                    act.wait_ge(h_ps, l * NG + (g + 1))
                    copy(hsb[:, grp(g), :], psum[0:NQ, 7, 0:GJ * F].rearrange("q (k f) -> q k f", f=F)).then_inc(h_sb, 1)

                def attr_copy(c, b):
                    act.wait_ge(at_ps, l * CH + c + 1)
                    copy(attr_T[:, b, :], psum[:, 5 + b, 0:256]).then_inc(at_sb, 1)

                def relu_edges(c, b):
                    act.wait_ge(ye_ps, l * CH + c + 1)
                    nc.scalar.activation(act_p[:, b, :], psum[:, b, :], ACT.Relu, bias=cur[:, C_BE1:C_BE1 + 1])\
                        .then_inc(ye_sb, 1)
                    nc.scalar.activation(act_n[:, b, :], psum[:, b, :], ACT.Relu, bias=cur[:, C_BE1N:C_BE1N + 1],
                                         scale=-1.0).then_inc(ye_sb, 1)

                def found_copy(c, s):
                    m = ON_PE[s % 2]
                    act.wait_ge(found_ps, l * CH + c + 1)
                    copy(gatherg[:, s, K - m:, :], psum[:, 4 + 3 * (s % 2), 0:m * F].rearrange("p (m f) -> p m f", f=F))\
                        .then_inc(found_sb, 1)

                attr_copy(0, 0)
                attr_copy(1, 1)
                relu_edges(0, 0)
                with act.Fori(0, LOOPS) as i:
                    for s in range(SL):
                        attr_copy(i * SL + (s + 2), s % 2)
                        relu_edges(i * SL + (s + 1), (s + 1) % 2)
                        found_copy(i * SL + s, s)
                for c in range(FULL, CH):
                    if c + 2 < CH:
                        attr_copy(c + 2, c % 2)
                    if c + 1 < CH:
                        relu_edges(c + 1, (c + 1) % 2)
                    found_copy(c, c % SL)

                for g in range(NG):
                    act.wait_ge(ln_var, l * NG + (2 * NG + g + 1))
                    ln_sqrt(g).then_inc(ln_std, 1)

        @block.tensor
        def _(pe):
            mm = nc.tensor.matmul

            def settle():
                pe.sem_inc(passed[1], 1)

            pe.wait_ge(consts_set, N_CONSTS)
            pe.wait_ge(att_in, 48)
            for h in range(H):
                ins = nc.tensor.transpose(psum[0:F, 0, h * F:(h + 1) * F], watt[:, h, :], ident[0:F, 0:F])
            ins.then_inc(v_T, 1)
            pe.wait_ge(v_Tsb, 1)
            for a in range(2):
                for h in range(H):
                    ins = mm(psum[0:F, 1, a * H + h:a * H + h + 1], wattT[:, h, :], avec[:, a, h:h + 1],
                             start=True, stop=True)
            ins.then_inc(v_ps, 1)

            def transpose_group(x_tile, bank, signal):
                for k in range(GJ):
                    ins = nc.tensor.transpose(psum[0:F, bank + k // 4, (k % 4) * P:(k % 4) * P + NQ],
                                              x_tile[:, k, :], ident[0:NQ, 0:NQ])
                ins.then_inc(signal, 1)

            for g in range(NG):
                pe.wait_ge(h0_ready, g + 1)
                if g:
                    pe.wait_ge(es_sb, 2 * g)
                transpose_group(t1[:, grp(g), 0:F], 2, h0_T)
                pe.wait_ge(h0_Tsb, g + 1)
                if g == 0:
                    pe.wait_ge(v_sb, 1)
                for k in range(GJ):
                    ins = mm(psum[0:NQ, 1, 64 + k * 2 * H:64 + (k + 1) * 2 * H], hT[:, k, :], vvec[:, :],
                             start=True, stop=True)
                ins.then_inc(es_ps, 1)

            pe.wait_ge(diag_ready, 1)
            for a in range(2):
                ins = mm(psum[:, 0, a * P:(a + 1) * P], ones[:, :], diag[:, a, :], start=True, stop=True)
            ins.then_inc(bc_ready, 1)

            pe.wait_ge(src_cols_set, 1)
            nc.tensor.transpose(psum[:, 6, 0:P], src_cols[:, 0:P], ident[:, :])
            nc.tensor.transpose(psum[0:PE_COLS - P, 6, P:2 * P], src_cols[:, P:], ident[:, :]).then_inc(src_T_ps, 1)

            degree = psum[0:NQ, 7, 0:NJ]
            mm(degree, zero16[:, :], zero16[:, 0:NJ], start=True, stop=False)

            def degrees(c, s):
                pe.wait_ge(hot_ready, c + 1)
                settle()
                for k in range(K):
                    ins = mm(degree, hot_q[:, s % 2, k, :], hot_j[:, s % 2, k, :], start=False, stop=False)
                ins.then_inc(hot_used, 1)

            pe.sem_inc(hot_used, 2)
            with pe.Fori(0, LOOPS) as i:
                for s in range(SL):
                    degrees(i * SL + s, s)
            for c in range(FULL, CH):
                degrees(c, c % SL)
            mm(degree, zero16[:, :], zero16[:, 0:NJ], start=False, stop=True).then_inc(deg_ready, 1)
            pe.wait_ge(rowtot, 1)
            mm(psum[0:NQ, 4, 0:1], above[0:NQ, 0:NQ], incl[:, NJ - 1:NJ], start=True, stop=True).then_inc(rowoff_ps, 1)
            pe.wait_ge(crossq_ready, 1)
            for j in range(NJ):
                if j >= 2:
                    pe.wait_ge(cross_sb, j - 1)
                nc.tensor.transpose(psum[:, 2 + j % 2, 0:NQ], crossq[:, j, :], ident[0:NQ, 0:NQ]).then_inc(cross_T, 1)

            def tails(tail, ready, used, base):
                for g in range(NG):
                    if g >= 2:
                        pe.wait_ge(used, base + (g - 1))
                        settle()
                    for k in range(GJ):
                        ins = mm(psum[0:NQ, 4 + g % 2, k * F:(k + 1) * F], cross[:, g * GJ + k, :], tail,
                                 start=True, stop=True)
                    ins.then_inc(ready, 1)

            pe.wait_ge(cross_sb, NJ)
            pe.wait_ge(hop_steps, CH * K)
            settle()
            tails(run1[:, (CH - 1) % SL, K - 1, :], c1_ready, c1_used, 0)

            for a in range(2):
                pe.wait_ge(diag4_ready, a + 1)
                mm(psum[:, a, :], ones[:, :], diag4[:, :, :].rearrange("p h n -> p (h n)"),
                   start=True, stop=True).then_inc(bc4_ready, 1)

            pe.wait_ge(gat_steps, (CH + 2) * K)
            settle()
            pe.wait_ge(weights_in, N_WEIGHTS * 16)
            tail2 = run2[:, (CH - 1) % 2, K - 1, :]

            def tails2(g):
                for j in range(g * GJ, (g + 1) * GJ):
                    if j >= 5:
                        pe.wait_ge(c2_used, j - 4)
                    mm(psum[0:NQ, j % 5, 0:WG], cross[:, j, :], tail2, start=True, stop=True).then_inc(c2_ready, 1)

            tails2(0)
            for i in range(NJ + 2):
                if i < NJ:
                    if i % GJ == 0:
                        if i // GJ + 1 < NG:
                            tails2(i // GJ + 1)
                        pe.wait_ge(cat2_ready, i // GJ + 1)
                    if i:
                        pe.wait_ge(aT_sb, i)
                    for c in range(3):
                        w = P if c < 2 else F
                        ins = nc.tensor.transpose(psum[0:w, 5, c * P:c * P + NQ],
                                                  cat2[:, i // GJ % 2, i % GJ, c * P:c * P + w], ident[0:NQ, 0:NQ])
                    ins.then_inc(aT_ps, 1)
                if i >= 2:
                    j = i - 2
                    g, k = j // GJ, j % GJ
                    pe.wait_ge(catT_sb, j + 1)
                    if k == 0 and g:
                        pe.wait_ge(x1_used, g)
                    o = psum[0:NQ, 7, k * F:(k + 1) * F]
                    mm(o, ones[0:1, 0:NQ], bw_row[0:1, :], start=True, stop=False)
                    ins = mm(o, catT[:, :], ww_sb[:, :], start=False, stop=True)
                    if k == GJ - 1:
                        ins.then_inc(x1_ps, 1)
                if 1 <= i <= NJ:
                    j = i - 1
                    pe.wait_ge(aT_sb, j + 1)
                    mm(psum[0:F, 6, 0:NQ], wstack[:, 0, :], aT[:, j % 2, 0, :], start=True, stop=False)
                    mm(psum[0:F, 6, 0:NQ], wstack[:, 1, :], aT[:, j % 2, 1, :], start=False, stop=True)
                    mm(psum[F:P, 6, 0:NQ], wg_sb[:, :], aT[0:F, j % 2, 2, :], start=True, stop=True).then_inc(catT_ps, 1)

            with pe.Fori(0, L) as l:
                w1 = cur[0:F, C_W1:C_W1 + F2]
                pe.wait_ge(cur_ready, l * 6 + 6)
                def transpose_x(g):
                    pe.wait_ge(x_ready, l * NG + (g + 1))
                    settle()
                    transpose_group(xg[:, grp(g), :], 0, xT_ps)

                transpose_x(0)
                for g in range(NG):
                    pe.wait_ge(xT_sb, l * NG + (g + 1))
                    settle()
                    for k in range(GJ):
                        ins = mm(psum[:, 2 + k // 4, (k % 4) * P:(k % 4) * P + NQ], w1, hT[:, k, :], start=True, stop=True)
                    ins.then_inc(y_ps, 1)
                    if g + 1 < NG:
                        transpose_x(g + 1)
                    pe.wait_ge(y_sb, l * (2 * NG) + 2 * (g + 1))
                    if g:
                        pe.wait_ge(h_sb, l * NG + g)
                    settle()
                    mm(psum[0:NQ, 7, 0:GJ * F], ones[0:1, 0:NQ],
                       cur_b[0:1, :].unsqueeze(1).to_broadcast([1, GJ, F]), start=True, stop=False, skip_group_check=True)
                    for k in range(GJ):
                        o = psum[0:NQ, 7, k * F:(k + 1) * F]
                        mm(o, yp[:, k, :], cur[:, C_W2:C_W2 + F], start=False, stop=False, skip_group_check=True)
                        ins = mm(o, yn[:, k, :], cur[:, C_W2N:C_W2N + F], start=False, stop=(k == GJ - 1), skip_group_check=True)
                    ins.then_inc(h_ps, 1)

                def transpose_attr(c, s, n):
                    pe.wait_ge(attr_in[s], n * 16)
                    settle()
                    for u in range(2):
                        ins = nc.tensor.transpose(psum[:, 5 + s % 2, u * P:(u + 1) * P],
                                                  attr_nat[:, s, u * P:(u + 1) * P], ident[:, :])
                    ins.then_inc(at_ps, 1)

                def first_half(c, b):
                    pe.wait_ge(at_sb, l * CH + c + 1)
                    settle()
                    for u in range(4):
                        ins = mm(psum[:, b, u * P:(u + 1) * P], cur[:, C_E1 + (u % 2) * P:C_E1 + (u % 2 + 1) * P],
                                 attr_T[:, b, (u // 2) * P:(u // 2 + 1) * P], start=True, stop=True)
                    ins.then_inc(ye_ps, 1)

                def look_up(c, b):
                    pe.wait_ge(hot_done, l * CH + c + 1)
                    pe.wait_ge(edge_steps, (l * CH + c) * (K + 1) + 1)
                    settle()
                    for m in range(ON_PE[b]):
                        for j in range(NJ):
                            for part in range(3):
                                ins = mm(psum[:, 4 + 3 * b, m * F:(m + 1) * F], hot[:, b, j, m, :], parts[:, j, part, :],
                                         start=(j == 0 and part == 0), stop=(j == NJ - 1 and part == 2))
                    ins.then_inc(found_ps, 1)

                def second_half(c, b):
                    pe.wait_ge(ye_sb, (l * CH + c + 1) * 2)
                    settle()
                    mm(psum[:, 2 + b, :], ones16[:, :], cur_be[:, :].unsqueeze(1).to_broadcast([96, K, F]),
                       start=True, stop=False, skip_group_check=True)
                    for u in range(4):
                        o = psum[:, 2 + b, u * P:(u + 1) * P]
                        mm(o, act_p[:, b, u * P:(u + 1) * P], cur[:, C_E2:C_E2 + P], start=False, stop=False, skip_group_check=True)
                        ins = mm(o, act_n[:, b, u * P:(u + 1) * P], cur[:, C_E2N:C_E2N + P], start=False,
                                 stop=(u == 3), skip_group_check=True)
                    ins.then_inc(e_ready, 1)

                def arrivals(s):
                    return len(range(s, CH, SL))

                pe.wait_ge(parts_ready, l * NG + NG)
                transpose_attr(0, 0, l * arrivals(0) + 1)
                transpose_attr(1, 1, l * arrivals(1) + 1)
                first_half(0, 0)
                with pe.Fori(0, LOOPS) as i:
                    for s in range(SL):
                        c = i * SL + s
                        s2 = (s + 2) % SL
                        transpose_attr(c + 2, s2, l * arrivals(s2) + i + (1 + (s + 2) // SL))
                        first_half(c + 1, (s + 1) % 2)
                        look_up(c, s % 2)
                        second_half(c, s % 2)
                for c in range(FULL, CH):
                    if c + 2 < CH:
                        s2 = (c + 2) % SL
                        transpose_attr(c + 2, s2, l * arrivals(s2) + ((c + 2) // SL + 1))
                    if c + 1 < CH:
                        first_half(c + 1, (c + 1) % 2)
                    look_up(c, c % 2)
                    second_half(c, c % 2)

                pe.wait_ge(edge_steps, 2 * (K + 1) + (l + 1) * (CH * (K + 1)))
                settle()
                tails(run1[:, (CH - 1) % SL, K - 1, :], cg_ready, cg_used, l * NG)

        @block.vector
        def _(dve):
            tt = nc.vector.tensor_tensor
            ts = nc.vector.tensor_scalar
            stt = nc.vector.scalar_tensor_tensor
            st = Steps(dve, dve_steps)

            def per_node(v, g, width=F):
                return v[:, grp(g)].unsqueeze(2).to_broadcast([NQ, GJ, width])

            def centred(xs, g):
                return stt(cen[:, g % 2, :, :], xs, float(F), st_sum[:, g % 2, :].unsqueeze(2).to_broadcast([NQ, GJ, F]),
                           ALU.mult, ALU.subtract)

            def square_sum(st, n, g):
                st.wait(n)
                st.then(tt(sq[:, :, :], cen[:, g % 2, :, :], cen[:, g % 2, :, :], ALU.mult))
                nc.vector.tensor_reduce(st_var[:, g % 2, :], sq[:, :, :], AX.X, ALU.add).then_inc(ln_var, 1)

            def norm_relu(st, xs, g, to, n_std, signal):
                front, back = g < NG, g > 0
                b = (g - 1) % 2
                if front:
                    n = st.done(nc.vector.tensor_reduce(st_sum[:, g % 2, :], xs[:, grp(g), :], AX.X, ALU.add))
                if back:
                    dve.wait_ge(ln_std, n_std)
                    m = st.done(nc.vector.reciprocal(st_std[:, b, :], st_std[:, b, :]))
                if front:
                    st.wait(n)
                    n = st.done(centred(xs[:, grp(g), :], g))
                if back:
                    st.wait(m)
                    stt(to[:, grp(g - 1), 0:F], cen[:, b, :, :], 0.0, st_std[:, b, :].unsqueeze(2).to_broadcast([NQ, GJ, F]),
                        ALU.max, ALU.mult).then_inc(signal, 1)
                if front:
                    square_sum(st, n, g)

            dve.wait_ge(x_in, 16)
            for g in range(NG + 1):
                norm_relu(st, xin, g, t1, g, h0_ready)

            dve.wait_ge(edges_in, 64)
            for s in range(SL):
                nc.vector.tensor_copy(idx[:, s, :], src_i[:, s * K:(s + 1) * K]).then_inc(idx1, 1)
            whole = CH // 2
            cols = src_cols[:, 0:whole * PAIR].rearrange("p (c m) -> p c m", m=PAIR)
            pairs = src_i[:, 0:whole * 2 * K].rearrange("p (c k) -> p c k", k=2 * K)
            st.done(nc.vector.tensor_copy(cols[:, :, 0:ON_PE[0]], pairs[:, :, K - ON_PE[0]:K]))
            st.done(nc.vector.tensor_copy(cols[:, :, ON_PE[0]:], pairs[:, :, 2 * K - ON_PE[1]:]))
            if CH % 2:
                st.done(nc.vector.tensor_copy(src_cols[:, whole * PAIR:], src_i[:, T - ON_PE[0]:T]))
            dve.wait_ge(dve_steps, st.n)
            ts(src_cols[:, :], src_cols[:, :], float(MID), None, ALU.subtract).then_inc(src_cols_set, 1)
            st.then(nc.vector.tensor_copy(dst_f[:, :], dst_i[:, :]))
            st.done(nc.vector.memset(mask[:, 0:1], 0.0))
            st.done(nc.vector.memset(pen[:, T:T + 1], -BIG))
            st.then(tt(mask[:, 1:T], dst_f[:, 1:T], dst_f[:, 0:T - 1], ALU.is_equal))
            st.done(ts(pen[:, 0:T], mask[:, :], 1.0, BIG, ALU.subtract, ALU.mult))
            st.done(ts(pen_first[:, :], dst_f[:, :], dst_f[:, 0:1], 1.0, ALU.is_equal, ALU.subtract))
            st.then(ts(pen_last[:, :], dst_f[:, :], dst_f[:, T - 1:T], 1.0, ALU.is_equal, ALU.subtract))
            st.done(ts(pen_first[:, :], pen_first[:, :], BIG, None, ALU.mult))
            st.done(ts(pen_last[:, :], pen_last[:, :], BIG, None, ALU.mult))
            st.then(ts(d25[:, :], dst_f[:, :], 1.0 / NJ, 0.48, ALU.mult, ALU.subtract))
            st.then(ts(d25[:, :], d25[:, :], ROUND, ROUND, ALU.add, ALU.subtract))
            st.then(ts(d25[:, :], d25[:, :], float(NJ), None, ALU.mult))
            st.then(tt(drem[:, :], dst_f[:, :], d25[:, :], ALU.subtract))
            dve.wait_ge(consts_set, N_CONSTS)
            ts(diag[:, 0, :], ident[:, :], dst_f[:, T - 1:T], None, ALU.mult)
            ts(diag[:, 1, :], ident[:, :], dst_f[:, 0:1], None, ALU.mult).then_inc(diag_ready, 1)
            dve.wait_ge(bc_ready, 1)
            st.done(ts(pen_m[:, 0, :], psum[:, 0, 0:P], dst_f[:, 0:1], None, ALU.is_equal))
            st.then(ts(pen_m[:, 1, :], psum[:, 0, P:2 * P], dst_f[:, T - 1:T], None, ALU.is_equal))
            st.done(tt(pen_m[:, 0, :], pen_m[:, 0, :], below[:, :], ALU.mult))
            st.then(tt(pen_m[:, 1, :], pen_m[:, 1, :], above[:, :], ALU.mult))
            st.then(ts(pen_m[:, :, :], pen_m[:, :, :], 1.0, BIG, ALU.subtract, ALU.mult))

            dve.wait_ge(weights_in, N_WEIGHTS * 16)
            be = Steps(dve, be_steps)
            be.then(nc.vector.tensor_copy(be_tmp[:, :, :], be_rows[:, :, :]))
            be.done(nc.vector.tensor_copy(be_parts[0:32, :, :], be_tmp[0:32, :, :]))
            be.then(tt(be_rows[:, :, :], be_rows[:, :, :], be_tmp[:, :, :], ALU.subtract))
            be.then(nc.vector.tensor_copy(be_tmp[:, :, :], be_rows[:, :, :]))
            be.done(nc.vector.tensor_copy(be_parts[32:64, :, :], be_tmp[32:64, :, :]))
            be.then(tt(be_parts[64:96, :, :], be_rows[64:96, :, :], be_tmp[64:96, :, :], ALU.subtract))
            assert be.n == N_BE

            def hop_chunk(c, s, n, more):
                prev = run1[:, (s - 1) % SL, K - 1, :]
                dve.wait_ge(g1_ready[s], n * (16 * K))
                dve.wait_ge(run1_free, c + 1)
                for k in range(K):
                    stt(run1[:, s, k, :], prev, mask[:, bass.ds(c * K + k, 1)], gather1[:, s, k, 0:F],
                        ALU.mult, ALU.add).then_inc(hop_steps, 1)
                    prev = run1[:, s, k, :]
                    if k == 0:
                        dve.wait_ge(hot_used, c + 1)
                        tt(hot_q[:, s % 2, :, :], d25[:, bass.ds(c * K, K)].unsqueeze(2).to_broadcast([P, K, NQ]),
                           q25[:, :].unsqueeze(1).to_broadcast([P, K, NQ]), ALU.is_equal)
                    if k == 1:
                        tt(hot_j[:, s % 2, :, :], drem[:, bass.ds(c * K, K)].unsqueeze(2).to_broadcast([P, K, NJ]),
                           jcol[:, :].unsqueeze(1).to_broadcast([P, K, NJ]), ALU.is_equal).then_inc(hot_ready, 1)
                    if k == 2:
                        nc.vector.tensor_copy(es_w[:, bass.ds(c * K, K), :], gather1[:, s, :, F:F + H]).then_inc(es_done, 1)
                    if k < K - 1:
                        dve.wait_ge(hop_steps, c * K + (k + 1))
                if more:
                    nc.vector.tensor_copy(idx[:, s, :], src_i[:, bass.ds((c + SL) * K, K)]).then_inc(idx1, 1)
                dve.wait_ge(hop_steps, c * K + K)

            with dve.Fori(0, LOOPS) as i:
                for s in range(SL):
                    hop_chunk(i * SL + s, s, i + 1, True)
            for c in range(FULL, CH):
                hop_chunk(c, c % SL, c // SL + 1, c + SL < CH)

            dve.wait_ge(deg_ready, 1)
            st.then(nc.vector.tensor_copy(deg, psum[0:NQ, 7, 0:NJ]))
            nc.vector.tensor_tensor_scan(incl, zeros[0:NQ, 0:NJ], deg, 0.0, ALU.add, ALU.add).then_inc(rowtot, 1)
            dve.wait_ge(rowoff_ps, 1)
            st.then(nc.vector.tensor_copy(rowoff[:, :], psum[0:NQ, 4, 0:1]))
            st.then(ts(last, incl, rowoff[:, 0:1], 1.0, ALU.add, ALU.subtract))
            st.done(ts(nonempty, deg, 0.5, None, ALU.is_gt))
            st.then(ts(lastc, last, float(EP), None, ALU.subtract))
            st.then(tt(lastc, lastc, nonempty, ALU.mult))
            ts(last_i[:, :], lastc, float(EP), None, ALU.add).then_inc(last_ready, 1)
            st.then(tt(first, last, deg, ALU.subtract))
            st.done(ts(first, first, 1.0, None, ALU.add))
            st.then(ts(cmean, deg, 1.0, None, ALU.max))
            st.then(nc.vector.reciprocal(cmean, cmean))
            st.done(tt(cmean, cmean, nonempty, ALU.mult))
            st.then(tt(tmpn, first, spare[0:NQ, :], ALU.subtract))
            st.then(tt(tmpn, tmpn, nonempty, ALU.mult))
            st.then(tt(tmpn, tmpn, spare[0:NQ, :], ALU.add))
            nc.vector.tensor_copy(slot_i[:, :], tmpn).then_inc(slots_ready, 1)
            dve.wait_ge(ed_zeroed, 80)
            dve.wait_ge(attr_padded, 32)
            bounds = bound[0:NQ, :].unsqueeze(1).to_broadcast([NQ, NJ, P])
            st.done(tt(crossq, bounds, first.unsqueeze(2).to_broadcast([NQ, NJ, P]), ALU.is_gt))
            st.then(tt(crossq2, bounds, last.unsqueeze(2).to_broadcast([NQ, NJ, P]), ALU.is_le))
            tt(crossq, crossq, crossq2, ALU.mult).then_inc(crossq_ready, 1)

            for g in range(NG):
                dve.wait_ge(agg1_in[g], GJ * 16)
                dve.wait_ge(c1_ready, g + 1)
                tt(agg[:, grp(g), :], agg[:, grp(g), :], psum[0:NQ, 4 + g % 2, 0:GJ * F].rearrange("q (k f) -> q k f", f=F),
                   ALU.add).then_inc(c1_used, 1)
                dve.wait_ge(c1_used, g + 1)
                tt(t2[:, grp(g), 0:F], agg[:, grp(g), :], per_node(cmean, g), ALU.mult).then_inc(t2_ready, 1)
            for s in range(SL):
                nc.vector.tensor_copy(idx[:, s, :], src_i[:, s * K:(s + 1) * K]).then_inc(idx2, 1)

            dve.wait_ge(edx_in, 16)
            dve.wait_ge(ed0_in, 16)
            dve.wait_ge(es_done, CH)
            st.then(nc.vector.tensor_copy(sm_a[:, 0, :], ed0[:, :]))
            for h in range(H):
                st.done(nc.vector.tensor_tensor_scan(sm_b[:, :, h], mask[:, :], sm_a[:, :, h], 0.0, ALU.mult, ALU.add))
            dve.wait_ge(dve_steps, st.n)
            st.then(tt(es_w[:, :, :], es_w[:, :, :], sm_b, ALU.add))
            st.then(stt(es_w[:, :, :].rearrange("p t h -> p (t h)"), es_w[:, :, :].rearrange("p t h -> p (t h)"), NEG,
                        es_w[:, :, :].rearrange("p t h -> p (t h)"), ALU.mult, ALU.max))
            for h in range(H):
                st.done(nc.vector.tensor_tensor_scan(sm_a[:, :, h], pen[:, 0:T], es_w[:, :, h], 0.0, ALU.add, ALU.max))
                st.done(nc.vector.tensor_tensor_scan(sm_b[:, ::-1, h], pen[:, T:0:-1], es_w[:, ::-1, h], 0.0,
                                                     ALU.add, ALU.max))
            dve.wait_ge(dve_steps, st.n)
            for a, state in ((0, sm_a[:, T - 1, :]), (1, sm_b[:, 0, :])):
                if a:
                    dve.wait_ge(bc4_ready, a)
                tt(diag4[:, :, :], ident[:, :].unsqueeze(1).to_broadcast([P, H, P]),
                   state.unsqueeze(2).to_broadcast([P, H, P]), ALU.mult).then_inc(diag4_ready, 1)
            st.then(tt(sm_a, sm_a, sm_b, ALU.max))
            for a in range(2):
                dve.wait_ge(bc4_ready, a + 1)
                st.then(tt(reached, psum[:, a, :].rearrange("p (h n) -> p h n", h=H),
                           pen_m[:, a, :].unsqueeze(1).to_broadcast([P, H, P]), ALU.add))
                st.then(nc.vector.tensor_reduce(carry[:, a, :], reached, AX.X, ALU.max))
            for a, reach in ((0, pen_first), (1, pen_last)):
                for h in range(H):
                    st.done(stt(sm_a[:, :, h], reach[:, :], carry[:, a, h:h + 1], sm_a[:, :, h], ALU.add, ALU.max))
                dve.wait_ge(dve_steps, st.n)
            tt(es_w[:, :, :], es_w[:, :, :], sm_a, ALU.subtract).then_inc(w_arg, 1)
            dve.wait_ge(w_ready, 1)

            def weigh(c, s, k):
                return tt(msg2[:, s % 2, k, F:WG].rearrange("p (h w) -> p h w", h=H),
                          gather2[:, s, k, F:W2R].unsqueeze(1).to_broadcast([P, H, WH]),
                          es_w[:, bass.ds(c * K + k, 1), :].rearrange("p a h -> p (a h)").unsqueeze(2)
                          .to_broadcast([P, H, WH]), ALU.mult)

            def gat_chunk(c, s, n2, more, ahead):
                dve.wait_ge(hopcopy, c + 1)
                dve.wait_ge(run2_free, c + 1)
                dve.wait_ge(msg_steps, (c + 1) * K)
                prev = run2[:, (s - 1) % 2, K - 1, :]
                for k in range(K):
                    stt(run2[:, s % 2, k, :], prev, mask[:, bass.ds(c * K + k, 1)], msg2[:, s % 2, k, :],
                        ALU.mult, ALU.add).then_inc(gat_steps, 1)
                    prev = run2[:, s % 2, k, :]
                    if ahead:
                        s1 = (s + 1) % SL
                        if k == 0:
                            dve.wait_ge(g2_ready[s1], n2 * (16 * K))
                        weigh(c + 1, s1, k).then_inc(msg_steps, 1)
                    if more and k == K - 1:
                        nc.vector.tensor_copy(idx[:, s, :], src_i[:, bass.ds((c + SL) * K, K)]).then_inc(idx2, 1)
                    dve.wait_ge(gat_steps, (c + 2) * K + (k + 1))

            dve.sem_inc(gat_steps, 2 * K)
            dve.wait_ge(g2_ready[0], 16 * K)
            for k in range(K):
                weigh(0, 0, k).then_inc(msg_steps, 1)
            with dve.Fori(0, LOOPS) as i:
                for s in range(SL):
                    gat_chunk(i * SL + s, s, i + (1 + (s + 1) // SL), True, True)
            for c in range(FULL, CH):
                gat_chunk(c, c % SL, (c + 1) // SL + 1, c + SL < CH, c + 1 < CH)

            def gat_nodes(g):
                dve.wait_ge(agg2_in[g], GJ * 16)
                for k in range(GJ):
                    j = g * GJ + k
                    dve.wait_ge(c2_ready, j + 1)
                    stt(agg2[:, j, :], agg2[:, j, :], nonempty[:, j:j + 1], psum[0:NQ, j % 5, 0:WG], ALU.mult, ALU.add)\
                        .then_inc(c2_used, 1)
                dve.wait_ge(c2_used, (g + 1) * GJ)
                heads = agg2[:, grp(g), F:WG].rearrange("q j (h w) -> q j h w", h=H)
                st.then(ts(recd[:, :, :], heads[:, :, :, F], 1e-16, None, ALU.max))
                st.then(nc.vector.reciprocal(recd[:, :, :], recd[:, :, :]))
                c2 = cat2[:, g % 2, :, :]
                if g >= 2:
                    dve.wait_ge(aT_sb, (g - 1) * GJ)
                for k in range(GJ):
                    st.done(tt(c2[:, k, 0:H * F].rearrange("q (h f) -> q h f", h=H), heads[:, k, :, 0:F],
                               recd[:, k, :].unsqueeze(2).to_broadcast([NQ, H, F]), ALU.mult))
                tt(c2[:, :, H * F:], agg2[:, grp(g), 0:F], per_node(cmean, g), ALU.mult).then_inc(cat2_ready, 1)

            def residual(g):
                dve.wait_ge(x1_ps, g + 1)
                tt(x1[:, grp(g), :], xin[:, grp(g), :], psum[0:NQ, 7, 0:GJ * F].rearrange("q (k f) -> q k f", f=F),
                   ALU.add).then_inc(x1_used, 1)
                dve.wait_ge(x1_used, g + 1)

            for g in range(NG + 1):
                if g < NG:
                    gat_nodes(g)
                if g:
                    residual(g - 1)
                    norm_relu(st, x1, g - 1, xg, NG + g - 1, x_ready)
            norm_relu(st, x1, NG, xg, 2 * NG, x_ready)

            dve.sem_inc(edge_steps, 2 * (K + 1))
            dve.wait_ge(weights_in, N_WEIGHTS * 16)
            with dve.Fori(0, L) as l:
                for s in range(SL):
                    nc.vector.tensor_copy(idx[:, s, :], src_i[:, s * K:(s + 1) * K]).then_inc(idxg, 1)
                gs = Steps(dve, prep_steps, l * N_GINE_STEPS)
                dve.wait_ge(x_ready, l * NG + NG)
                gs.then(nc.vector.tensor_copy(cur_ln[:, :], lnp[:, bass.ds(l, 1), :].rearrange("q a c -> q (a c)")))
                gs.then(tt(cur_ln[:, 2 * F:2 * F + 1], cur_ln[:, 2 * F:2 * F + 1], cur_ln[:, 2 * F + 1:2 * F + 2], ALU.mult))
                dve.sem_inc(passed[3], 1)

                def one_hot(b, s, j0, j1):
                    m = ON_PE[s % 2]
                    shape = [NQ, j1 - j0, m, P]
                    return tt(hot[:, b, j0:j1, 0:m, :], src_row[:, s, 0:m, :].unsqueeze(1).to_broadcast(shape),
                              node_id[:, j0:j1, :].unsqueeze(2).to_broadcast(shape), ALU.is_equal)

                def passes(s):
                    return len(range(s, CH, SL))

                for c in range(2):
                    dve.wait_ge(src_in[c], l * (passes(c) * 16) + 16)
                    one_hot(c, c, 0, NJ).then_inc(hot_done, 1)
                for g in range(NG):
                    dve.wait_ge(h_sb, l * NG + (g + 1))
                    gs.then(nc.vector.tensor_copy(parts[:, grp(g), 0, :], hsb[:, grp(g), :]))
                    gs.then(tt(sq[:, :, :], hsb[:, grp(g), :], parts[:, grp(g), 0, :], ALU.subtract))
                    gs.then(nc.vector.tensor_copy(parts[:, grp(g), 1, :], sq[:, :, :]))
                    tt(parts[:, grp(g), 2, :], sq[:, :, :], parts[:, grp(g), 1, :], ALU.subtract).then_inc(parts_ready, 1)
                    dve.wait_ge(parts_ready, l * NG + (g + 1))
                dve.sem_inc(passed[3], 1)

                def edge_chunk(c, s, n, more, n2):
                    done = 2 * (K + 1) + (l * CH + c) * (K + 1)
                    prev = run1[:, (s - 1) % SL, K - 1, :]
                    dve.wait_ge(e_ready, l * CH + c + 1)
                    b, m = s % 2, ON_PE[s % 2]
                    e = psum[:, 2 + b, :].rearrange("p (k f) -> p k f", f=F)
                    dve.wait_ge(found_sb, l * CH + c + 1)
                    dve.wait_ge(gg_ready[s], n * (16 * (K - m)))
                    tt(msgg[:, :, :], e, gatherg[:, s, :, :], ALU.mult).then_inc(edge_steps, 1)
                    dve.wait_ge(rung_free, l * CH + c + 1)
                    dve.wait_ge(edge_steps, done + 1)
                    for k in range(K):
                        stt(run1[:, s, k, :], prev, mask[:, bass.ds(c * K + k, 1)], msgg[:, k, :], ALU.mult, ALU.add)\
                            .then_inc(edge_steps, 1)
                        prev = run1[:, s, k, :]
                        if k == 0 and more:
                            nc.vector.tensor_copy(idx[:, s, :], src_i[:, bass.ds((c + SL) * K, K)]).then_inc(idxg, 1)
                        if n2 is not None:
                            if k == 0:
                                dve.wait_ge(src_in[(s + 2) % SL], n2 * 16)
                            piece = one_hot(b, (s + 2) % SL, NJ * k // K, NJ * (k + 1) // K)
                            if k == K - 1:
                                piece.then_inc(hot_done, 1)
                        dve.wait_ge(edge_steps, done + (k + 2))

                with dve.Fori(0, LOOPS) as i:
                    for s in range(SL):
                        edge_chunk(i * SL + s, s, l * passes(s) + i + 1, True,
                                   l * passes((s + 2) % SL) + i + ((s + 2) // SL + 1))
                for c in range(FULL, CH):
                    edge_chunk(c, c % SL, l * passes(c % SL) + (c // SL + 1), c + SL < CH,
                               l * passes((c + 2) % SL) + ((c + 2) // SL + 1) if c + 2 < CH else None)

                for g in range(NG + 1):
                    front, back = g < NG, g > 0
                    b = (g - 1) % 2
                    if front:
                        a = agg[:, grp(g), :]
                        dve.wait_ge(aggg_in[g], l * (GJ * 16) + GJ * 16)
                        dve.wait_ge(cg_ready, l * NG + (g + 1))
                        tt(a, a, psum[0:NQ, 4 + g % 2, 0:GJ * F].rearrange("q (k f) -> q k f", f=F), ALU.add)\
                            .then_inc(cg_used, 1)
                    if back:
                        dve.wait_ge(ln_std, l * NG + (2 * NG + g))
                        m = gs.done(nc.vector.reciprocal(st_std[:, b, :], st_std[:, b, :]))
                    if front:
                        dve.wait_ge(cg_used, l * NG + (g + 1))
                        n = gs.done(stt(a, a, cur_ln[:, 2 * F:2 * F + 1], xg[:, grp(g), :], ALU.mult, ALU.add))
                    if back:
                        gs.wait(m)
                        m = gs.done(tt(cen[:, b, :, :], cen[:, b, :, :],
                                       st_std[:, b, :].unsqueeze(2).to_broadcast([NQ, GJ, F]), ALU.mult))
                    if front:
                        gs.wait(n)
                        n = gs.done(nc.vector.tensor_reduce(st_sum[:, g % 2, :], a, AX.X, ALU.add))
                    if back:
                        gs.wait(m)
                        m = gs.done(tt(cen[:, b, :, :], cen[:, b, :, :],
                                       cur_ln[:, 0:F].unsqueeze(1).to_broadcast([NQ, GJ, F]), ALU.mult))
                    if front:
                        gs.wait(n)
                        n = gs.done(centred(a, g))
                    if back:
                        gs.wait(m)
                        tt(xg[:, grp(g - 1), :], cen[:, b, :, :], cur_ln[:, F:2 * F].unsqueeze(1).to_broadcast([NQ, GJ, F]),
                           ALU.add).then_inc(x_ready, 1)
                    if front:
                        square_sum(gs, n, g)
                assert gs.n == N_GINE_STEPS, gs.n

            dve.wait_ge(x_ready, (L + 1) * NG)
            tt(xin[:, :, :], x1[:, :, :], xg[:, :, :], ALU.add).then_inc(out_ready, 1)

    return nc


N_WEIGHTS = 4 + 1 + 4 + 4
N_PACK = 3 + 4 + 4
N_CONSTS = 21
N_BE = 6
N_GINE_STEPS = 2 + NG * (3 + 4 + 3)


def kernel(x, src, dst, edge_attr_32, **weights):
    import concourse.bacc as bacc
    from concourse.bass_utils import run_bass_kernel_spmd

    nc = bacc.Bacc("TRN2", target_bir_lowering=False, num_devices=1)
    names = ("W_att", "a_src", "a_dst", "W_g", "b_g", "W_w", "b_w")
    ordered = [x, src, dst, edge_attr_32] + [weights["L0_gnn_" + n] for n in names]
    names = ("W1", "b1", "W2", "b2", "We1", "be1", "We2", "be2", "res_w", "dot_scale", "ln_g", "ln_b")
    ordered += [weights["L1_gnn_" + n] for n in names]
    arrays, args = {}, []
    for i, a in enumerate(ordered):
        a = np.ascontiguousarray(a)
        arrays[f"in_{i}_dram"] = a
        args.append(nc.dram_tensor(f"in_{i}_dram", a.shape, mybir.dt.from_np(a.dtype), kind="ExternalInput").ap())
    out = nc.dram_tensor("out_dram", (N, F), F32, kind="ExternalOutput").ap()
    build(nc, *args, out)
    return run_bass_kernel_spmd(nc, [arrays], core_ids=[0]).results[0]["out_dram"]
```

```python
from contextlib import ExitStack

import numpy as np
import concourse.bass as bass
from concourse import mybir
from concourse.alu_op_type import AluOpType as ALU

ACT = mybir.ActivationFunctionType
AX = mybir.AxisListType
F32 = mybir.dt.float32
BF16 = mybir.dt.bfloat16
F16 = mybir.dt.float16
I32 = mybir.dt.int32

P = 128
N, F, E, ED = 3125, 64, 103125, 32
H, L = 4, 5
F2 = 2 * F
K = 8
SL = 4
T = -(-E // (P * K)) * K
EP = P * T
CH = T // K
LOOPS = CH // SL - 1
FULL = LOOPS * SL
LAST = E - (P - 1) * T
ON_PE1, ON_PE2, ON_PE = (2, 1), (1, 1), (2, 1)
ON_ACT = 4
KPE = 2
PE_COLS = CH * KPE
NJ = 25
NQ = N // NJ
GJ = 5
NG = NJ // GJ
W1R = F + H
W2R = 2 * F + 1
WH = F + 1
WG = F + H * WH
BIG = 1.0e38
MID = N // 2
ROUND = 12582912.0
NEG = 0.2
LEAK = 0.1
EPS = 1e-5

C_W1 = 0
C_W2 = C_W1 + F2
C_B1 = C_W2 + F
CN = C_B1 + 1
C_E1 = 0
C_E2 = C_E1 + 2 * P
C_BE1 = C_E2 + P
CE = C_BE1 + 1
CW = CN + CE
C_E2N = CE
C_BE1N = C_E2N + P
CP = C_BE1N + 1


class Steps:

    def __init__(self, eng, sem, base=0):
        self.eng, self.sem, self.base, self.n = eng, sem, base, 0

    def done(self, ins):
        self.n += 1
        ins.then_inc(self.sem, 1)
        return self.n

    def wait(self, n):
        self.eng.wait_ge(self.sem, self.base + n)

    def then(self, ins):
        self.wait(self.done(ins))


def build(nc, x, src, dst, attr, W_att, a_src, a_dst, W_g, b_g, W_w, b_w, W1, b1, W2, b2, We1, be1, We2, be2,
          res_w, dot_scale, ln_g, ln_b, out):
    ctx = ExitStack()
    with ctx:
        def sb(name, shape, dt=F32):
            return ctx.enter_context(nc.sbuf_tensor(name, shape, dt))

        def sem(name):
            return ctx.enter_context(nc.semaphore(name))

        def dram(name, shape, dt=F32):
            return nc.dram_tensor(name, shape, dt, kind="Internal").ap()

        attr_last = dram("attr_last", (T, ED))
        table1 = dram("table1", (N, W1R))
        table2 = dram("table2", (N, W2R))
        tableh = dram("tableh", (N, F))
        rows1 = dram("rows1", (EP + 1, F))
        rows2 = dram("rows2", (EP + 1, WG))
        rowsg = dram("rowsg", (EP + 1, F))
        ed_nodes = dram("ed_nodes", (N, H))
        ed_edges = dram("ed_edges", (EP + N, H))

        pe_src = dram("pe_src", (PE_COLS, P), F16)

        src_i = sb("src_i", [P, T], I32)
        dst_i = sb("dst_i", [P, T], I32)
        dst_f = sb("dst_f", [P, T])
        mask = sb("mask", [P, T])
        penalty = sb("penalty", [P, 3 * T + 1])
        pen = penalty[:, 0:T + 1]
        pen_first = penalty[:, T + 1:2 * T + 1]
        pen_last = penalty[:, 2 * T + 1:]
        parts = penalty[0:NQ, 0:NJ * 3 * F // 2].bitcast(BF16)\
            .rearrange("q (j a f) -> q j a f", j=NJ, a=3)
        es_w = sb("es_w", [P, T, H])
        union = sb("union", [P, NJ * WG])
        agg2 = union[0:NQ, :].rearrange("q (j w) -> q j w", w=WG)
        crossq = union[0:NQ, 0:NJ * P].rearrange("q (j p) -> q j p", p=P)
        crossq2 = union[0:NQ, NJ * P:2 * NJ * P].rearrange("q (j p) -> q j p", p=P)
        sm_a = union[:, 0:T * H].rearrange("p (t h) -> p t h", h=H)
        sm_b = union[:, T * H:2 * T * H].rearrange("p (t h) -> p t h", h=H)
        d25 = union[:, 2 * T * H:2 * T * H + T]
        drem = union[:, 2 * T * H + T:2 * T * H + 2 * T]
        reached = union[:, 2 * T * H:2 * T * H + H * P].rearrange("p (h n) -> p h n", h=H)
        zeros = union[:, 0:T * H // 2]
        hot = union[:, 0:NJ * KPE * P].bitcast(BF16)[0:NQ, :]\
            .rearrange("q (b j m e) -> q b j m e", b=2, j=NJ, e=P)
        node_id = sb("node_id", [NQ, NJ, P], F16)
        src_row = dst_f[0:NQ, 0:SL * KPE * P // 2].bitcast(F16)\
            .rearrange("q (s m e) -> q s m e", s=SL, e=P)
        src_cols = sb("src_cols", [P, PE_COLS])
        src_T = sb("src_T", [P, 2, P], F16)
        diag4 = sb("diag4", [P, H, P])
        flat4 = diag4[0:96, :, :].rearrange("p h n -> p (h n)")
        be_rows = flat4[:, 0:L * F].rearrange("p (l f) -> p l f", l=L)
        be_tmp = flat4[:, L * F:L * F + L * F // 2].bitcast(BF16).rearrange("p (l f) -> p l f", l=L)
        be_parts = sb("be_parts", [96, L, F], BF16)
        cur_be = sb("cur_be", [96, F], BF16)
        ones16 = sb("ones16", [96, P], BF16)
        cross = sb("cross", [P, NJ, NQ])
        idx = sb("idx", [P, SL, K], I32)
        gring = sb("gring", [P, SL * K * W2R])
        pack = es_w[:, :, :].rearrange("p t h -> p (t h)")[:, 0:L * CW].rearrange("p (l c) -> p l c", l=L)
        gather1 = gring[:, 0:SL * K * W1R].rearrange("p (s k w) -> p s k w", s=SL, k=K)
        gather2 = gring[:, :].rearrange("p (s k w) -> p s k w", s=SL, k=K)
        gatherg = gring[:, 0:SL * K * F].rearrange("p (s k w) -> p s k w", s=SL, k=K)
        stage = sb("stage", [P, 4 * K * WG])
        msg2 = stage[:, 0:2 * K * WG].rearrange("p (b k w) -> p b k w", b=2, k=K)
        run2 = stage[:, 2 * K * WG:].rearrange("p (b k w) -> p b k w", b=2, k=K)
        t1 = stage[0:NQ, 0:NJ * W1R].rearrange("q (j w) -> q j w", w=W1R)
        t2 = stage[0:NQ, NJ * W1R:NJ * (W1R + W2R)].rearrange("q (j w) -> q j w", w=W2R)
        t_floats = NJ * (W1R + W2R)
        rest1 = stage[0:NQ, t_floats:t_floats + NJ * W1R].rearrange("q (j w) -> q j w", j=NJ)
        after = 2 * K * WG
        rest2 = stage[0:NQ, after + T * H:after + T * H + NJ * F].rearrange("q (j f) -> q j f", j=NJ)
        highest = stage[:, after:after + T * H].rearrange("p (t h) -> p t h", h=H)
        from_right = gring[:, 0:T * H].rearrange("p (t h) -> p t h", h=H)
        used = [0]

        def part(width):
            used[0] += width
            return stage[:, used[0] - width:used[0]]

        attr_nat = part(SL * K * ED).rearrange("p (s d) -> p s d", s=SL)
        attr_T = part(2 * K * ED).rearrange("p (b d) -> p b d", b=2)
        act_p = part(8 * P).rearrange("p (b n) -> p b n", b=2)
        act_n = part(8 * P).rearrange("p (b n) -> p b n", b=2)
        cat2 = gring[0:NQ, 0:2 * GJ * (H + 1) * F].rearrange("q (b k w) -> q b k w", b=2, k=GJ)
        aT = gring[:, 2 * GJ * (H + 1) * F:2 * GJ * (H + 1) * F + 6 * NQ].rearrange("p (b c q) -> p b c q", b=2, c=3)
        msgg = part(K * F).rearrange("p (k f) -> p k f", k=K)
        yp = part(GJ * NQ).rearrange("p (k n) -> p k n", k=GJ)
        z = part(GJ * NQ).rearrange("p (k n) -> p k n", k=GJ)
        cur_n = part(CN)
        cur = part(CP)
        hsb = part(NJ * F)[0:NQ, :].rearrange("q (j f) -> q j f", j=NJ)
        run1 = sb("run1", [P, SL, K, F])
        hot_q = sb("hot_q", [P, 2, K, NQ], BF16)
        hot_j = sb("hot_j", [P, 2, K, NJ], BF16)
        q25 = sb("q25", [P, NQ])
        jcol = sb("jcol", [P, NJ])
        bound = sb("bound", [P, P])
        spare = sb("spare", [P, NJ])
        ident = sb("ident", [P, P])
        below = sb("below", [P, P])
        above = sb("above", [P, P])
        zero16 = sb("zero16", [P, NQ], BF16)
        ones = sb("ones", [P, P])
        xin = sb("xin", [NQ, NJ, F])
        x_nodes = sb("x_nodes", [NQ, 2 * NJ * F])
        x1 = x_nodes[:, 0:NJ * F].rearrange("q (j f) -> q j f", f=F)
        xg = x_nodes[:, NJ * F:].rearrange("q (j f) -> q j f", f=F)
        parts1 = x_nodes[:, 0:NJ * 3 * W1R // 2].bitcast(BF16)\
            .rearrange("q (j a w) -> q j a w", j=NJ, a=3)
        agg = sb("agg", [NQ, NJ, F])
        ed_sb = sb("ed_sb", [NQ, NJ, H])
        ed0 = sb("ed0", [P, H])
        cen = sb("cen", [NQ, 2, GJ, F])
        sq = sb("sq", [NQ, GJ, F])
        st_sum = sb("st_sum", [NQ, 2, GJ])
        st_var = sb("st_var", [NQ, 2, GJ])
        st_std = sb("st_std", [NQ, 2, GJ])
        eps_f = sb("eps_f", [NQ, 1])
        node = sb("node", [NQ, 8, NJ])
        deg, incl, last, first = (node[:, i, :] for i in range(4))
        nonempty, cmean, tmpn, lastc = (node[:, i, :] for i in range(4, 8))
        rowoff = sb("rowoff", [NQ, 1])
        last_i = sb("last_i", [NQ, NJ], I32)
        slot_i = sb("slot_i", [NQ, NJ], I32)
        diag = sb("diag", [P, 2, P])
        pen_m = sb("pen_m", [P, 2, P])
        carry = sb("carry", [P, 2, H])
        watt = sb("watt", [F, H, F])
        wattT = sb("wattT", [F, H, F])
        wstack = sb("wstack", [P, 2, F])
        avec = sb("avec", [F, 2, H])
        vvec = sb("vvec", [F, 2 * H])
        wg_sb = sb("wg_sb", [F, F])
        ww_sb = sb("ww_sb", [P, F])
        cat_s = sb("cat_s", [P, 2])
        bw_row = sb("bw_row", [1, F])
        hT = sb("hT", [F, GJ, NQ])
        catT = sb("catT", [P, NQ])
        recd = sb("recd", [NQ, GJ, H])
        b2_rows = sb("b2_rows", [NQ, L, F])
        lnp = sb("lnp", [NQ, L, 2 * F + 2])
        cur_ln = sb("cur_ln", [NQ, 2 * F + 2])

        psum = ctx.enter_context(nc.psum_tensor("psum", [P, 8, 512], F32))

        passed = [sem(f"passed_{e}") for e in ("pool", "pe", "act", "dve")]
        pads_set, consts_set, pack_zero = sem("pads_set"), sem("consts_set"), sem("pack_zero")
        x_in, edges_in, att_in, weights_in = sem("x_in"), sem("edges_in"), sem("att_in"), sem("weights_in")
        attr_padded, ed_zeroed = sem("attr_padded"), sem("ed_zeroed")
        ln_var, ln_std = sem("ln_var"), sem("ln_std")
        dve_steps, prep_steps = sem("dve_steps"), sem("prep_steps")
        v_T, v_Tsb, v_ps, v_sb = sem("v_T"), sem("v_Tsb"), sem("v_ps"), sem("v_sb")
        h0_ready, h0_T, h0_Tsb, es_ps, es_sb, t1_out = (sem(n) for n in (
            "h0_ready", "h0_T", "h0_Tsb", "es_ps", "es_sb", "t1_out"))
        ed_out = sem("ed_out")
        idx1, g1_ready = sem("idx1"), [sem(f"g1_ready{s}") for s in range(SL)]
        hop_steps, hot_ready, hot_used, es_done = sem("hop_steps"), sem("hot_ready"), sem("hot_used"), sem("es_done")
        run1_free, rows1_out, rows1_all = sem("run1_free"), sem("rows1_out"), sem("rows1_all")
        deg_ready, rowtot, rowoff_ps, last_ready = sem("deg_ready"), sem("rowtot"), sem("rowoff_ps"), sem("last_ready")
        crossq_ready, cross_T, cross_sb = sem("crossq_ready"), sem("cross_T"), sem("cross_sb")
        slots_ready, ed_scattered, ed0_in, edx_in = sem("slots_ready"), sem("ed_scattered"), sem("ed0_in"), sem("edx_in")
        agg_in = [sem(f"agg_in{g}") for g in range(NG)]
        c1_ready, c1_used, t2_ready, t2h_ready, t2_out = (sem(n) for n in (
            "c1_ready", "c1_used", "t2_ready", "t2h_ready", "t2_out"))
        diag_ready, bc_ready, diag4_ready, bc4_ready = sem("diag_ready"), sem("bc_ready"), sem("diag4_ready"), sem("bc4_ready")
        w_arg, w_ready = sem("w_arg"), sem("w_ready")
        idx2, g2_ready = sem("idx2"), [sem(f"g2_ready{s}") for s in range(SL)]
        hopcopy, msg_steps, gat_steps = sem("hopcopy"), sem("msg_steps"), sem("gat_steps")
        run2_free, rows2_out, rows2_all = sem("run2_free"), sem("rows2_out"), sem("rows2_all")
        c2_ready, c2_used, cat2_ready, aT_ps, aT_sb = (sem(n) for n in (
            "c2_ready", "c2_used", "cat2_ready", "aT_ps", "aT_sb"))
        catT_ps, catT_sb, x1_ps, x1_used = sem("catT_ps"), sem("catT_sb"), sem("x1_ps"), sem("x1_used")
        x_ready, packed, pack_in = sem("x_ready"), sem("packed"), sem("pack_in")
        cur_n_ready, cur_ready, z_sb = sem("cur_n_ready"), sem("cur_ready"), sem("z_sb")
        xT_ps, xT_sb, y_ps, y_sb, h_ps, h_sb, table_out = (sem(n) for n in (
            "xT_ps", "xT_sb", "y_ps", "y_sb", "h_ps", "h_sb", "table_out"))
        idxg, gg_ready = sem("idxg"), [sem(f"gg_ready{s}") for s in range(SL)]
        attr_in = [sem(f"attr_in{s}") for s in range(SL)]
        at_ps, at_sb, ye_ps, ye_sb, e_ready, edge_steps = (sem(n) for n in (
            "at_ps", "at_sb", "ye_ps", "ye_sb", "e_ready", "edge_steps"))
        rung_free, rowsg_out, rowsg_all = sem("rung_free"), sem("rowsg_out"), sem("rowsg_all")
        cg_ready, cg_used = sem("cg_ready"), sem("cg_used")
        src_cols_set, src_T_ps, src_T_sb, pe_src_out = (sem(n) for n in (
            "src_cols_set", "src_T_ps", "src_T_sb", "pe_src_out"))
        src_in = [sem(f"src_in{s}") for s in range(SL)]
        found_ps, found_sb = sem("found_ps"), sem("found_sb")
        eps_set, node_id_set = sem("eps_set"), sem("node_id_set")
        found2_ps, found2_sb, hot2_done, parts2_ready = (sem(n) for n in (
            "found2_ps", "found2_sb", "hot2_done", "parts2_ready"))
        found1_ps, found1_sb, hot1_done, parts1_ready, dst_used = (sem(n) for n in (
            "found1_ps", "found1_sb", "hot1_done", "parts1_ready", "dst_used"))
        hot_done, parts_ready, be_steps = sem("hot_done"), sem("parts_ready"), sem("be_steps")
        out_ready, out_done = sem("out_ready"), sem("out_done")

        def chunk_rows(rows, c, width):
            return rows[0:EP, :].rearrange("(p t) w -> p t w", p=P)[:, bass.ds(c * K, K), 0:width]

        def node_rows(table):
            return table.rearrange("(q j) w -> q j w", j=NJ)

        def grp(g):
            return slice(g * GJ, (g + 1) * GJ)

        block = ctx.enter_context(nc.Block())

        @block.sync
        def _(sp):
            sp.dma_start(xin[:, :, :], x.rearrange("(q j) f -> q j f", j=NJ)).then_inc(x_in, 16)
            sp.dma_start(watt[:, :, :], W_att.rearrange("h i o -> i h o")).then_inc(att_in, 16)
            with nc.allow_non_contiguous_dma(reason="two vectors of 256 elements"):
                sp.dma_start(avec[:, 0, :], a_src.rearrange("h o -> o h")).then_inc(att_in, 16)
                sp.dma_start(avec[:, 1, :], a_dst.rearrange("h o -> o h")).then_inc(att_in, 16)
            sp.wait_ge(pads_set, 2)
            for to, of in ((src_i, src), (dst_i, dst)):
                sp.dma_start(to[0:P - 1, :], of[0:(P - 1) * T].rearrange("(p t) -> p t", p=P - 1))\
                    .then_inc(edges_in, 16)
                sp.dma_start(to[P - 1:P, 0:LAST], of[(P - 1) * T:E].rearrange("(p t) -> p t", p=1))\
                    .then_inc(edges_in, 16)
            for g in range(NG):
                if g == NG - 1:
                    sp.wait_ge(src_T_sb, 1)
                    sp.dma_start(pe_src[0:P, :], src_T[:, 0, :]).then_inc(pe_src_out, 16)
                    sp.dma_start(pe_src[P:, :], src_T[0:PE_COLS - P, 1, :]).then_inc(pe_src_out, 16)
                sp.wait_ge(es_sb, 2 * g + 2)
                sp.dma_start(node_rows(table1)[:, grp(g), :], t1[:, grp(g), :]).then_inc(t1_out, 16)
            sp.dma_start(node_rows(ed_nodes), ed_sb[:, :, :]).then_inc(ed_out, 16)
            sp.wait_ge(consts_set, 2)
            half = ed_edges[0:EP, :].rearrange("(p a t) h -> p a (t h)", p=P, a=2)
            for a in range(2):
                sp.dma_start(half[:, a, :], zeros[:, :]).then_inc(ed_zeroed, 16)
            for rows, width in ((rows1, F), (rows2, WG), (rowsg, F)):
                sp.dma_start(rows[EP:EP + 1, :], zeros[0:1, 0:width]).then_inc(ed_zeroed, 16)
            pad = T - LAST
            rows = 13
            assert pad % rows == 0
            sp.dma_start(attr_last[LAST:T, :].rearrange("(a b) d -> a (b d)", a=rows), zeros[0:rows, 0:pad // rows * ED])\
                .then_inc(ed_zeroed, 16)
            sp.dma_start(attr_last[0:LAST, :], attr[(P - 1) * T:E, :]).then_inc(attr_padded, 16)
            sp.dma_start(wstack[:, :, :], W_att.rearrange("(c b) i o -> (b i) c o", b=2)).then_inc(weights_in, 16)
            sp.dma_start(wg_sb[:, :], W_g).then_inc(weights_in, 16)
            sp.dma_start(ww_sb[:, :], W_w).then_inc(weights_in, 16)
            sp.dma_start(bw_row[:, :], b_w.rearrange("(a f) -> a f", a=1)).then_inc(weights_in, 16)
            sp.wait_ge(consts_set, N_CONSTS)
            with nc.allow_non_contiguous_dma(reason="bias vector"):
                sp.dma_start(cat_s[F:P, 1:2], b_g.rearrange("(f a) -> f a", a=1)).then_inc(weights_in, 16)
            for k in range(3):
                sp.dma_start(be_rows[32 * k:32 * k + 1, :, :], be2.rearrange("(a l) f -> a l f", a=1)).then_inc(weights_in, 16)
            sp.dma_start(b2_rows[:, :, :], b2.partition_broadcast(NQ)).then_inc(weights_in, 16)
            sp.dma_start(lnp[:, :, 0:F], ln_g.partition_broadcast(NQ)).then_inc(weights_in, 16)
            sp.dma_start(lnp[:, :, F:2 * F], ln_b.partition_broadcast(NQ)).then_inc(weights_in, 16)
            with nc.allow_non_contiguous_dma(reason="one number per layer"):
                sp.dma_start(lnp[:, :, 2 * F], dot_scale.partition_broadcast(NQ)).then_inc(weights_in, 16)
                sp.dma_start(lnp[:, :, 2 * F + 1], res_w.partition_broadcast(NQ)).then_inc(weights_in, 16)

            def load_src(c, s, m):
                of = pe_src[bass.ds(c * KPE + (KPE - m), m), :].rearrange("m e -> (m e)")
                sp.dma_start(src_row[:, s, 0:m, :].rearrange("q m e -> q (m e)"), of.partition_broadcast(NQ))\
                    .then_inc(src_in[s], 16)

            def store1(c, s, more):
                if more:
                    sp.wait_ge(hot1_done, c + 1)
                    load_src(c + SL, s, ON_PE1[s % 2])
                sp.wait_ge(hop_steps, (c + 1) * K)
                sp.dma_start(chunk_rows(rows1, c, F), run1[:, s, :, :]).then_inc(rows1_out, 16)
                sp.wait_ge(rows1_out, (c + 1) * 16)
                sp.sem_inc(run1_free, 1)

            sp.sem_inc(run1_free, SL)
            sp.wait_ge(pe_src_out, 32)
            sp.wait_ge(dst_used, 1)
            for c in range(SL):
                load_src(c, c, ON_PE1[c % 2])
            with sp.Fori(0, LOOPS) as i:
                for s in range(SL):
                    store1(i * SL + s, s, True)
            for c in range(FULL, CH):
                store1(c, c % SL, c + SL < CH)
            sp.sem_inc(rows1_all, 1)

            for c in range(SL):
                load_src(c, c, ON_PE2[c % 2])
            for g in range(NG):
                sp.wait_ge(t2_ready, g + 1)
                if g == 0:
                    sp.wait_ge(t2h_ready, 1)
                sp.dma_start(node_rows(table2)[:, grp(g), :], t2[:, grp(g), :]).then_inc(t2_out, 16)
            sp.wait_ge(ed_scattered, NJ * 16)
            sp.wait_ge(cross_sb, NJ)
            sp.dma_start(sm_a, ed_edges[0:EP, :].rearrange("(p t) h -> p t h", p=P)).then_inc(edx_in, 16)

            def store2(c, s, more):
                if more:
                    sp.wait_ge(hot2_done, c + 1)
                    load_src(c + SL, s, ON_PE2[s % 2])
                sp.wait_ge(gat_steps, (c + 3) * K)
                sp.dma_start(chunk_rows(rows2, c, WG), run2[:, s % 2, :, :]).then_inc(rows2_out, 16)
                sp.wait_ge(rows2_out, (c + 1) * 16)
                sp.sem_inc(run2_free, 1)

            sp.sem_inc(run2_free, 2)
            with sp.Fori(0, LOOPS) as i:
                for s in range(SL):
                    store2(i * SL + s, s, True)
            for c in range(FULL, CH):
                store2(c, c % SL, c + SL < CH)
            sp.sem_inc(rows2_all, 1)

            sp.wait_ge(pack_zero, 1)
            loads = [(pack[0:F, :, C_W1:C_W1 + F2], W1.rearrange("l d m -> d l m")),
                     (pack[:, :, C_W2:C_W2 + F], W2.rearrange("l m d -> m l d")),
                     (pack[:, :, C_B1], b1.rearrange("l m -> m l"))]
            for q in range(4):
                col = C_E1 + (q // 2) * P + (q % 2) * F
                loads.append((pack[q * ED:(q + 1) * ED, :, CN + col:CN + col + F], We1.rearrange("l a d -> a l d")))
            for q in range(2):
                col = C_E2 + q * F
                loads.append((pack[q * F:(q + 1) * F, :, CN + col:CN + col + F], We2.rearrange("l d e -> d l e")))
                loads.append((pack[q * F:(q + 1) * F, :, CN + C_BE1], be1.rearrange("l d -> d l")))
            assert len(loads) == N_PACK
            with nc.allow_non_contiguous_dma(reason="bias vectors"):
                for to, of in loads:
                    sp.dma_start(to, of).then_inc(pack_in, 16)

            def load_attr(c, s):
                to = attr_nat[:, s, :].rearrange("p (k d) -> p k d", d=ED)
                most = attr[0:(P - 1) * T, :].rearrange("(p t) d -> p t d", p=P - 1)[:, bass.ds(c * K, K), :]
                sp.dma_start(to[0:P - 1, :, :], most).then_inc(attr_in[s], 16)
                last_rows = attr_last[bass.ds(c * K, K), :].rearrange("(p k) d -> p k d", p=1)
                sp.dma_start(to[P - 1:P, :, :], last_rows).then_inc(attr_in[s], 16)

            def store_g(l, c, s):
                sp.wait_ge(edge_steps, 2 * (K + 1) + (l * CH + c + 1) * (K + 1))
                sp.dma_start(chunk_rows(rowsg, c, F), run1[:, s, :, :]).then_inc(rowsg_out, 16)
                sp.wait_ge(rowsg_out, (l * CH + c + 1) * 16)
                sp.sem_inc(rung_free, 1)

            def store_table(l):
                for g in range(NG):
                    sp.wait_ge(h_sb, l * NG + (g + 1))
                    sp.dma_start(node_rows(tableh)[:, grp(g), :], hsb[:, grp(g), :]).then_inc(table_out, 16)

            def edge_loads(l, more):
                with sp.Fori(0, LOOPS) as i:
                    for s in range(SL):
                        c = i * SL + s
                        sp.wait_ge(at_ps, l * CH + c + 1)
                        load_attr(c + SL, s)
                        sp.wait_ge(hot_done, l * CH + c + 1)
                        load_src(c + SL, s, ON_PE[s % 2])
                        store_g(l, c, s)
                for c in range(FULL, CH):
                    if c + SL < CH:
                        sp.wait_ge(at_ps, l * CH + (c + 1))
                        load_attr(c + SL, c % SL)
                        sp.wait_ge(hot_done, l * CH + (c + 1))
                        load_src(c + SL, c % SL, ON_PE[c % 2])
                    if c == CH - 1 and more:
                        sp.wait_ge(hot_done, l * CH + CH)
                        sp.wait_ge(at_ps, l * CH + CH)
                        for n in range(SL):
                            load_src(n, n, ON_PE[n % 2])
                            load_attr(n, n)
                    store_g(l, c, c % SL)
                sp.sem_inc(rowsg_all, 1)

            sp.sem_inc(rung_free, SL)
            sp.wait_ge(attr_padded, 16)
            sp.wait_ge(x_ready, NG)
            for c in range(SL):
                load_src(c, c, ON_PE[c % 2])
                load_attr(c, c)
            store_table(0)
            with sp.Fori(0, L - 1) as l:
                edge_loads(l, True)
                store_table(l + 1)
            edge_loads(L - 1, False)

            sp.wait_ge(out_ready, 1)
            sp.dma_start(out.rearrange("(q j) f -> q j f", j=NJ), xin[:, :, :]).then_inc(out_done, 16)
            sp.wait_ge(out_done, 16)

        @block.gpsimd
        def _(pool):
            def settle():
                pool.sem_inc(passed[0], 1)

            pool.memset(eps_f[:, :], F * F * EPS).then_inc(eps_set, 1)
            pool.memset(src_i[:, :], 0).then_inc(pads_set, 1)
            pool.memset(dst_i[:, :], 4095).then_inc(pads_set, 1)
            pool.memset(ident[:, :], 0.0).then_inc(consts_set, 1)
            pool.memset(zeros[:, :], 0.0).then_inc(consts_set, 1)
            pool.memset(below[:, :], 1.0).then_inc(consts_set, 1)
            pool.memset(above[:, :], 1.0).then_inc(consts_set, 1)
            pool.wait_ge(consts_set, 4)
            pool.affine_select(out=ident[:, :], in_=ident[:, :], compare_op=ALU.not_equal, fill=1.0, base=0,
                               pattern=[[-1, P]], channel_multiplier=1).then_inc(consts_set, 1)
            pool.affine_select(out=below[:, :], in_=below[:, :], compare_op=ALU.is_gt, fill=0.0, base=0,
                               pattern=[[-1, P]], channel_multiplier=1).then_inc(consts_set, 1)
            pool.affine_select(out=above[:, :], in_=above[:, :], compare_op=ALU.is_gt, fill=0.0, base=0,
                               pattern=[[1, P]], channel_multiplier=-1).then_inc(consts_set, 1)
            pool.iota(q25[:, :], [[NJ, NQ]], base=0, channel_multiplier=0,
                      allow_small_or_imprecise_dtypes=True).then_inc(consts_set, 1)
            pool.iota(jcol[:, :], [[1, NJ]], base=0, channel_multiplier=0,
                      allow_small_or_imprecise_dtypes=True).then_inc(consts_set, 1)
            pool.iota(bound[:, :], [[T, P]], base=T, channel_multiplier=0,
                      allow_small_or_imprecise_dtypes=True).then_inc(consts_set, 1)
            pool.iota(spare[:, :], [[1, NJ]], base=EP, channel_multiplier=NJ,
                      allow_small_or_imprecise_dtypes=True).then_inc(consts_set, 1)
            pool.memset(zero16[:, :], 0.0).then_inc(consts_set, 1)
            pool.memset(ones[:, :], 1.0).then_inc(consts_set, 1)
            pool.memset(t2[:, :, 2 * F:], 1.0).then_inc(consts_set, 1)
            pool.memset(run1[:, SL - 1, K - 1, :], 0.0).then_inc(consts_set, 1)
            pool.memset(run2[:, 1, K - 1, :], 0.0).then_inc(consts_set, 1)
            pool.memset(cat_s[:, :], 0.0).then_inc(consts_set, 1)
            pool.memset(be_rows[:, :, :], 0.0).then_inc(consts_set, 1)
            pool.memset(ones16[:, :], 1.0).then_inc(consts_set, 1)
            pool.iota(node_id[:, :, :], [[1, NJ], [0, P]], base=-MID, channel_multiplier=NJ,
                      allow_small_or_imprecise_dtypes=True).then_inc(node_id_set, 1)

            def gather_chunk(idx_ready, n, table, ring, ready, s, on_pe):
                pool.wait_ge(idx_ready, n)
                settle()
                for k in range(K - on_pe[s % 2]):
                    pool.indirect_dma_start(ring[:, s, k, :], None, table,
                                            bass.IndirectOffsetOnAxis(ap=idx[:, s, k:k + 1], axis=0))\
                        .then_inc(ready[s], 16)

            def gather_pass(idx_ready, base, table, ring, ready, on_pe=(0, 0)):
                with pool.Fori(0, LOOPS) as i:
                    for s in range(SL):
                        gather_chunk(idx_ready, base + i * SL + (s + 1), table, ring, ready, s, on_pe)
                for c in range(FULL, CH):
                    gather_chunk(idx_ready, base + (c + 1), table, ring, ready, c % SL, on_pe)

            def gather_nodes(rows, to, arrived):
                for j in range(NJ):
                    pool.indirect_dma_start(to[:, j, :], None, rows,
                                            bass.IndirectOffsetOnAxis(ap=last_i[:, j:j + 1], axis=0))\
                        .then_inc(arrived[j // GJ], 16)

            pool.wait_ge(t1_out, NG * 16)
            gather_pass(idx1, 0, table1, gather1, g1_ready, ON_PE1)
            pool.wait_ge(rows1_all, 1)
            pool.wait_ge(last_ready, 1)
            pool.wait_ge(ed_zeroed, 96)
            settle()
            gather_nodes(rows1, agg, agg_in)
            pool.wait_ge(slots_ready, 1)
            pool.wait_ge(ed_out, 16)
            settle()
            for j in range(NJ):
                pool.indirect_dma_start(ed_edges, bass.IndirectOffsetOnAxis(ap=slot_i[:, j:j + 1], axis=0),
                                        ed_sb[:, j, :], None).then_inc(ed_scattered, 16)
            pool.indirect_dma_start(ed0[:, :], None, ed_nodes,
                                    bass.IndirectOffsetOnAxis(ap=dst_i[:, 0:1], axis=0)).then_inc(ed0_in, 16)
            pool.wait_ge(t2_out, NG * 16)
            settle()
            gather_pass(idx2, 0, table2, gather2, g2_ready, ON_PE2)
            pool.wait_ge(rows2_all, 1)
            settle()
            gather_nodes(rows2, agg2, agg_in)
            pool.memset(pack, 0.0).then_inc(pack_zero, 1)
            with pool.Fori(0, L) as l:
                pool.wait_ge(table_out, (l + 1) * (NG * 16))
                settle()
                gather_pass(idxg, l * CH, tableh, gatherg, gg_ready, ON_PE)
                pool.wait_ge(rowsg_all, l + 1)
                settle()
                gather_nodes(rowsg, agg, agg_in)

        def es_group(act, copy, g):
            act.wait_ge(h0_T, g + 1)
            copy(hT[:, :, :], psum[0:F, 2:4, :].rearrange("p b n -> p (b n)")[:, 0:GJ * P]
                 .rearrange("p (k n) -> p k n", n=P)[:, :, 0:NQ]).then_inc(h0_Tsb, 1)
            act.wait_ge(es_ps, g + 1)
            scores = psum[0:NQ, 1, 64:64 + GJ * 2 * H].rearrange("q (k h) -> q k h", k=GJ)
            copy(t1[:, grp(g), F:F + H], scores[:, :, 0:H]).then_inc(es_sb, 1)
            copy(ed_sb[:, grp(g), :], scores[:, :, H:2 * H]).then_inc(es_sb, 1)

        @block.scalar
        def _(act):
            copy = nc.scalar.copy

            def settle():
                act.sem_inc(passed[2], 1)

            def ln_sqrt(g):
                return nc.scalar.activation(st_std[:, g % 2, :], st_var[:, g % 2, :], ACT.Sqrt, scale=1.0 / F, bias=eps_f[:, 0:1])

            act.wait_ge(eps_set, 1)
            for g in range(NG):
                act.wait_ge(ln_var, g + 1)
                ln_sqrt(g).then_inc(ln_std, 1)
            act.wait_ge(v_T, 1)
            copy(wattT[:, :, :], psum[0:F, 0, 0:H * F].rearrange("p (h i) -> p h i", h=H)).then_inc(v_Tsb, 1)
            act.wait_ge(v_ps, 1)
            copy(vvec[:, :], psum[0:F, 1, 0:2 * H]).then_inc(v_sb, 1)
            for g in range(NG):
                if g == NG - 1:
                    act.wait_ge(src_T_ps, 1)
                    copy(src_T[:, 0, :], psum[:, 6, 0:P])
                    copy(src_T[0:PE_COLS - P, 1, :], psum[0:PE_COLS - P, 6, P:2 * P]).then_inc(src_T_sb, 1)
                es_group(act, copy, g)
            copy(t2[:, :, F:2 * F], t1[:, :, 0:F]).then_inc(t2h_ready, 1)

            act.wait_ge(weights_in, N_WEIGHTS * 16)
            act.wait_ge(consts_set, N_CONSTS)
            nc.scalar.activation(cat_s[0:F, 0:1], ident[0:F, 0:1], ACT.Copy, scale=0.0, bias=1.0 / H).then_inc(packed, 1)
            nc.scalar.activation(cat_s[F:P, 0:1], ident[F:P, 0:1], ACT.Copy, scale=0.0, bias=1.0).then_inc(packed, 1)

            def found1_copy(c, s):
                m = ON_PE1[s % 2]
                act.wait_ge(found1_ps, c + 1)
                copy(gather1[:, s, K - m:, :], psum[:, 4 + s % 2, 0:m * W1R].rearrange("p (m w) -> p m w", w=W1R))\
                    .then_inc(found1_sb, 1)

            act.sem_inc(found1_sb, 2)
            with act.Fori(0, LOOPS) as i:
                for s in range(SL):
                    found1_copy(i * SL + s, s)
            for c in range(FULL, CH):
                found1_copy(c, c % SL)

            for j in range(NJ):
                act.wait_ge(cross_T, j + 1)
                copy(cross[:, j, :], psum[:, 2 + j % 2, 0:NQ]).then_inc(cross_sb, 1)

            act.wait_ge(w_arg, 1)
            nc.scalar.activation(es_w[:, :, :], es_w[:, :, :], ACT.Exp).then_inc(w_ready, 1)

            def messages(c, s, n):
                m = ON_PE2[s % 2]
                act.wait_ge(g2_ready[s], n * (16 * (K - m)))
                act.wait_ge(gat_steps, (c + 1) * K)
                settle()
                for k in range(ON_ACT):
                    for h in range(H):
                        weight = es_w[:, bass.ds(c * K + k, 1), h]
                        nc.scalar.activation(msg2[:, s % 2, k, F + h * WH:F + (h + 1) * WH], gather2[:, s, k, F:W2R],
                                             ACT.Copy, scale=weight)
                act.wait_ge(found2_ps, c + 1)
                copy(gather2[:, s, K - m:, 0:2 * F], psum[:, 2 + s % 2, 0:m * 2 * F].rearrange("p (m w) -> p m w", w=2 * F))\
                    .then_inc(found2_sb, 1)
                act.wait_ge(found2_sb, c + 3)
                settle()
                copy(msg2[:, s % 2, :, 0:F], gather2[:, s, :, 0:F]).then_inc(hopcopy, 1)

            act.wait_ge(w_ready, 1)
            act.wait_ge(parts2_ready, 1)
            act.sem_inc(found2_sb, 2)
            with act.Fori(0, LOOPS) as i:
                for s in range(SL):
                    messages(i * SL + s, s, i + 1)
            for c in range(FULL, CH):
                messages(c, c % SL, c // SL + 1)

            for j in range(NJ + 1):
                if j < NJ:
                    act.wait_ge(aT_ps, j + 1)
                    copy(aT[:, j % 2, 0:2, :], psum[:, 5, 0:2 * P].rearrange("p (c q) -> p c q", c=2)[:, :, 0:NQ])
                    copy(aT[0:F, j % 2, 2, :], psum[0:F, 5, 2 * P:2 * P + NQ]).then_inc(aT_sb, 1)
                if j:
                    act.wait_ge(catT_ps, j)
                    nc.scalar.activation(catT[:, :], psum[:, 6, 0:NQ], ACT.Identity, scale=cat_s[:, 0:1],
                                         bias=cat_s[:, 1:2]).then_inc(catT_sb, 1)
                if j >= GJ and j % GJ == 3:
                    act.wait_ge(ln_var, NG + j // GJ)
                    ln_sqrt(j // GJ - 1).then_inc(ln_std, 1)

            def node_weights(l):
                copy(cur_n[:, :], pack[:, bass.ds(l, 1), 0:CN].rearrange("p a c -> p (a c)")).then_inc(cur_n_ready, 1)

            def edge_weights(l):
                copy(cur[:, 0:CE], pack[:, bass.ds(l, 1), CN:].rearrange("p a c -> p (a c)")).then_inc(cur_ready, 1)
                copy(cur_be[:, :], be_parts[:, bass.ds(l, 1), :].rearrange("p a f -> p (a f)")).then_inc(cur_ready, 1)
                act.wait_ge(cur_ready, l * 4 + 2)
                nc.scalar.mul(cur[:, C_E2N:C_E2N + P], cur[:, C_E2:C_E2 + P], -LEAK).then_inc(cur_ready, 1)
                nc.scalar.mul(cur[:, C_BE1N:C_BE1N + 1], cur[:, C_BE1:C_BE1 + 1], -1.0).then_inc(cur_ready, 1)
                act.wait_ge(cur_ready, l * 4 + 4)

            def copy_xT(l, g):
                act.wait_ge(xT_ps, l * NG + (g + 1))
                copy(hT[:, :, :], psum[0:F, 0:2, :].rearrange("p b n -> p (b n)")[:, 0:GJ * P]
                     .rearrange("p (k n) -> p k n", n=P)[:, :, 0:NQ]).then_inc(xT_sb, 1)

            def biased(l, g):
                act.wait_ge(y_ps, l * NG + (g + 1))
                y = psum[:, 2:4, :].rearrange("p b n -> p (b n)")[:, 0:GJ * P]\
                    .rearrange("p (k n) -> p k n", n=P)[:, :, 0:NQ]
                nc.scalar.activation(z[:, :, :], y, ACT.Identity, bias=cur_n[:, C_B1:C_B1 + 1]).then_inc(z_sb, 1)

            def edge_acts(l):
                def attr_copy(c, b):
                    act.wait_ge(at_ps, l * CH + c + 1)
                    copy(attr_T[:, b, :], psum[:, 5 + b, 0:256]).then_inc(at_sb, 1)

                def relu_edges(c, b):
                    act.wait_ge(ye_ps, l * CH + c + 1)
                    nc.scalar.activation(act_p[:, b, :], psum[:, b, :], ACT.Relu, bias=cur[:, C_BE1:C_BE1 + 1])\
                        .then_inc(ye_sb, 1)
                    nc.scalar.activation(act_n[:, b, :], psum[:, b, :], ACT.Relu, bias=cur[:, C_BE1N:C_BE1N + 1],
                                         scale=-1.0).then_inc(ye_sb, 1)

                def found_copy(c, s):
                    m = ON_PE[s % 2]
                    act.wait_ge(found_ps, l * CH + c + 1)
                    copy(gatherg[:, s, K - m:, :], psum[:, 4 + 3 * (s % 2), 0:m * F].rearrange("p (m f) -> p m f", f=F))\
                        .then_inc(found_sb, 1)

                attr_copy(0, 0)
                attr_copy(1, 1)
                relu_edges(0, 0)
                with act.Fori(0, LOOPS) as i:
                    for s in range(SL):
                        attr_copy(i * SL + (s + 2), s % 2)
                        relu_edges(i * SL + (s + 1), (s + 1) % 2)
                        found_copy(i * SL + s, s)
                for c in range(FULL, CH):
                    if c + 2 < CH:
                        attr_copy(c + 2, c % 2)
                    if c + 1 < CH:
                        relu_edges(c + 1, (c + 1) % 2)
                    found_copy(c, c % SL)

            def node_acts(l, more):
                if more:
                    act.wait_ge(e_ready, l * CH + CH)
                    settle()
                    edge_weights(l + 1)
                for g in range(NG + 1):
                    if g and more:
                        copy_xT(l + 1, g - 1)
                    if g < NG:
                        act.wait_ge(ln_var, l * NG + (2 * NG + g + 1))
                        ln_sqrt(g).then_inc(ln_std, 1)
                    if g and more:
                        biased(l + 1, g - 1)
                if more:
                    act.wait_ge(h_ps, l * NG + 2 * NG)
                    settle()

            act.wait_ge(packed, 2)
            act.wait_ge(be_steps, N_BE)
            act.wait_ge(pack_in, N_PACK * 16)
            node_weights(0)
            edge_weights(0)
            for g in range(NG):
                copy_xT(0, g)
                if g == 0:
                    act.wait_ge(ln_var, 2 * NG)
                    ln_sqrt(NG - 1).then_inc(ln_std, 1)
                biased(0, g)
            act.wait_ge(h_ps, NG)
            settle()
            with act.Fori(0, L - 1) as l:
                node_weights(l + 1)
                edge_acts(l)
                node_acts(l, True)
            edge_acts(L - 1)
            node_acts(L - 1, False)

        @block.tensor
        def _(pe):
            mm = nc.tensor.matmul

            def settle():
                pe.sem_inc(passed[1], 1)

            pe.wait_ge(consts_set, N_CONSTS)
            pe.wait_ge(att_in, 48)
            for h in range(H):
                ins = nc.tensor.transpose(psum[0:F, 0, h * F:(h + 1) * F], watt[:, h, :], ident[0:F, 0:F])
            ins.then_inc(v_T, 1)
            pe.wait_ge(v_Tsb, 1)
            for a in range(2):
                for h in range(H):
                    ins = mm(psum[0:F, 1, a * H + h:a * H + h + 1], wattT[:, h, :], avec[:, a, h:h + 1],
                             start=True, stop=True)
            ins.then_inc(v_ps, 1)

            def transpose_group(x_tile, bank, signal):
                for k in range(GJ):
                    ins = nc.tensor.transpose(psum[0:F, bank + k // 4, (k % 4) * P:(k % 4) * P + NQ],
                                              x_tile[:, k, :], ident[0:NQ, 0:NQ])
                ins.then_inc(signal, 1)

            pe.wait_ge(h0_ready, 1)
            transpose_group(t1[:, grp(0), 0:F], 2, h0_T)
            pe.wait_ge(v_sb, 1)
            for g in range(NG):
                if g == NG - 1:
                    pe.wait_ge(src_cols_set, 1)
                    nc.tensor.transpose(psum[:, 6, 0:P], src_cols[:, 0:P], ident[:, :])
                    nc.tensor.transpose(psum[0:PE_COLS - P, 6, P:2 * P], src_cols[:, P:], ident[:, :]).then_inc(src_T_ps, 1)
                pe.wait_ge(h0_Tsb, g + 1)
                if g:
                    pe.wait_ge(es_sb, 2 * g)
                for k in range(GJ):
                    ins = mm(psum[0:NQ, 1, 64 + k * 2 * H:64 + (k + 1) * 2 * H], hT[:, k, :], vvec[:, :],
                             start=True, stop=True)
                ins.then_inc(es_ps, 1)
                if g + 1 < NG:
                    pe.wait_ge(h0_ready, g + 2)
                    transpose_group(t1[:, grp(g + 1), 0:F], 2, h0_T)

            pe.wait_ge(diag_ready, 1)
            for a in range(2):
                ins = mm(psum[:, 0, a * P:(a + 1) * P], ones[:, :], diag[:, a, :], start=True, stop=True)
            ins.then_inc(bc_ready, 1)

            degree = psum[0:NQ, 7, 0:NJ]
            mm(degree, zero16[:, :], zero16[:, 0:NJ], start=True, stop=False)

            def look_up1(c, b):
                pe.wait_ge(hot1_done, c + 1)
                pe.wait_ge(found1_sb, c + 1)
                settle()
                for m in range(ON_PE1[b]):
                    for j in range(NJ):
                        for part in range(3):
                            ins = mm(psum[:, 4 + b, m * W1R:(m + 1) * W1R], hot[:, b, j, m, :], parts1[:, j, part, :],
                                     start=(j == 0 and part == 0), stop=(j == NJ - 1 and part == 2))
                ins.then_inc(found1_ps, 1)

            def degrees(c, s):
                pe.wait_ge(hot_ready, c + 1)
                settle()
                for k in range(K):
                    ins = mm(degree, hot_q[:, s % 2, k, :], hot_j[:, s % 2, k, :], start=False, stop=False)
                ins.then_inc(hot_used, 1)

            pe.sem_inc(hot_used, 2)
            pe.wait_ge(parts1_ready, 1)
            look_up1(0, 0)
            with pe.Fori(0, LOOPS) as i:
                for s in range(SL):
                    look_up1(i * SL + (s + 1), (s + 1) % 2)
                    degrees(i * SL + s, s)
            for c in range(FULL, CH):
                if c + 1 < CH:
                    look_up1(c + 1, (c + 1) % 2)
                degrees(c, c % SL)
            mm(degree, zero16[:, :], zero16[:, 0:NJ], start=False, stop=True).then_inc(deg_ready, 1)
            pe.wait_ge(rowtot, 1)
            mm(psum[0:NQ, 4, 0:1], above[0:NQ, 0:NQ], incl[:, NJ - 1:NJ], start=True, stop=True).then_inc(rowoff_ps, 1)
            pe.wait_ge(crossq_ready, 1)
            for j in range(NJ):
                if j >= 2:
                    pe.wait_ge(cross_sb, j - 1)
                nc.tensor.transpose(psum[:, 2 + j % 2, 0:NQ], crossq[:, j, :], ident[0:NQ, 0:NQ]).then_inc(cross_T, 1)

            def tails_group(g, tail, ready, used, base):
                if g >= 3:
                    pe.wait_ge(used, base + (g - 2))
                    settle()
                for k in range(GJ):
                    ins = mm(psum[0:NQ, 4 + g % 3, k * F:(k + 1) * F], cross[:, g * GJ + k, :], tail,
                             start=True, stop=True)
                ins.then_inc(ready, 1)

            def tails(tail, ready, used, base):
                for g in range(NG):
                    tails_group(g, tail, ready, used, base)

            for a in range(2):
                pe.wait_ge(diag4_ready, a + 1)
                mm(psum[:, a, :], ones[:, :], diag4[:, :, :].rearrange("p h n -> p (h n)"),
                   start=True, stop=True).then_inc(bc4_ready, 1)

            pe.wait_ge(cross_sb, NJ)
            pe.wait_ge(hop_steps, CH * K)
            settle()
            tails(run1[:, (CH - 1) % SL, K - 1, :], c1_ready, c1_used, 0)

            def look_up2(c, b):
                pe.wait_ge(hot2_done, c + 1)
                pe.wait_ge(found2_sb, c + 1)
                settle()
                for m in range(ON_PE2[b]):
                    for half, of in enumerate((parts, parts1)):
                        o = psum[:, 2 + b, (2 * m + half) * F:(2 * m + half + 1) * F]
                        for j in range(NJ):
                            for part in range(3):
                                ins = mm(o, hot[:, b, j, m, :], of[:, j, part, 0:F],
                                         start=(j == 0 and part == 0), stop=(j == NJ - 1 and part == 2))
                ins.then_inc(found2_ps, 1)

            pe.wait_ge(parts2_ready, 1)
            with pe.Fori(0, LOOPS) as i:
                for s in range(SL):
                    look_up2(i * SL + s, s % 2)
            for c in range(FULL, CH):
                look_up2(c, c % 2)

            pe.wait_ge(gat_steps, (CH + 2) * K)
            settle()
            pe.wait_ge(weights_in, N_WEIGHTS * 16)
            tail2 = run2[:, (CH - 1) % 2, K - 1, :]

            def tails2(g):
                for j in range(g * GJ, (g + 1) * GJ):
                    if j >= 5:
                        pe.wait_ge(c2_used, j - 4)
                    mm(psum[0:NQ, j % 5, 0:WG], cross[:, j, :], tail2, start=True, stop=True).then_inc(c2_ready, 1)

            tails2(0)
            for i in range(NJ + 2):
                if i < NJ:
                    if i % GJ == 0:
                        if i // GJ + 1 < NG:
                            tails2(i // GJ + 1)
                        pe.wait_ge(cat2_ready, i // GJ + 1)
                    if i:
                        pe.wait_ge(aT_sb, i)
                    for c in range(3):
                        w = P if c < 2 else F
                        ins = nc.tensor.transpose(psum[0:w, 5, c * P:c * P + NQ],
                                                  cat2[:, i // GJ % 2, i % GJ, c * P:c * P + w], ident[0:NQ, 0:NQ])
                    ins.then_inc(aT_ps, 1)
                if i >= 2:
                    j = i - 2
                    g, k = j // GJ, j % GJ
                    pe.wait_ge(catT_sb, j + 1)
                    if k == 0 and g:
                        pe.wait_ge(x1_used, g)
                    o = psum[0:NQ, 7, k * F:(k + 1) * F]
                    mm(o, ones[0:1, 0:NQ], bw_row[0:1, :], start=True, stop=False)
                    ins = mm(o, catT[:, :], ww_sb[:, :], start=False, stop=True)
                    if k == GJ - 1:
                        ins.then_inc(x1_ps, 1)
                if 1 <= i <= NJ:
                    j = i - 1
                    pe.wait_ge(aT_sb, j + 1)
                    mm(psum[0:F, 6, 0:NQ], wstack[:, 0, :], aT[:, j % 2, 0, :], start=True, stop=False)
                    mm(psum[0:F, 6, 0:NQ], wstack[:, 1, :], aT[:, j % 2, 1, :], start=False, stop=True)
                    mm(psum[F:P, 6, 0:NQ], wg_sb[:, :], aT[0:F, j % 2, 2, :], start=True, stop=True).then_inc(catT_ps, 1)

            def transpose_x(l, g):
                pe.wait_ge(x_ready, l * NG + (g + 1))
                settle()
                transpose_group(xg[:, grp(g), :], 0, xT_ps)

            def node_mlp(l, tail):
                pe.wait_ge(cur_n_ready, l + 1)
                settle()
                if tail is None:
                    pe.wait_ge(x1_used, NG)
                transpose_x(l, 0)
                for g in range(NG):
                    pe.wait_ge(xT_sb, l * NG + (g + 1))
                    settle()
                    for k in range(GJ):
                        ins = mm(psum[:, 2 + k // 4, (k % 4) * P:(k % 4) * P + NQ], cur_n[0:F, C_W1:C_W1 + F2], hT[:, k, :],
                                 start=True, stop=True)
                    ins.then_inc(y_ps, 1)
                    if tail is not None and g + 3 < NG:
                        tails_group(g + 3, tail, cg_ready, cg_used, (l - 1) * NG)
                    if g + 1 < NG:
                        transpose_x(l, g + 1)
                    pe.wait_ge(y_sb, l * NG + (g + 1))
                    if g:
                        pe.wait_ge(h_sb, l * NG + g)
                    settle()
                    for k in range(GJ):
                        ins = mm(psum[0:NQ, 7, k * F:(k + 1) * F], yp[:, k, :], cur_n[:, C_W2:C_W2 + F], start=True, stop=True)
                    ins.then_inc(h_ps, 1)

            def arrivals(s):
                return len(range(s, CH, SL))

            def edge_products(l):
                def transpose_attr(c, s, n):
                    pe.wait_ge(attr_in[s], n * 32)
                    settle()
                    for u in range(2):
                        ins = nc.tensor.transpose(psum[:, 5 + s % 2, u * P:(u + 1) * P],
                                                  attr_nat[:, s, u * P:(u + 1) * P], ident[:, :])
                    ins.then_inc(at_ps, 1)

                def first_half(c, b):
                    pe.wait_ge(at_sb, l * CH + c + 1)
                    settle()
                    for u in range(4):
                        ins = mm(psum[:, b, u * P:(u + 1) * P], cur[:, C_E1 + (u % 2) * P:C_E1 + (u % 2 + 1) * P],
                                 attr_T[:, b, (u // 2) * P:(u // 2 + 1) * P], start=True, stop=True)
                    ins.then_inc(ye_ps, 1)

                def look_up(c, b):
                    pe.wait_ge(hot_done, l * CH + c + 1)
                    pe.wait_ge(edge_steps, (l * CH + c) * (K + 1) + 1)
                    settle()
                    for m in range(ON_PE[b]):
                        for j in range(NJ):
                            for part in range(3):
                                ins = mm(psum[:, 4 + 3 * b, m * F:(m + 1) * F], hot[:, b, j, m, :], parts[:, j, part, :],
                                         start=(j == 0 and part == 0), stop=(j == NJ - 1 and part == 2))
                    ins.then_inc(found_ps, 1)

                def second_half(c, b):
                    pe.wait_ge(ye_sb, (l * CH + c + 1) * 2)
                    settle()
                    mm(psum[:, 2 + b, :], ones16[:, :], cur_be[:, :].unsqueeze(1).to_broadcast([96, K, F]),
                       start=True, stop=False, skip_group_check=True)
                    for u in range(4):
                        o = psum[:, 2 + b, u * P:(u + 1) * P]
                        mm(o, act_p[:, b, u * P:(u + 1) * P], cur[:, C_E2:C_E2 + P], start=False, stop=False, skip_group_check=True)
                        ins = mm(o, act_n[:, b, u * P:(u + 1) * P], cur[:, C_E2N:C_E2N + P], start=False,
                                 stop=(u == 3), skip_group_check=True)
                    ins.then_inc(e_ready, 1)

                pe.wait_ge(cur_ready, l * 4 + 4)
                transpose_attr(0, 0, l * arrivals(0) + 1)
                transpose_attr(1, 1, l * arrivals(1) + 1)
                first_half(0, 0)
                pe.wait_ge(parts_ready, l + 1)
                settle()
                with pe.Fori(0, LOOPS) as i:
                    for s in range(SL):
                        c = i * SL + s
                        s2 = (s + 2) % SL
                        transpose_attr(c + 2, s2, l * arrivals(s2) + i + (1 + (s + 2) // SL))
                        first_half(c + 1, (s + 1) % 2)
                        look_up(c, s % 2)
                        second_half(c, s % 2)
                for c in range(FULL, CH):
                    if c + 2 < CH:
                        s2 = (c + 2) % SL
                        transpose_attr(c + 2, s2, l * arrivals(s2) + ((c + 2) // SL + 1))
                    if c + 1 < CH:
                        first_half(c + 1, (c + 1) % 2)
                    look_up(c, c % 2)
                    second_half(c, c % 2)
                pe.wait_ge(edge_steps, 2 * (K + 1) + (l + 1) * (CH * (K + 1)))
                settle()

            tail_g = run1[:, (CH - 1) % SL, K - 1, :]
            node_mlp(0, None)
            with pe.Fori(0, L - 1) as l:
                edge_products(l)
                for g in range(3):
                    tails_group(g, tail_g, cg_ready, cg_used, l * NG)
                node_mlp(l + 1, tail_g)
            edge_products(L - 1)
            tails(tail_g, cg_ready, cg_used, (L - 1) * NG)

        @block.vector
        def _(dve):
            tt = nc.vector.tensor_tensor
            ts = nc.vector.tensor_scalar
            stt = nc.vector.scalar_tensor_tensor
            st = Steps(dve, dve_steps)

            def per_node(v, g, width=F):
                return v[:, grp(g)].unsqueeze(2).to_broadcast([NQ, GJ, width])

            def centred(xs, g):
                return stt(cen[:, g % 2, :, :], xs, float(F), st_sum[:, g % 2, :].unsqueeze(2).to_broadcast([NQ, GJ, F]),
                           ALU.mult, ALU.subtract)

            def square_sum(st, n, g):
                st.wait(n)
                st.then(tt(sq[:, :, :], cen[:, g % 2, :, :], cen[:, g % 2, :, :], ALU.mult))
                nc.vector.tensor_reduce(st_var[:, g % 2, :], sq[:, :, :], AX.X, ALU.add).then_inc(ln_var, 1)

            def norm_relu(st, xs, g, to, n_std, signal):
                front, back = g < NG, g > 0
                b = (g - 1) % 2
                if front:
                    n = st.done(nc.vector.tensor_reduce(st_sum[:, g % 2, :], xs[:, grp(g), :], AX.X, ALU.add))
                if back:
                    dve.wait_ge(ln_std, n_std)
                    m = st.done(nc.vector.reciprocal(st_std[:, b, :], st_std[:, b, :]))
                if front:
                    st.wait(n)
                    n = st.done(centred(xs[:, grp(g), :], g))
                if back:
                    st.wait(m)
                    stt(to[:, grp(g - 1), 0:F], cen[:, b, :, :], 0.0, st_std[:, b, :].unsqueeze(2).to_broadcast([NQ, GJ, F]),
                        ALU.max, ALU.mult).then_inc(signal, 1)
                if front:
                    square_sum(st, n, g)

            dve.wait_ge(x_in, 16)
            for g in range(NG + 1):
                norm_relu(st, xin, g, t1, g, h0_ready)

            dve.wait_ge(edges_in, 64)
            for s in range(SL):
                nc.vector.tensor_copy(idx[:, s, :], src_i[:, s * K:(s + 1) * K]).then_inc(idx1, 1)
            st.done(nc.vector.tensor_copy(src_cols[:, :].rearrange("p (c m) -> p c m", m=KPE),
                                          src_i[:, :].rearrange("p (c k) -> p c k", k=K)[:, :, K - KPE:]))
            dve.wait_ge(dve_steps, st.n)
            ts(src_cols[:, :], src_cols[:, :], float(MID), None, ALU.subtract).then_inc(src_cols_set, 1)
            st.then(nc.vector.tensor_copy(dst_f[:, :], dst_i[:, :]))
            st.done(nc.vector.memset(mask[:, 0:1], 0.0))
            st.done(nc.vector.memset(pen[:, T:T + 1], -BIG))
            st.then(tt(mask[:, 1:T], dst_f[:, 1:T], dst_f[:, 0:T - 1], ALU.is_equal))
            st.done(ts(pen[:, 0:T], mask[:, :], 1.0, BIG, ALU.subtract, ALU.mult))
            st.done(ts(pen_first[:, :], dst_f[:, :], dst_f[:, 0:1], 1.0, ALU.is_equal, ALU.subtract))
            st.then(ts(pen_last[:, :], dst_f[:, :], dst_f[:, T - 1:T], 1.0, ALU.is_equal, ALU.subtract))
            st.done(ts(pen_first[:, :], pen_first[:, :], BIG, None, ALU.mult))
            st.done(ts(pen_last[:, :], pen_last[:, :], BIG, None, ALU.mult))
            st.then(ts(d25[:, :], dst_f[:, :], 1.0 / NJ, 0.48, ALU.mult, ALU.subtract))
            st.then(ts(d25[:, :], d25[:, :], ROUND, ROUND, ALU.add, ALU.subtract))
            st.then(ts(d25[:, :], d25[:, :], float(NJ), None, ALU.mult))
            st.then(tt(drem[:, :], dst_f[:, :], d25[:, :], ALU.subtract))
            dve.wait_ge(consts_set, N_CONSTS)
            ts(diag[:, 0, :], ident[:, :], dst_f[:, T - 1:T], None, ALU.mult)
            ts(diag[:, 1, :], ident[:, :], dst_f[:, 0:1], None, ALU.mult).then_inc(diag_ready, 1)
            dve.wait_ge(bc_ready, 1)
            st.done(ts(pen_m[:, 0, :], psum[:, 0, 0:P], dst_f[:, 0:1], None, ALU.is_equal))
            st.then(ts(pen_m[:, 1, :], psum[:, 0, P:2 * P], dst_f[:, T - 1:T], None, ALU.is_equal))
            st.done(tt(pen_m[:, 0, :], pen_m[:, 0, :], below[:, :], ALU.mult))
            st.then(tt(pen_m[:, 1, :], pen_m[:, 1, :], above[:, :], ALU.mult))
            st.then(ts(pen_m[:, :, :], pen_m[:, :, :], 1.0, BIG, ALU.subtract, ALU.mult))
            dve.sem_inc(dst_used, 1)

            dve.wait_ge(es_sb, 2 * NG)
            st.then(nc.vector.tensor_copy(parts1[:, :, 0, :], t1[:, :, :]))
            st.then(tt(rest1[:, :, :], t1[:, :, :], parts1[:, :, 0, :], ALU.subtract))
            st.then(nc.vector.tensor_copy(parts1[:, :, 1, :], rest1[:, :, :]))
            tt(parts1[:, :, 2, :], rest1[:, :, :], parts1[:, :, 1, :], ALU.subtract).then_inc(parts1_ready, 1)

            def passes(s):
                return len(range(s, CH, SL))

            def one_hot(b, s, m, j0, j1):
                shape = [NQ, j1 - j0, m, P]
                return tt(hot[:, b, j0:j1, 0:m, :], src_row[:, s, 0:m, :].unsqueeze(1).to_broadcast(shape),
                          node_id[:, j0:j1, :].unsqueeze(2).to_broadcast(shape), ALU.is_equal)

            def running_sums(to, c, rows, steps, n, between):
                prev = run1[:, (to - 1) % SL, K - 1, :]
                for k in range(K):
                    stt(run1[:, to, k, :], prev, mask[:, bass.ds(c * K + k, 1)], rows[:, k, :], ALU.mult, ALU.add)\
                        .then_inc(steps, 1)
                    prev = run1[:, to, k, :]
                    between(k)
                    dve.wait_ge(steps, n + (k + 1))

            def hop_chunk(c, s, n, more, n2):
                m, s2 = ON_PE1[s % 2], (s + 2) % SL
                dve.wait_ge(g1_ready[s], n * (16 * (K - m)))
                dve.wait_ge(found1_sb, c + 3)
                dve.wait_ge(run1_free, c + 1)

                def between(k):
                    if k == 0:
                        dve.wait_ge(hot_used, c + 1)
                        tt(hot_q[:, s % 2, :, :], d25[:, bass.ds(c * K, K)].unsqueeze(2).to_broadcast([P, K, NQ]),
                           q25[:, :].unsqueeze(1).to_broadcast([P, K, NQ]), ALU.is_equal)
                    if k == 1:
                        tt(hot_j[:, s % 2, :, :], drem[:, bass.ds(c * K, K)].unsqueeze(2).to_broadcast([P, K, NJ]),
                           jcol[:, :].unsqueeze(1).to_broadcast([P, K, NJ]), ALU.is_equal).then_inc(hot_ready, 1)
                        nc.vector.tensor_copy(es_w[:, bass.ds(c * K, K), :], gather1[:, s, :, F:F + H]).then_inc(es_done, 1)
                    if n2 is not None and k >= 2:
                        if k == 2:
                            dve.wait_ge(src_in[s2], n2 * 16)
                        piece = one_hot(s % 2, s2, m, NJ * (k - 2) // (K - 2), NJ * (k - 1) // (K - 2))
                        if k == K - 1:
                            piece.then_inc(hot1_done, 1)
                    if more and k == K - 1:
                        nc.vector.tensor_copy(idx[:, s, :], src_i[:, bass.ds((c + SL) * K, K)]).then_inc(idx1, 1)

                running_sums(s, c, gather1[:, s, :, 0:F], hop_steps, c * K, between)

            dve.wait_ge(ed_zeroed, 96)
            dve.wait_ge(node_id_set, 1)
            for c in range(2):
                dve.wait_ge(src_in[c], 16)
                one_hot(c, c, ON_PE1[c], 0, NJ).then_inc(hot1_done, 1)
            dve.wait_ge(weights_in, N_WEIGHTS * 16)
            be = Steps(dve, be_steps)
            be.then(nc.vector.tensor_copy(be_tmp[:, :, :], be_rows[:, :, :]))
            be.done(nc.vector.tensor_copy(be_parts[0:32, :, :], be_tmp[0:32, :, :]))
            be.then(tt(be_rows[:, :, :], be_rows[:, :, :], be_tmp[:, :, :], ALU.subtract))
            be.then(nc.vector.tensor_copy(be_tmp[:, :, :], be_rows[:, :, :]))
            be.done(nc.vector.tensor_copy(be_parts[32:64, :, :], be_tmp[32:64, :, :]))
            be.then(tt(be_parts[64:96, :, :], be_rows[64:96, :, :], be_tmp[64:96, :, :], ALU.subtract))
            assert be.n == N_BE

            with dve.Fori(0, LOOPS) as i:
                for s in range(SL):
                    hop_chunk(i * SL + s, s, i + 1, True, i + ((s + 2) // SL + 1))
            for c in range(FULL, CH):
                hop_chunk(c, c % SL, c // SL + 1, c + SL < CH, (c + 2) // SL + 1 if c + 2 < CH else None)

            dve.wait_ge(deg_ready, 1)
            st.then(nc.vector.tensor_copy(deg, psum[0:NQ, 7, 0:NJ]))
            nc.vector.tensor_tensor_scan(incl, ones[0:NQ, 0:NJ], deg, 0.0, ALU.mult, ALU.add).then_inc(rowtot, 1)
            dve.wait_ge(rowoff_ps, 1)
            st.then(nc.vector.tensor_copy(rowoff[:, :], psum[0:NQ, 4, 0:1]))
            st.then(ts(last, incl, rowoff[:, 0:1], 1.0, ALU.add, ALU.subtract))
            st.done(ts(nonempty, deg, 0.5, None, ALU.is_gt))
            st.then(ts(lastc, last, float(EP), None, ALU.subtract))
            st.then(tt(lastc, lastc, nonempty, ALU.mult))
            ts(last_i[:, :], lastc, float(EP), None, ALU.add).then_inc(last_ready, 1)
            st.then(tt(first, last, deg, ALU.subtract))
            st.done(ts(first, first, 1.0, None, ALU.add))
            st.then(ts(cmean, deg, 1.0, None, ALU.max))
            st.then(nc.vector.reciprocal(cmean, cmean))
            st.done(tt(cmean, cmean, nonempty, ALU.mult))
            st.then(tt(tmpn, first, spare[0:NQ, :], ALU.subtract))
            st.then(tt(tmpn, tmpn, nonempty, ALU.mult))
            st.then(tt(tmpn, tmpn, spare[0:NQ, :], ALU.add))
            nc.vector.tensor_copy(slot_i[:, :], tmpn).then_inc(slots_ready, 1)
            bounds = bound[0:NQ, :].unsqueeze(1).to_broadcast([NQ, NJ, P])
            st.done(tt(crossq, bounds, first.unsqueeze(2).to_broadcast([NQ, NJ, P]), ALU.is_gt))
            st.then(tt(crossq2, bounds, last.unsqueeze(2).to_broadcast([NQ, NJ, P]), ALU.is_le))
            tt(crossq, crossq, crossq2, ALU.mult).then_inc(crossq_ready, 1)

            dve.wait_ge(es_done, CH)
            for h in range(H):
                st.done(nc.vector.tensor_tensor_scan(highest[:, :, h], pen[:, 0:T], es_w[:, :, h], 0.0, ALU.add, ALU.max))
                st.done(nc.vector.tensor_tensor_scan(from_right[:, ::-1, h], pen[:, T:0:-1], es_w[:, ::-1, h], 0.0,
                                                     ALU.add, ALU.max))
            st.wait(st.n)
            for a, state in ((0, highest[:, T - 1, :]), (1, from_right[:, 0, :])):
                if a:
                    dve.wait_ge(bc4_ready, a)
                tt(diag4[:, :, :], ident[:, :].unsqueeze(1).to_broadcast([P, H, P]),
                   state.unsqueeze(2).to_broadcast([P, H, P]), ALU.mult).then_inc(diag4_ready, 1)
            st.then(tt(highest, highest, from_right, ALU.max))
            st.done(nc.vector.memset(gather2[:, :, K - max(ON_PE2):, 2 * F:], 1.0))
            for a in range(2):
                dve.wait_ge(bc4_ready, a + 1)
                st.then(tt(reached, psum[:, a, :].rearrange("p (h n) -> p h n", h=H),
                           pen_m[:, a, :].unsqueeze(1).to_broadcast([P, H, P]), ALU.add))
                st.then(nc.vector.tensor_reduce(carry[:, a, :], reached, AX.X, ALU.max))
            for a, reach in ((0, pen_first), (1, pen_last)):
                for h in range(H):
                    st.done(stt(highest[:, :, h], reach[:, :], carry[:, a, h:h + 1], highest[:, :, h], ALU.add, ALU.max))
                st.wait(st.n)

            for s in range(SL):
                nc.vector.tensor_copy(idx[:, s, :], src_i[:, s * K:(s + 1) * K]).then_inc(idx2, 1)
            for g in range(NG):
                dve.wait_ge(agg_in[g], GJ * 16)
                dve.wait_ge(c1_ready, g + 1)
                tt(agg[:, grp(g), :], agg[:, grp(g), :], psum[0:NQ, 4 + g % 3, 0:GJ * F].rearrange("q (k f) -> q k f", f=F),
                   ALU.add).then_inc(c1_used, 1)
                dve.wait_ge(c1_used, g + 1)
                tt(t2[:, grp(g), 0:F], agg[:, grp(g), :], per_node(cmean, g), ALU.mult).then_inc(t2_ready, 1)
            dve.wait_ge(t2_ready, NG)
            st.then(nc.vector.tensor_copy(parts[:, :, 0, :], t2[:, :, 0:F]))
            st.then(tt(rest2[:, :, :], t2[:, :, 0:F], parts[:, :, 0, :], ALU.subtract))
            st.then(nc.vector.tensor_copy(parts[:, :, 1, :], rest2[:, :, :]))
            tt(parts[:, :, 2, :], rest2[:, :, :], parts[:, :, 1, :], ALU.subtract).then_inc(parts2_ready, 1)

            dve.wait_ge(edx_in, 16)
            dve.wait_ge(ed0_in, 16)
            st.then(nc.vector.tensor_copy(sm_a[:, 0, :], ed0[:, :]))
            for h in range(H):
                st.done(nc.vector.tensor_tensor_scan(sm_b[:, :, h], mask[:, :], sm_a[:, :, h], 0.0, ALU.mult, ALU.add))
            st.wait(st.n)
            scores = (es_w[:, :, :], highest)
            n = [st.done(tt(v, v, sm_b, ALU.add)) for v in scores]
            for v, m in zip(scores, n):
                st.wait(m)
                v = v.rearrange("p t h -> p (t h)")
                m = st.done(stt(v, v, NEG, v, ALU.mult, ALU.max))
            st.wait(m)
            tt(es_w[:, :, :], es_w[:, :, :], highest, ALU.subtract).then_inc(w_arg, 1)
            for c in range(2):
                dve.wait_ge(src_in[c], passes(c) * 16 + 16)
                one_hot(c, c, ON_PE2[c], 0, NJ).then_inc(hot2_done, 1)
            dve.wait_ge(w_ready, 1)

            def weigh(c, s, k):
                return tt(msg2[:, s % 2, k, F:WG].rearrange("p (h w) -> p h w", h=H),
                          gather2[:, s, k, F:W2R].unsqueeze(1).to_broadcast([P, H, WH]),
                          es_w[:, bass.ds(c * K + k, 1), :].rearrange("p a h -> p (a h)").unsqueeze(2)
                          .to_broadcast([P, H, WH]), ALU.mult)

            ON_DVE = K - ON_ACT

            def gat_chunk(c, s, n1, more, n2):
                s1, s2, m1 = (s + 1) % SL, (s + 2) % SL, ON_PE2[(s + 1) % 2]
                dve.wait_ge(hopcopy, c + 1)
                dve.wait_ge(run2_free, c + 1)
                dve.wait_ge(msg_steps, (c + 1) * ON_DVE)
                prev = run2[:, (s - 1) % 2, K - 1, :]
                for k in range(K):
                    stt(run2[:, s % 2, k, :], prev, mask[:, bass.ds(c * K + k, 1)], msg2[:, s % 2, k, :],
                        ALU.mult, ALU.add).then_inc(gat_steps, 1)
                    prev = run2[:, s % 2, k, :]
                    if n2 is not None and k < ON_ACT:
                        if k == 0:
                            dve.wait_ge(src_in[s2], (passes(s2) + n2) * 16)
                        piece = one_hot(s % 2, s2, ON_PE2[s % 2], NJ * k // ON_ACT, NJ * (k + 1) // ON_ACT)
                        if k == ON_ACT - 1:
                            piece.then_inc(hot2_done, 1)
                    if n1 is not None and k >= ON_ACT:
                        if k == ON_ACT:
                            dve.wait_ge(g2_ready[s1], n1 * (16 * (K - m1)))
                        if k == K - m1:
                            dve.wait_ge(found2_sb, c + 4)
                        weigh(c + 1, s1, k).then_inc(msg_steps, 1)
                    if more and k == K - 1:
                        nc.vector.tensor_copy(idx[:, s, :], src_i[:, bass.ds((c + SL) * K, K)]).then_inc(idx2, 1)
                    dve.wait_ge(gat_steps, (c + 2) * K + (k + 1))

            dve.sem_inc(gat_steps, 2 * K)
            dve.wait_ge(g2_ready[0], 16 * (K - ON_PE2[0]))
            dve.wait_ge(found2_sb, 3)
            for k in range(ON_ACT, K):
                weigh(0, 0, k).then_inc(msg_steps, 1)
            with dve.Fori(0, LOOPS) as i:
                for s in range(SL):
                    gat_chunk(i * SL + s, s, i + (1 + (s + 1) // SL), True, i + (1 + (s + 2) // SL))
            for c in range(FULL, CH):
                gat_chunk(c, c % SL, (c + 1) // SL + 1 if c + 1 < CH else None, c + SL < CH,
                          (c + 2) // SL + 1 if c + 2 < CH else None)

            def gat_nodes(g):
                dve.wait_ge(agg_in[g], 2 * GJ * 16)
                for k in range(GJ):
                    j = g * GJ + k
                    dve.wait_ge(c2_ready, j + 1)
                    stt(agg2[:, j, :], agg2[:, j, :], nonempty[:, j:j + 1], psum[0:NQ, j % 5, 0:WG], ALU.mult, ALU.add)\
                        .then_inc(c2_used, 1)
                dve.wait_ge(c2_used, (g + 1) * GJ)
                heads = agg2[:, grp(g), F:WG].rearrange("q j (h w) -> q j h w", h=H)
                st.then(ts(recd[:, :, :], heads[:, :, :, F], 1e-16, None, ALU.max))
                st.then(nc.vector.reciprocal(recd[:, :, :], recd[:, :, :]))
                c2 = cat2[:, g % 2, :, :]
                if g >= 2:
                    dve.wait_ge(aT_sb, (g - 1) * GJ)
                for k in range(GJ):
                    st.done(tt(c2[:, k, 0:H * F].rearrange("q (h f) -> q h f", h=H), heads[:, k, :, 0:F],
                               recd[:, k, :].unsqueeze(2).to_broadcast([NQ, H, F]), ALU.mult))
                tt(c2[:, :, H * F:], agg2[:, grp(g), 0:F], per_node(cmean, g), ALU.mult).then_inc(cat2_ready, 1)

            def residual(g):
                dve.wait_ge(x1_ps, g + 1)
                tt(x1[:, grp(g), :], xin[:, grp(g), :], psum[0:NQ, 7, 0:GJ * F].rearrange("q (k f) -> q k f", f=F),
                   ALU.add).then_inc(x1_used, 1)
                dve.wait_ge(x1_used, g + 1)

            for g in range(NG + 1):
                if g < NG:
                    gat_nodes(g)
                if g:
                    residual(g - 1)
                    norm_relu(st, x1, g - 1, xg, NG + g - 1, x_ready)
            norm_relu(st, x1, NG, xg, 2 * NG, x_ready)

            dve.sem_inc(edge_steps, 2 * (K + 1))

            def first_indices():
                for s in range(SL):
                    nc.vector.tensor_copy(idx[:, s, :], src_i[:, s * K:(s + 1) * K]).then_inc(idxg, 1)

            def first_one_hots(l):
                for c in range(2):
                    dve.wait_ge(src_in[c], l * (passes(c) * 16) + (2 * passes(c) + 1) * 16)
                    one_hot(c, c, ON_PE[c], 0, NJ).then_inc(hot_done, 1)

            def leaky(l, g):
                dve.wait_ge(z_sb, l * NG + (g + 1))
                stt(yp[:, :, :], z[:, :, :], LEAK, z[:, :, :], ALU.mult, ALU.max).then_inc(y_sb, 1)

            def add_b2(l, g):
                dve.wait_ge(h_ps, l * NG + (g + 1))
                tt(hsb[:, grp(g), :], psum[0:NQ, 7, 0:GJ * F].rearrange("q (k f) -> q k f", f=F),
                   b2_rows[:, bass.ds(l, 1), :].to_broadcast([NQ, GJ, F]), ALU.add).then_inc(h_sb, 1)

            def split_h(st, l):
                dve.wait_ge(h_sb, l * NG + NG)
                st.then(nc.vector.tensor_copy(parts[:, :, 0, :], hsb[:, :, :]))
                st.then(tt(agg[:, :, :], hsb[:, :, :], parts[:, :, 0, :], ALU.subtract))
                st.then(nc.vector.tensor_copy(parts[:, :, 1, :], agg[:, :, :]))
                tt(parts[:, :, 2, :], agg[:, :, :], parts[:, :, 1, :], ALU.subtract).then_inc(parts_ready, 1)

            def edge_sums(l, gs):
                gs.then(nc.vector.tensor_copy(cur_ln[:, :], lnp[:, bass.ds(l, 1), :].rearrange("q a c -> q (a c)")))
                gs.then(tt(cur_ln[:, 2 * F:2 * F + 1], cur_ln[:, 2 * F:2 * F + 1], cur_ln[:, 2 * F + 1:2 * F + 2], ALU.mult))
                dve.sem_inc(passed[3], 1)

                def edge_chunk(c, s, n, more, n2):
                    done = 2 * (K + 1) + (l * CH + c) * (K + 1)
                    b, m, s2 = s % 2, ON_PE[s % 2], (s + 2) % SL
                    dve.wait_ge(e_ready, l * CH + c + 1)
                    dve.wait_ge(found_sb, l * CH + c + 1)
                    dve.wait_ge(gg_ready[s], n * (16 * (K - m)))
                    tt(msgg[:, :, :], psum[:, 2 + b, :].rearrange("p (k f) -> p k f", f=F), gatherg[:, s, :, :],
                       ALU.mult).then_inc(edge_steps, 1)
                    dve.wait_ge(rung_free, l * CH + c + 1)
                    dve.wait_ge(edge_steps, done + 1)

                    def between(k):
                        if k == 0 and more:
                            nc.vector.tensor_copy(idx[:, s, :], src_i[:, bass.ds((c + SL) * K, K)]).then_inc(idxg, 1)
                        if n2 is not None:
                            if k == 0:
                                dve.wait_ge(src_in[s2], n2 * 16)
                            piece = one_hot(b, s2, m, NJ * k // K, NJ * (k + 1) // K)
                            if k == K - 1:
                                piece.then_inc(hot_done, 1)

                    running_sums(s, c, msgg, edge_steps, done + 1, between)

                with dve.Fori(0, LOOPS) as i:
                    for s in range(SL):
                        edge_chunk(i * SL + s, s, l * passes(s) + i + 1, True,
                                   l * passes((s + 2) % SL) + i + ((s + 2) // SL + 1) + 2 * passes((s + 2) % SL))
                for c in range(FULL, CH):
                    edge_chunk(c, c % SL, l * passes(c % SL) + (c // SL + 1), c + SL < CH,
                               l * passes((c + 2) % SL) + ((c + 2) // SL + 1 + 2 * passes((c + 2) % SL)) if c + 2 < CH else None)

            def node_norm(l, gs, more):
                for g in range(NG + 1):
                    front, back = g < NG, g > 0
                    b = (g - 1) % 2
                    if front:
                        a = agg[:, grp(g), :]
                        dve.wait_ge(agg_in[g], l * (GJ * 16) + 3 * GJ * 16)
                        dve.wait_ge(cg_ready, l * NG + (g + 1))
                        tt(a, a, psum[0:NQ, 4 + g % 3, 0:GJ * F].rearrange("q (k f) -> q k f", f=F), ALU.add)\
                            .then_inc(cg_used, 1)
                    if back:
                        dve.wait_ge(ln_std, l * NG + (2 * NG + g))
                        m = gs.done(nc.vector.reciprocal(st_std[:, b, :], st_std[:, b, :]))
                    if front:
                        dve.wait_ge(cg_used, l * NG + (g + 1))
                        n = gs.done(stt(a, a, cur_ln[:, 2 * F:2 * F + 1], xg[:, grp(g), :], ALU.mult, ALU.add))
                    if back:
                        gs.wait(m)
                        m = gs.done(tt(cen[:, b, :, :], cen[:, b, :, :],
                                       st_std[:, b, :].unsqueeze(2).to_broadcast([NQ, GJ, F]), ALU.mult))
                    if front:
                        gs.wait(n)
                        n = gs.done(nc.vector.tensor_reduce(st_sum[:, g % 2, :], a, AX.X, ALU.add))
                    if back:
                        gs.wait(m)
                        m = gs.done(tt(cen[:, b, :, :], cen[:, b, :, :],
                                       cur_ln[:, 0:F].unsqueeze(1).to_broadcast([NQ, GJ, F]), ALU.mult))
                    if front:
                        gs.wait(n)
                        n = gs.done(centred(a, g))
                    if back:
                        gs.wait(m)
                        tt(xg[:, grp(g - 1), :], cen[:, b, :, :], cur_ln[:, F:2 * F].unsqueeze(1).to_broadcast([NQ, GJ, F]),
                           ALU.add).then_inc(x_ready, 1)
                    if front:
                        square_sum(gs, n, g)
                    if more and g >= 3:
                        add_b2(l + 1, g - 3)
                    if more and g >= 2:
                        leaky(l + 1, g - 2)
                if more:
                    add_b2(l + 1, NG - 2)
                    leaky(l + 1, NG - 1)
                    add_b2(l + 1, NG - 1)
                dve.wait_ge(x_ready, l * NG + 2 * NG)

            first_indices()
            dve.wait_ge(weights_in, N_WEIGHTS * 16)
            for g in range(NG):
                leaky(0, g)
                add_b2(0, g)
            first_one_hots(0)
            split_h(st, 0)
            with dve.Fori(0, L - 1) as l:
                gs = Steps(dve, prep_steps, l * N_GINE_STEPS)
                edge_sums(l, gs)
                first_indices()
                first_one_hots(l + 1)
                node_norm(l, gs, True)
                split_h(gs, l + 1)
                assert gs.n == N_GINE_STEPS, gs.n
            gs = Steps(dve, prep_steps, (L - 1) * N_GINE_STEPS)
            edge_sums(L - 1, gs)
            node_norm(L - 1, gs, False)

            dve.wait_ge(x_ready, (L + 1) * NG)
            tt(xin[:, :, :], x1[:, :, :], xg[:, :, :], ALU.add).then_inc(out_ready, 1)

    return nc


N_WEIGHTS = 4 + 1 + 4 + 4
N_PACK = 3 + 4 + 4
N_CONSTS = 19
N_BE = 6
N_GINE_STEPS = 2 + NG * (4 + 3) + 3


def kernel(x, src, dst, edge_attr_32, **weights):
    import concourse.bacc as bacc
    from concourse.bass_utils import run_bass_kernel_spmd

    nc = bacc.Bacc("TRN2", target_bir_lowering=False, num_devices=1)
    names = ("W_att", "a_src", "a_dst", "W_g", "b_g", "W_w", "b_w")
    ordered = [x, src, dst, edge_attr_32] + [weights["L0_gnn_" + n] for n in names]
    names = ("W1", "b1", "W2", "b2", "We1", "be1", "We2", "be2", "res_w", "dot_scale", "ln_g", "ln_b")
    ordered += [weights["L1_gnn_" + n] for n in names]
    arrays, args = {}, []
    for i, a in enumerate(ordered):
        a = np.ascontiguousarray(a)
        arrays[f"in_{i}_dram"] = a
        args.append(nc.dram_tensor(f"in_{i}_dram", a.shape, mybir.dt.from_np(a.dtype), kind="ExternalInput").ap())
    out = nc.dram_tensor("out_dram", (N, F), F32, kind="ExternalOutput").ap()
    build(nc, *args, out)
    return run_bass_kernel_spmd(nc, [arrays], core_ids=[0]).results[0]["out_dram"]
```
